# Optimizing a Trainium2 kernel written in Bass

```python
import numpy as np
import jax
import jax.numpy as jnp

def _softmax(x, axis=-1):
    return jax.nn.softmax(x, axis=axis)

def _gelu(x):
    return jax.nn.gelu(x, approximate=True)

def _silu(x):
    return jax.nn.silu(x)

def _sigmoid(x):
    return jax.nn.sigmoid(x)

def _layernorm(x, axis=-1, eps=1e-05):
    m = jnp.mean(x, axis=axis, keepdims=True)
    v = jnp.var(x, axis=axis, keepdims=True)
    return (x - m) / jnp.sqrt(v + eps)

def _scatter_add(tgt, idx, src, axis=0):
    return tgt.at[idx].add(src)

def _segment_sum(src, seg, n):
    return jax.ops.segment_sum(src, seg, n)
kernel_name = 'mk_gnn_resnorm_d4_gnn_r8_fee91b'

def setup_inputs(seed: int=0):
    np.random.seed(seed)
    _w = jnp.asarray

    def _rec_inputs():
        import jax
        import jax.numpy as jnp
        _gk = jax.random.key(seed)
        x = -0.0003713 + 1 * jax.random.normal(jax.random.fold_in(_gk, 1), (6250, 128), jnp.float32)
        src = jax.random.randint(jax.random.fold_in(_gk, 2), (100000,), 0, 6250, jnp.int32)
        dst = jnp.minimum((6250 * jax.random.uniform(jax.random.fold_in(_gk, 3), (100000,)) ** 2.0).astype(jnp.int32), 49999)
        _o = jnp.argsort(dst, stable=True)
        src = src[_o]
        dst = dst[_o]
        edge_type_200 = jax.random.randint(jax.random.fold_in(_gk, 15), (100000,), 0, 200, jnp.int32)
        return (x, src, dst, edge_type_200)
    x, src, dst, edge_type_200 = _rec_inputs()

    def _L0_gnn_setup():
        import jax, jax.numpy as jnp
        import numpy as np
        N, E = (12500, 200000)
        IN_C, H, C = (128, 4, 32)
        NEG_SLOPE = 0.2
        key = jax.random.key(seed)
        ks = jax.random.split(key, 10)
        s = 0.05
        x = jax.random.normal(ks[0], (N, IN_C), dtype=jnp.float32)
        edge_index = jax.random.randint(ks[1], (2, E), 0, N, dtype=jnp.int32)
        W_l = jax.random.normal(ks[2], (IN_C, H * C), dtype=jnp.float32) * s
        b_l = jnp.zeros((H * C,), dtype=jnp.float32)
        W_r = jax.random.normal(ks[3], (IN_C, H * C), dtype=jnp.float32) * s
        b_r = jnp.zeros((H * C,), dtype=jnp.float32)
        att = jax.random.normal(ks[4], (H, C), dtype=jnp.float32) * s
        bias = jnp.zeros((H * C,), dtype=jnp.float32)
        gamma = jnp.ones((H * C,), dtype=jnp.float32)
        beta = jnp.zeros((H * C,), dtype=jnp.float32)
        return {'x': x, 'edge_index': edge_index, 'W_l': W_l, 'b_l': b_l, 'W_r': W_r, 'b_r': b_r, 'att': att, 'bias': bias, 'gamma': gamma, 'beta': beta}
    _L0_gnn_all = _L0_gnn_setup()
    _L0_gnn_in = {k: v for k, v in _L0_gnn_all.items() if k in ('W_l', 'b_l', 'W_r', 'b_r', 'att', 'bias', 'gamma', 'beta')}
    del _L0_gnn_all

    def _L1_gnn_setup():
        import jax, jax.numpy as jnp
        import numpy as np
        N_NODES = 12500
        N_EDGES = 200000
        D_FEAT = 128
        UNITS = 128
        LEAKY_ALPHA = 0.2
        key = jax.random.key(seed)
        k1, k2, k3, k4 = jax.random.split(key, 4)
        node_states = jax.random.normal(k1, (N_NODES, D_FEAT), dtype=jnp.float32)
        edges = jax.random.randint(k2, (N_EDGES, 2), 0, N_NODES, dtype=jnp.int64)
        kernel = jax.random.normal(k3, (D_FEAT, UNITS), dtype=jnp.float32) * (1.0 / np.sqrt(D_FEAT))
        kernel_attention = jax.random.normal(k4, (2 * UNITS, 1), dtype=jnp.float32) * (1.0 / np.sqrt(2 * UNITS))
        return {'node_states': node_states, 'edges': edges, 'kernel': kernel, 'kernel_attention': kernel_attention}
    _L1_gnn_all = _L1_gnn_setup()
    _L1_gnn_in = {k: v for k, v in _L1_gnn_all.items() if k in ('kernel', 'kernel_attention')}
    del _L1_gnn_all

    def _L2_gnn_setup():
        import jax, jax.numpy as jnp
        import numpy as np
        N = 6250
        E = 100000
        F = 128
        UNITS = 128
        ATT_UNITS = 128
        HEADS = 8

        def segment_softmax(scores, seg, num_segments):
            smax = jax.ops.segment_max(scores, seg, num_segments=num_segments)
            sexp = jnp.exp(scores - smax[seg])
            ssum = jax.ops.segment_sum(sexp, seg, num_segments=num_segments)
            return sexp / ssum[seg]
        key = jax.random.key(seed)
        ks = jax.random.split(key, 6)
        s = 1.0 / np.sqrt(F).astype(np.float32)
        return {'x': jax.random.normal(ks[0], (N, F), dtype=jnp.float32), 'edge_index': jax.random.randint(ks[1], (2, E), 0, N, dtype=jnp.int32), 'query_kernel': jax.random.normal(ks[2], (F, ATT_UNITS), dtype=jnp.float32) * s, 'query_bias': jnp.zeros((ATT_UNITS,), jnp.float32), 'key_kernel': jax.random.normal(ks[3], (F, ATT_UNITS), dtype=jnp.float32) * s, 'key_bias': jnp.zeros((ATT_UNITS,), jnp.float32), 'kernel': jax.random.normal(ks[4], (F, UNITS), dtype=jnp.float32) * s, 'bias': jnp.zeros((UNITS,), jnp.float32)}
    _L2_gnn_all = _L2_gnn_setup()
    _L2_gnn_in = {k: v for k, v in _L2_gnn_all.items() if k in ('query_kernel', 'query_bias', 'key_kernel', 'key_bias', 'kernel', 'bias')}
    del _L2_gnn_all

    def _L3_gnn_setup():
        import jax, jax.numpy as jnp
        import numpy as np
        N_ENTS = 6250
        N_EDGES = 62500
        N_RELS = 200
        RANK = 128
        N_LAYERS = 2
        RRELU_SLOPE = (1.0 / 8.0 + 1.0 / 3.0) / 2.0
        key = jax.random.key(seed)
        ks = jax.random.split(key, 9)
        return {'ent_emb': jax.random.normal(ks[0], (N_ENTS, RANK), dtype=jnp.float32), 'rel_emb': jax.random.normal(ks[1], (N_RELS, RANK), dtype=jnp.float32), 'norm': jax.random.uniform(ks[2], (N_ENTS, 1), dtype=jnp.float32), 'Wn': jax.random.normal(ks[3], (N_LAYERS, RANK, RANK), dtype=jnp.float32) * 0.05, 'Wl': jax.random.normal(ks[4], (N_LAYERS, RANK, RANK), dtype=jnp.float32) * 0.05, 'Wa': jax.random.normal(ks[5], (N_LAYERS, RANK, RANK), dtype=jnp.float32) * 0.05, 'src': jax.random.randint(ks[6], (N_EDGES,), 0, N_ENTS, dtype=jnp.int32), 'dst': jax.random.randint(ks[7], (N_EDGES,), 0, N_ENTS, dtype=jnp.int32), 'etype': jax.random.randint(ks[8], (N_EDGES,), 0, N_RELS, dtype=jnp.int32)}
    _L3_gnn_all = _L3_gnn_setup()
    _L3_gnn_in = {k: v for k, v in _L3_gnn_all.items() if k in ('rel_emb', 'Wn', 'Wl', 'Wa')}
    del _L3_gnn_all
    return {'x': x, 'src': src, 'dst': dst, 'edge_type_200': edge_type_200, 'L0_gnn_W_l': _L0_gnn_in['W_l'], 'L0_gnn_b_l': _L0_gnn_in['b_l'], 'L0_gnn_W_r': _L0_gnn_in['W_r'], 'L0_gnn_b_r': _L0_gnn_in['b_r'], 'L0_gnn_att': _L0_gnn_in['att'], 'L0_gnn_bias': _L0_gnn_in['bias'], 'L0_gnn_gamma': _L0_gnn_in['gamma'], 'L0_gnn_beta': _L0_gnn_in['beta'], 'L1_gnn_kernel': _L1_gnn_in['kernel'], 'L1_gnn_kernel_attention': _L1_gnn_in['kernel_attention'], 'L2_gnn_query_kernel': _L2_gnn_in['query_kernel'], 'L2_gnn_query_bias': _L2_gnn_in['query_bias'], 'L2_gnn_key_kernel': _L2_gnn_in['key_kernel'], 'L2_gnn_key_bias': _L2_gnn_in['key_bias'], 'L2_gnn_kernel': _L2_gnn_in['kernel'], 'L2_gnn_bias': _L2_gnn_in['bias'], 'L3_gnn_rel_emb': _L3_gnn_in['rel_emb'], 'L3_gnn_Wn': _L3_gnn_in['Wn'], 'L3_gnn_Wl': _L3_gnn_in['Wl'], 'L3_gnn_Wa': _L3_gnn_in['Wa']}

def reference(x, src, dst, edge_type_200, L0_gnn_W_l, L0_gnn_b_l, L0_gnn_W_r, L0_gnn_b_r, L0_gnn_att, L0_gnn_bias, L0_gnn_gamma, L0_gnn_beta, L1_gnn_kernel, L1_gnn_kernel_attention, L2_gnn_query_kernel, L2_gnn_query_bias, L2_gnn_key_kernel, L2_gnn_key_bias, L2_gnn_kernel, L2_gnn_bias, L3_gnn_rel_emb, L3_gnn_Wn, L3_gnn_Wl, L3_gnn_Wa):
    import jax
    import jax.numpy as jnp

    def _L0_gnn_ref(x, edge_index, W_l, b_l, W_r, b_r, att, bias, gamma, beta):
        import jax, jax.numpy as jnp
        import numpy as np
        N, E = (12500, 200000)
        IN_C, H, C = (128, 4, 32)
        NEG_SLOPE = 0.2
        n = x.shape[0]
        x_l = (x @ W_l + b_l).reshape(n, H, C)
        x_r = (x @ W_r + b_r).reshape(n, H, C)
        loop = jnp.arange(n, dtype=edge_index.dtype)
        src = jnp.concatenate([edge_index[0], loop])
        dst = jnp.concatenate([edge_index[1], loop])
        e = jax.nn.leaky_relu(x_l[src] + x_r[dst], NEG_SLOPE)
        logits = jnp.einsum('ehc,hc->eh', e, att)
        m = jax.ops.segment_max(logits, dst, num_segments=n)
        m = jnp.where(jnp.isfinite(m), m, 0.0)
        p = jnp.exp(logits - jax.lax.stop_gradient(m)[dst])
        denom = jax.ops.segment_sum(p, dst, num_segments=n)
        alpha = p / (denom[dst] + 1e-16)
        msg = x_l[src] * alpha[:, :, None]
        out = jax.ops.segment_sum(msg, dst, num_segments=n)
        out = out.reshape(n, H * C) + bias
        mu = out.mean(axis=-1, keepdims=True)
        var = out.var(axis=-1, keepdims=True)
        out = (out - mu) * jax.lax.rsqrt(var + 1e-05) * gamma + beta
        return jax.nn.elu(out)

    def _L1_gnn_ref(node_states, edges, kernel, kernel_attention):
        import jax, jax.numpy as jnp
        import numpy as np
        N_NODES = 12500
        N_EDGES = 200000
        D_FEAT = 128
        UNITS = 128
        LEAKY_ALPHA = 0.2
        n = node_states.shape[0]
        tgt_idx = edges[:, 0]
        src_idx = edges[:, 1]
        h = node_states @ kernel
        ka_t = kernel_attention[:UNITS, 0]
        ka_s = kernel_attention[UNITS:, 0]
        score_t = h @ ka_t
        score_s = h @ ka_s
        e = score_t[tgt_idx] + score_s[src_idx]
        e = jax.nn.leaky_relu(e, negative_slope=LEAKY_ALPHA)
        e = jnp.exp(jnp.clip(e, -2.0, 2.0))
        sum_e = jax.ops.segment_sum(e, tgt_idx, num_segments=n)
        attention = e / (sum_e[tgt_idx] + 1e-09)
        messages = h[src_idx] * attention[:, None]
        output = jax.ops.segment_sum(messages, tgt_idx, num_segments=n)
        return output

    def _L2_gnn_ref(x, edge_index, query_kernel, query_bias, key_kernel, key_bias, kernel, bias):
        import jax, jax.numpy as jnp
        import numpy as np
        N = 6250
        E = 100000
        F = 128
        UNITS = 128
        ATT_UNITS = 128
        HEADS = 8

        def segment_softmax(scores, seg, num_segments):
            smax = jax.ops.segment_max(scores, seg, num_segments=num_segments)
            sexp = jnp.exp(scores - smax[seg])
            ssum = jax.ops.segment_sum(sexp, seg, num_segments=num_segments)
            return sexp / ssum[seg]
        num_nodes = x.shape[0]
        loop = jnp.arange(num_nodes, dtype=edge_index.dtype)
        row = jnp.concatenate([edge_index[0], loop])
        col = jnp.concatenate([edge_index[1], loop])
        Q = jax.nn.relu(x @ query_kernel + query_bias)[row]
        K = jax.nn.relu(x @ key_kernel + key_bias)[col]
        V = (x @ kernel)[col]
        Qh = Q.reshape(-1, HEADS, ATT_UNITS // HEADS)
        Kh = K.reshape(-1, HEADS, ATT_UNITS // HEADS)
        att = jnp.sum(Qh * Kh, axis=-1)
        alpha = segment_softmax(att, row, num_nodes)
        Vh = V.reshape(-1, HEADS, UNITS // HEADS)
        msg = Vh * alpha[:, :, None]
        out = jax.ops.segment_sum(msg, row, num_segments=num_nodes)
        out = out.reshape(num_nodes, UNITS)
        out = out + bias
        return out

    def _L3_gnn_ref(ent_emb, rel_emb, norm, Wn, Wl, Wa, src, dst, etype):
        import jax, jax.numpy as jnp
        import numpy as np
        N_ENTS = 6250
        N_EDGES = 62500
        N_RELS = 200
        RANK = 128
        N_LAYERS = 2
        RRELU_SLOPE = (1.0 / 8.0 + 1.0 / 3.0) / 2.0
        n = ent_emb.shape[0]
        in_deg = jax.ops.segment_sum(jnp.ones_like(dst, dtype=jnp.float32), dst, num_segments=n)
        has_in = (in_deg > 0)[:, None]
        h = ent_emb
        for l in range(Wn.shape[0]):
            msg = (h[src] + rel_emb[etype]) @ Wn[l]
            agg = jax.ops.segment_sum(msg, dst, num_segments=n) * norm
            loop = jnp.where(has_in, h @ Wl[l], h @ Wa[l])
            h = agg + loop
            h = jnp.where(h >= 0, h, h * RRELU_SLOPE)
        return h
    edge_index = jnp.stack([src, dst])
    edge_index_t = jnp.stack([src, dst], axis=1)
    deg = jnp.maximum(jax.ops.segment_sum(jnp.ones(dst.shape, jnp.float32), dst, num_segments=6250), 1.0)
    deg_isqrt = deg ** (-0.5)
    x = _layernorm(x + _L0_gnn_ref(x, edge_index, L0_gnn_W_l, L0_gnn_b_l, L0_gnn_W_r, L0_gnn_b_r, L0_gnn_att, L0_gnn_bias, L0_gnn_gamma, L0_gnn_beta), axis=-1)
    x = _layernorm(x + _L1_gnn_ref(x, edge_index_t, L1_gnn_kernel, L1_gnn_kernel_attention), axis=-1)
    x = _layernorm(x + _L2_gnn_ref(x, edge_index, L2_gnn_query_kernel, L2_gnn_query_bias, L2_gnn_key_kernel, L2_gnn_key_bias, L2_gnn_kernel, L2_gnn_bias), axis=-1)
    x = _layernorm(x + _L3_gnn_ref(x, L3_gnn_rel_emb, deg_isqrt[:, None], L3_gnn_Wn, L3_gnn_Wl, L3_gnn_Wa, src, dst, edge_type_200), axis=-1)
    return x

_drawn_inputs = setup_inputs


def setup_inputs(seed=0):
    import zlib

    import numpy as np

    out = dict(_drawn_inputs(seed))
    spreads = {'L0_gnn_b_l': (0.0, 0.1),
     'L0_gnn_b_r': (0.0, 2.0),
     'L0_gnn_bias': (0.0, 0.1),
     'L0_gnn_gamma': (1.0, 0.2),
     'L0_gnn_beta': (0.0, 0.1),
     'L2_gnn_query_bias': (0.0, 0.294),
     'L2_gnn_key_bias': (0.0, 0.443),
     'L2_gnn_bias': (0.0, 0.1)}
    factors = {'L0_gnn_W_r': 3.642, 'L3_gnn_Wa': 30.128}
    for name, (base, spread) in spreads.items():
        noise = np.random.default_rng([zlib.crc32(name.encode()), seed]).standard_normal(out[name].shape)
        drawn = base * np.exp(spread * noise) if base else spread * noise
        out[name] = jnp.asarray(drawn.astype(out[name].dtype))
    for name, factor in factors.items():
        out[name] = (out[name] * factor).astype(out[name].dtype)
    return out
```

```python
from contextlib import ExitStack

import numpy as np
import concourse.bass as bass
from concourse import mybir

F32 = mybir.dt.float32
BF16 = mybir.dt.bfloat16
I32 = mybir.dt.int32
ALU = mybir.AluOpType
ACT = mybir.ActivationFunctionType
AX = mybir.AxisListType

P = 128
N, E, D = 6250, 100000, 128
NT = -(-N // P)
NP = NT * P
NW = NP + P
ET = 125
UT = E // ET
UG = 8
US = UT // UG
G = 4
RING = 4
T = -(-(E + NP) // (P * G * RING)) * G * RING
GROUPS = T // G
POS = T * P
PADS = POS - E - NP
TB = 104
NBLK = T // TB
BIG = 1e30
LEAK = 0.2
RRELU = (1.0 / 8.0 + 1.0 / 3.0) / 2.0
LN_EPS = 1e-5
RELS = 200
CB = 7
CW = CB * P
CS = NP // CW
HW = CW // 2


def replicate(ap, dim, count):
    a = ap.unsqueeze(dim)
    shape = list(a.shape)
    shape[dim] = count
    return a.to_broadcast(shape)


class Kit:

    def __init__(self, nc, stack):
        self.nc, self.stack, self.sems = nc, stack, 0

    def sb(self, name, shape, dt=F32):
        return self.stack.enter_context(self.nc.sbuf_tensor(name, shape, dt))

    def ps(self, name, shape, dt=F32):
        size = int(np.prod(shape[1:]))
        bank = 512 if dt == F32 else 1024
        t = self.stack.enter_context(self.nc.psum_tensor(name, [shape[0], -(-size // bank) * bank], dt))
        letters = "abcd"[:len(shape) - 1]
        sizes = {x: n for x, n in zip(letters[1:], shape[2:])}
        return t[:, 0:size].rearrange(f"p ({' '.join(letters)}) -> p {' '.join(letters)}", **sizes)

    def sem(self, name):
        if not self.sems:
            self.stack.callback(self.nc.all_engine_barrier)
        self.sems += 1
        sem = self.stack.enter_context(self.nc.semaphore(name))
        self.stack.callback(self.nc.sync.sem_clear, sem)
        return sem


def staggered(eng, emit, lag):
    for k in range(RING):
        emit(k, k % RING)
    with eng.Fori(1, GROUPS // RING) as m:
        for q in range(RING):
            emit(m * RING + q, q)
    for k in range(GROUPS, GROUPS + lag):
        emit(k, k % RING)


def in_pairs(eng, body):
    body(0)
    with eng.Fori(1, US // 2) as m:
        body(m)


def inside(k, lag):
    return not isinstance(k, int) or 0 <= k - lag < GROUPS


def wait_count(eng, sem, value):
    if not isinstance(value, int) or value > 0:
        eng.wait_ge(sem, value)


def turn4(k, lag=0):
    return (k - lag) // RING


def turn2(k, lag=0):
    return (k - lag) // 2


def constants(nc, c):
    with ExitStack() as st:
        kit = Kit(nc, st)
        cst_done, cst_int, cst_cast = kit.sem("cst_done"), kit.sem("cst_int"), kit.sem("cst_cast")
        io = kit.sb("iota_int", [P, P], I32)
        nodes = kit.sb("nodes_int", [P, NT], I32)
        block = st.enter_context(nc.Block())

        @block.gpsimd
        def _(pool):
            n = 0
            for t, v in ((c.ident, 0.0), (c.identb, 0.0), (c.ones, 1.0), (c.mean_w, 1.0 / D),
                         (c.before, 1.0), (c.after, 1.0), (c.first_row, 0.0), (c.hsel4, 1.0), (c.hsel8, 1.0),
                         (c.one_row, 1.0), (c.eps, LN_EPS)):
                pool.memset(t[:], v).then_inc(cst_done, 1)
                n += 1
            pool.iota(io[:], pattern=[[1, P]], base=0, channel_multiplier=0).then_inc(cst_int, 1)
            pool.iota(nodes[:], pattern=[[P, NT]], base=0, channel_multiplier=1).then_inc(cst_int, 1)
            pool.wait_ge(cst_done, n)
            for t in (c.ident, c.identb):
                pool.affine_select(out=t[:], in_=t[:], compare_op=ALU.not_equal, fill=1.0, base=0,
                                   pattern=[[-1, P]], channel_multiplier=1).then_inc(cst_done, 1)
            pool.affine_select(out=c.before[:], in_=c.before[:], compare_op=ALU.is_gt, fill=0.0, base=0,
                               pattern=[[1, P]], channel_multiplier=-1).then_inc(cst_done, 1)
            pool.affine_select(out=c.after[:], in_=c.after[:], compare_op=ALU.is_gt, fill=0.0, base=0,
                               pattern=[[-1, P]], channel_multiplier=1).then_inc(cst_done, 1)
            pool.affine_select(out=c.first_row[:], in_=c.first_row[:], compare_op=ALU.not_equal, fill=1.0,
                               base=0, pattern=[[0, P]], channel_multiplier=1).then_inc(cst_done, 1)
            for t, heads in ((c.hsel4, 4), (c.hsel8, 8)):
                w = D // heads
                pool.affine_select(out=t[:], in_=t[:], compare_op=ALU.is_ge, fill=0.0, base=0,
                                   pattern=[[1, P]], channel_multiplier=-w).then_inc(cst_done, 1)
                n += 1
                pool.wait_ge(cst_done, n + 5)
                pool.affine_select(out=t[:], in_=t[:], compare_op=ALU.is_ge, fill=0.0, base=w - 1,
                                   pattern=[[-1, P]], channel_multiplier=w).then_inc(cst_done, 1)
                n += 1

        @block.vector
        def _(dve):
            dve.wait_ge(cst_int, 2)
            dve.tensor_copy(c.iota_f[:], io[:]).then_inc(cst_cast, 1)
            dve.tensor_copy(c.iota_b[:], io[:]).then_inc(cst_cast, 1)
            dve.tensor_copy(c.node_id[:], nodes[:]).then_inc(cst_cast, 1)


def edge_columns(nc, c, src, dst, etype):
    with ExitStack() as st:
        kit = Kit(nc, st)
        rows = kit.sb("edge_rows", [100, 3, UG, ET], I32)
        rows_f = kit.sb("edge_rows_f", [100, 3, UG, ET])
        cols_i = kit.sb("edge_cols_i", [ET, 2, UT], I32)
        part_i = kit.sb("edge_part_i", [ET, 2, UT], I32)
        ps = [kit.ps(f"edge_ps{i}", [ET, UG // 2, P]) for i in range(6)]
        loaded, floated, turned, copied = (kit.sem(n) for n in
                                           ("edges_loaded", "edges_floated", "edges_turned", "edges_copied"))
        block = st.enter_context(nc.Block())

        @block.sync
        def _(sp):
            for f, a in enumerate((src, dst, etype)):
                sp.dma_start(rows[:, f], a.rearrange("(b t j) -> t b j", b=UG, j=ET)).then_inc(loaded, 16)

        @block.tensor
        def _(pe):
            pe.wait_ge(floated, 1)
            for f in range(3):
                for b in range(UG):
                    mm = pe.transpose(ps[2 * f + b // 4][:, b % 4, 0:100], rows_f[:, f, b, :],
                                      c.ident[0:100, 0:100])
            mm.then_inc(turned, 1)

        @block.vector
        def _(dve):
            dve.wait_ge(loaded, 48)
            dve.tensor_copy(rows_f[:], rows[:]).then_inc(floated, 1)
            dve.wait_ge(turned, 1)
            for f in range(3):
                for h in range(2):
                    cols = c.edge[:, f, 400 * h:400 * h + 400].rearrange("p (b t) -> p b t", b=4)
                    dve.tensor_copy(cols, ps[2 * f + h][:, :, 0:100]).then_inc(copied, 1)
            dve.wait_ge(copied, 6)
            dve.tensor_copy(cols_i[:], c.edge[:, 0:2, :]).then_inc(copied, 1)
            dve.wait_ge(copied, 7)
            dve.tensor_single_scalar(part_i[:], cols_i[:], 7, ALU.arith_shift_right).then_inc(copied, 1)
            dve.wait_ge(copied, 8)
            dve.tensor_copy(c.high[:], part_i[:]).then_inc(copied, 1)
            dve.wait_ge(copied, 9)
            dve.tensor_single_scalar(part_i[:], cols_i[:], P - 1, ALU.bitwise_and).then_inc(copied, 1)
            dve.wait_ge(copied, 10)
            dve.tensor_copy(c.low[:], part_i[:]).then_inc(copied, 1)


def counting_sort(nc, c, key, key_dram, sorted_rows):
    name = ("src", "dst")[key]
    with ExitStack() as st:
        kit = Kit(nc, st)
        lo = kit.sb(f"{name}_lo", [ET, 2, UG, P], BF16)
        hi = kit.sb(f"{name}_hi", [ET, 2, UG, NT], BF16)
        zero_lo = kit.sb(f"{name}_zero_lo", [ET, P], BF16)
        lo_t = kit.sb(f"{name}_lo_t", [P, 2, UG, ET])
        key_row = kit.sb(f"{name}_key_row", [ET, 2, UG, ET], I32)
        table = kit.sb(f"{name}_table", [P, UG + 1, NT])
        count = kit.sb(f"{name}_count", [P, NT])
        ahead = kit.sb(f"{name}_ahead", [P, NT])
        total = kit.sb(f"{name}_total", [P, NT])
        begin = kit.sb(f"{name}_begin", [P, NT])
        begin_i = kit.sb(f"{name}_begin_i", [P, NT], I32)
        self_row = kit.sb(f"{name}_self_row", [P, NT, 4])
        pad_row = kit.sb(f"{name}_pad_row", [PADS // 2, 2, 4])
        payload = kit.sb(f"{name}_payload", [ET, UT, 4])
        staged = kit.sb(f"{name}_staged", [ET, 2, UG, 4])
        same = kit.sb(f"{name}_same", [ET, UG, ET])
        same2 = kit.sb(f"{name}_same2", [ET, UG, ET])
        picked = kit.sb(f"{name}_picked", [ET, UG, NT])
        rank = kit.sb(f"{name}_rank", [ET, UG])
        base = kit.sb(f"{name}_base", [ET, UG])
        position = kit.sb(f"{name}_position", [ET, 2, UG], I32)
        zero_nt = kit.sb(f"{name}_zero_nt", [P, NT])
        ps_count = kit.ps(f"{name}_ps_count", [P, 512])
        ps_pre = kit.ps(f"{name}_ps_pre", [P, 2, NT])
        ps_hist = [kit.ps(f"{name}_ps_hist{i}", [P, UG, NT]) for i in range(2)]
        ps_lo_t = [kit.ps(f"{name}_ps_lo_t{i}", [P, UG, P], BF16) for i in range(2)]
        ps_base = kit.ps(f"{name}_ps_base", [ET, UG, NT])
        prep, zeroed, onehot, counted, off, prefixed, begun = (kit.sem(f"{name}_{n}") for n in
                                                 ("prep", "zeroed", "onehot", "counted", "off", "prefixed", "begun"))
        onehot2, hist_done, turned, turn_copied, table_done, base_done = (
            kit.sem(f"{name}_{n}") for n in
            ("onehot2", "hist_done", "turned", "turn_copied", "table_done", "base_done"))
        chain, pos_done, pay_done = (kit.sem(f"{name}_{n}") for n in ("chain", "pos_done", "pay_done"))
        fenced = kit.sem(f"{name}_fenced")
        row_in = [kit.sem(f"{name}_row_in{i}") for i in range(2)]
        *sent, self_sent = c.pool_dma[0:3]
        before = list(c.pool_count)
        keys_by_step = key_dram.rearrange("(s n) -> s n", s=US)
        block = st.enter_context(nc.Block())

        def one_hots(dve, s, b, sem):
            low = c.low[:, key, bass.ds(s * UG, UG)]
            high = c.high[:, key, bass.ds(s * UG, UG)]
            dve.tensor_tensor(lo[:, b], replicate(low, 2, P), replicate(c.iota_b[0:ET, :], 1, UG),
                              ALU.is_equal).then_inc(sem, 1)
            dve.tensor_tensor(hi[:, b], replicate(high, 2, NT), replicate(c.iota_b[0:ET, 0:NT], 1, UG),
                              ALU.is_equal).then_inc(sem, 1)

        @block.vector
        def _(dve):
            dve.memset(zero_lo[:], 0.0).then_inc(zeroed, 1)
            def two_steps(m):
                for b in range(2):
                    wait_count(dve, counted, m * 2 + b)
                    one_hots(dve, m * 2 + b, b, onehot)
            in_pairs(dve, two_steps)
            dve.wait_ge(counted, US + 1)
            dve.tensor_single_scalar(count[:], ps_count[:, 0:NT], 1.0, ALU.add).then_inc(off, 1)
            dve.wait_ge(prefixed, 1)
            dve.tensor_copy(ahead[:], ps_pre[:, 0]).then_inc(chain, 1)
            dve.tensor_copy(total[:], ps_pre[:, 1]).then_inc(chain, 1)
            dve.memset(zero_nt[:], 0.0).then_inc(chain, 1)
            dve.wait_ge(chain, 3)
            dve.tensor_tensor_scan(begin[:], total[:], zero_nt[:], 0.0, ALU.add, ALU.add).then_inc(chain, 1)
            dve.wait_ge(chain, 4)
            dve.tensor_tensor(begin[:], begin[:], total[:], ALU.subtract).then_inc(chain, 1)
            dve.wait_ge(chain, 5)
            dve.tensor_tensor(begin[:], begin[:], ahead[:], ALU.add).then_inc(chain, 1)
            dve.wait_ge(chain, 6)
            dve.tensor_copy(begin_i[:], begin[:]).then_inc(begun, 1)
            dve.tensor_single_scalar(table[:, 0], begin[:], 1.0, ALU.add).then_inc(chain, 1)
            dve.wait_ge(chain, 7)
            def two_steps(m):
                for b in range(2):
                    s = m * 2 + b
                    cb = s * 6 + 7
                    one_hots(dve, s, b, onehot2)
                    dve.wait_ge(row_in[b], m * 16 + 16)
                    keys = c.edge[:, key, bass.ds(s * UG, UG)]
                    dve.tensor_tensor(same[:], key_row[:, b], replicate(keys, 2, ET), ALU.is_equal)\
                       .then_inc(chain, 1)
                    dve.wait_ge(chain, cb + 1)
                    dve.tensor_tensor(same2[:], same[:], replicate(c.after[0:ET, 0:ET], 1, UG), ALU.mult)\
                       .then_inc(chain, 1)
                    dve.wait_ge(chain, cb + 2)
                    dve.tensor_reduce(rank[:], same2[:], AX.X, ALU.add).then_inc(chain, 1)
                    dve.wait_ge(hist_done, s + 1)
                    for g in range(UG):
                        if g:
                            wait_count(dve, table_done, s * UG + g)
                        dve.tensor_tensor(table[:, g + 1], table[:, g], ps_hist[b][:, g], ALU.add)\
                           .then_inc(table_done, 1)
                    dve.wait_ge(base_done, s + 1)
                    dve.tensor_tensor(picked[:], ps_base[:], hi[:, b], ALU.mult).then_inc(chain, 1)
                    dve.wait_ge(table_done, s * UG + UG)
                    dve.tensor_copy(table[:, 0], table[:, UG]).then_inc(chain, 1)
                    dve.wait_ge(chain, cb + 5)
                    dve.tensor_reduce(base[:], picked[:], AX.X, ALU.add).then_inc(chain, 1)
                    dve.wait_ge(chain, cb + 6)
                    wait_count(dve, sent[b], before[b] + m * (16 * UG))
                    dve.tensor_tensor(position[:, b], base[:], rank[:], ALU.add).then_inc(pos_done, 1)
            in_pairs(dve, two_steps)

        @block.tensor
        def _(pe):
            pe.wait_ge(zeroed, 1)
            pe.matmul(ps_count[:, 0:NT], zero_lo[:], zero_lo[:, 0:NT], start=True, stop=False,
                      skip_group_check=True).then_inc(counted, 1)
            def two_steps(m):
                for b in range(2):
                    pe.wait_ge(onehot, (m * 2 + b) * 2 + 2)
                    for g in range(UG):
                        mm = pe.matmul(ps_count[:, 0:NT], lo[:, b, g], hi[:, b, g], start=False, stop=False,
                                       skip_group_check=True)
                    mm.then_inc(counted, 1)
            in_pairs(pe, two_steps)
            pe.wait_ge(off, 1)
            pe.matmul(ps_pre[:, 0], c.before[:], count[:], start=True, stop=True)
            pe.matmul(ps_pre[:, 1], c.ones[:], count[:], start=True, stop=True).then_inc(prefixed, 1)
            def two_steps(m):
                for b in range(2):
                    s = m * 2 + b
                    pe.wait_ge(onehot2, s * 2 + 2)
                    for g in range(UG):
                        mm = pe.transpose(ps_lo_t[b][:, g, 0:ET], lo[:, b, g], c.identb[0:ET, 0:ET])
                    mm.then_inc(turned, 1)
                    for g in range(UG):
                        mm = pe.matmul(ps_hist[b][:, g], lo[:, b, g], hi[:, b, g], start=True, stop=True)
                    mm.then_inc(hist_done, 1)
                    pe.wait_ge(turn_copied, s + 1)
                    pe.wait_ge(table_done, s * UG + UG - 1)
                    for g in range(UG):
                        mm = pe.matmul(ps_base[:, g], lo_t[:, b, g], table[:, g], start=True, stop=True)
                    mm.then_inc(base_done, 1)
            in_pairs(pe, two_steps)

        @block.scalar
        def _(act):
            act.activation(payload[:, :, 0], c.edge[:, 1 - key, :], ACT.Copy).then_inc(pay_done, 1)
            act.activation(payload[:, :, 1], c.edge[:, key, :], ACT.Copy).then_inc(pay_done, 1)
            act.activation(payload[:, :, 2], c.edge[:, 2, :], ACT.Copy).then_inc(pay_done, 1)
            act.wait_ge(pay_done, 3)
            act.wait_ge(prep, 6)
            def two_steps(m):
                for b in range(2):
                    s = m * 2 + b
                    act.wait_ge(turned, s + 1)
                    act.activation(lo_t[:, b], ps_lo_t[b][:, :, 0:ET], ACT.Copy).then_inc(turn_copied, 1)
                    wait_count(act, sent[b], before[b] + m * (16 * UG))
                    act.activation(staged[:, b], payload[:, bass.ds(s * UG, UG), :], ACT.Copy)\
                       .then_inc(pay_done, 1)
            in_pairs(act, two_steps)

        @block.sync
        def _(sp):
            def two_steps(m):
                for b in range(2):
                    s = m * 2 + b
                    wait_count(sp, pos_done, m * 2)
                    row = keys_by_step[bass.ds(s, 1), :].to_broadcast([ET, UG * ET])
                    sp.dma_start(key_row[:, b].rearrange("p g j -> p (g j)"), row).then_inc(row_in[b], 16)
            in_pairs(sp, two_steps)

        @block.gpsimd
        def _(pool):
            pool.memset(payload[:, :, 3], 1.0).then_inc(prep, 1)
            pool.tensor_copy(self_row[:, :, 0], c.node_id[:]).then_inc(prep, 1)
            pool.tensor_copy(self_row[:, :, 1], c.node_id[:]).then_inc(prep, 1)
            pool.memset(self_row[:, :, 2:4], 0.0).then_inc(prep, 1)
            pool.memset(pad_row[:, :, 0:2], float(NP - 1)).then_inc(prep, 1)
            pool.memset(pad_row[:, :, 2:4], 0.0).then_inc(prep, 1)
            pool.wait_ge(prep, 6)
            pool.dma_start(sorted_rows[E + NP:POS, :].rearrange("(p n) f -> p (n f)", n=2),
                           pad_row[:].rearrange("p n f -> p (n f)")).then_inc(self_sent, 16)
            pool.wait_ge(begun, 1)
            for b in range(NT):
                pool.indirect_dma_start(sorted_rows, bass.IndirectOffsetOnAxis(ap=begin_i[:, b:b + 1], axis=0),
                                        self_row[:, b, :], None).then_inc(self_sent, 16)
            def two_steps(m):
                for b in range(2):
                    s = m * 2 + b
                    pool.wait_ge(pay_done, s + 4)
                    wait_count(pool, fenced, s)
                    pool.wait_ge(pos_done, s + 1)
                    pool.tensor_tensor(c.fence[:], c.ones[0:1, 0:1], c.ones[0:1, 0:1], ALU.add)\
                        .then_inc(fenced, 1)
                    for g in range(UG):
                        pool.indirect_dma_start(
                            sorted_rows, bass.IndirectOffsetOnAxis(ap=position[:, b, g:g + 1], axis=0),
                            staged[:, b, g, :], None).then_inc(sent[b], 16)
            in_pairs(pool, two_steps)
            pool.wait_ge(self_sent, before[2] + 16 * (NT + 1))
            for b in range(2):
                wait_count(pool, sent[b], before[b] + 16 * UG * (US // 2))
        c.pool_count[0:3] = [before[0] + 8 * UG * US, before[1] + 8 * UG * US, before[2] + 16 * (NT + 1)]


def read_sorted(nc, c, name, sorted_rows, runs, slot, real_slot, first, neighbour, etype):
    with ExitStack() as st:
        kit = Kit(nc, st)
        rows = kit.sb(f"{name}_rows", [TB, NBLK, P, 4])
        start = kit.sb(f"{name}_start", [TB, NBLK, 2, P])
        cols = kit.sb(f"{name}_cols", [P, 4, T])
        tmp = kit.sb(f"{name}_tmp", [P, T])
        ps = [kit.ps(f"{name}_ps{i}", [P, 4, P]) for i in range(2)]
        ps_first = [kit.ps(f"{name}_ps_first{i}", [P, T // 2]) for i in range(2)]
        loaded, turned, copied, step, stored = (kit.sem(f"{name}_back_{n}") for n in
                                                ("loaded", "turned", "copied", "step", "stored"))
        block = st.enter_context(nc.Block())
        n_steps = 8 + (etype is not None)

        @block.sync
        def _(sp):
            view = sorted_rows.rearrange("(b t p) f -> t b (p f)", t=TB, p=P)
            sp.dma_start(rows[:].rearrange("t b p f -> t b (p f)"), view).then_inc(loaded, 16)
            sp.wait_ge(step, 3)
            for kind in range(2):
                view = runs[kind].rearrange("(b t p) -> t b p", t=TB, p=P)
                sp.dma_start(view, start[:, :, kind, :]).then_inc(stored, 16)
            sp.wait_ge(stored, 32)

        @block.tensor
        def _(pe):
            pe.wait_ge(loaded, 16)
            for b in range(NBLK):
                if b >= 2:
                    pe.wait_ge(copied, b - 1)
                for f in range(4):
                    mm = pe.transpose(ps[b % 2][:, f, 0:TB], rows[:, b, :, f], c.ident[0:TB, 0:TB])
                mm.then_inc(turned, 1)
            pe.wait_ge(copied, NBLK)
            for h in range(2):
                mm = pe.matmul(ps_first[h][:], c.first_row[:], cols[:, 1, h * (T // 2):(h + 1) * (T // 2)],
                               start=True, stop=True)
            mm.then_inc(turned, 1)

        @block.scalar
        def _(act):
            for b in range(NBLK):
                act.wait_ge(turned, b + 1)
                act.activation(cols[:, :, b * TB:(b + 1) * TB], ps[b % 2][:, :, 0:TB], ACT.Copy)\
                   .then_inc(copied, 1)

        @block.vector
        def _(dve):
            dve.wait_ge(loaded, 16)
            dve.tensor_scalar(start[:, :, 0, :], rows[:, :, :, 3], BIG, BIG, ALU.mult, ALU.subtract)\
               .then_inc(step, 1)
            dve.memset(start[:, :, 1, P - 1:P], -BIG).then_inc(step, 1)
            dve.tensor_scalar(start[:, :, 1, 0:P - 1], rows[:, :, 1:P, 3], BIG, BIG, ALU.mult, ALU.subtract)\
               .then_inc(step, 1)
            dve.wait_ge(turned, NBLK + 1)
            for h in range(2):
                part = slice(h * (T // 2), (h + 1) * (T // 2))
                dve.tensor_tensor(slot[:, part], cols[:, 1, part], ps_first[h][:], ALU.subtract)\
                   .then_inc(step, 1)
            dve.wait_ge(step, 5)
            dve.tensor_single_scalar(tmp[:], slot[:], 1.0, ALU.add).then_inc(step, 1)
            dve.wait_ge(step, 6)
            dve.tensor_tensor(tmp[:], tmp[:], cols[:, 3, :], ALU.mult).then_inc(step, 1)
            dve.wait_ge(step, 7)
            dve.tensor_single_scalar(real_slot[:], tmp[:], -1.0, ALU.add).then_inc(step, 1)
            dve.tensor_copy(neighbour[:], cols[:, 0, :]).then_inc(step, 1)
            dve.tensor_copy(first[:], cols[0:1, 1, :]).then_inc(step, 1)
            if etype is not None:
                dve.tensor_copy(etype[:], cols[:, 2, :]).then_inc(step, 1)


def gather_rows(pool, c, k, q, slots, table, index, rows, staged, landed):
    pool.tensor_copy(slots[:, q], index[:, bass.ds(k * G, G)]).then_inc(staged, 1)
    pool.wait_ge(staged, k * 2 + 1)
    pool.tensor_tensor(c.fence[:], c.ones[0:1, 0:1], c.ones[0:1, 0:1], ALU.add).then_inc(staged, 1)
    for g in range(G):
        pool.indirect_dma_start(rows[:, q, g, :], None, table,
                                bass.IndirectOffsetOnAxis(ap=slots[:, q, g:g + 1], axis=0)).then_inc(landed[q], 16)


def window_start(eng, first, k, g):
    return eng.value_load(first[0:1, bass.ds(k * G + g, 1)], min_val=0, max_val=NP - 1)


def attention_pass(nc, c, name, heads, dot, table, window_table, runs, slot, first, index):
    width = D // heads
    rw = 2 * D if dot else D
    v0 = rw - D
    with ExitStack() as st:
        kit = Kit(nc, st)
        slots = kit.sb(f"{name}_slots", [P, RING, G], I32)
        rows = kit.sb(f"{name}_rows", [P, RING, G, rw])
        win = kit.sb(f"{name}_win", [P, 2, G, D])
        run = kit.sb(f"{name}_run", [heads, 2, 2, G * P])
        sel = kit.sb(f"{name}_sel", [P, RING, G, P])
        sel_t = kit.sb(f"{name}_sel_t", [P, 2, G, P])
        z = kit.sb(f"{name}_z", [P, 2, G, D])
        score = kit.sb(f"{name}_score", [P, 2, G, heads])
        prefix = kit.sb(f"{name}_prefix", [heads, 2, G * P])
        top = kit.sb(f"{name}_top", [heads, 2, G * P])
        drop = kit.sb(f"{name}_drop", [heads, 2, G])
        less = kit.sb(f"{name}_less", [P, 2, G, heads])
        weight = kit.sb(f"{name}_weight", [P, 2, G, D])
        keep = kit.sb(f"{name}_keep", [P, RING, G])
        val = kit.sb(f"{name}_val", [P, 2, G, D])
        ps_t = kit.ps(f"{name}_ps_t", [P, G, P])
        ps_x = kit.ps(f"{name}_ps_x", [P, G, D])
        ps_s = kit.ps(f"{name}_ps_s", [heads, G * P])
        ps_m = kit.ps(f"{name}_ps_m", [P, G * heads + G])
        ps_n = [kit.ps(f"{name}_ps_n{i}", [P, 2, 2, P]) for i in range(4)]
        hsel = c.hsel4 if heads == 4 else c.hsel8
        (staged, sel_done, selt_ps, selt_done, spread_done, z_done, leaky_done, prod_done, score_done,
         score_t, prefix_done, top_done, drop_done, top_ps, less_done, exp_done, val_done, sums_done,
         copy_done, head_done, cleared) = (
            kit.sem(f"{name}_{n}") for n in
            ("staged", "sel_done", "selt_ps", "selt_done", "spread_done", "z_done", "leaky_done",
             "prod_done", "score_done", "score_t", "prefix_done", "top_done", "drop_done", "top_ps",
             "less_done", "exp_done", "val_done", "sums_done", "copy_done", "head_done", "cleared"))
        chain, first_prefix = kit.sem(f"{name}_chain"), kit.sem(f"{name}_first_prefix")
        landed, landed_before = c.pool_dma, list(c.pool_count)
        win_in = [kit.sem(f"{name}_win_in{i}") for i in range(2)]
        run_in = [kit.sem(f"{name}_run_in{i}") for i in range(2)]
        block = st.enter_context(nc.Block())

        @block.sync
        def _(sp):
            def emit(k, q):
                if inside(k, 0):
                    b = q % 2
                    starts = [window_start(sp, first, k, g) for g in range(G)]
                    wait_count(sp, spread_done, k - 1)
                    for g in range(G):
                        sp.dma_start(win[:, b, g, :], window_table[bass.ds(starts[g], P), :])\
                          .then_inc(win_in[b], 16)
                    wait_count(sp, top_done, k - 1)
                    rows_of = runs[:, bass.ds(k * G * P, G * P)]
                    sp.dma_start(run[:, b], replicate(rows_of, 0, heads)).then_inc(run_in[b], 16)
            staggered(sp, emit, 0)

        @block.gpsimd
        def _(pool):
            pool.memset(c.num[:], 0.0).then_inc(cleared, 1)

            def emit(k, q):
                if inside(k, 0):
                    wait_count(pool, val_done, k - RING + 1)
                    gather_rows(pool, c, k, q, slots, table, index, rows, staged, landed)
            staggered(pool, emit, 0)

        @block.tensor
        def _(pe):
            def emit(k, q):
                b = q % 2
                if inside(k, 0):
                    pe.wait_ge(sel_done, k + 1)
                    wait_count(pe, selt_done, k)
                    for g in range(G):
                        mm = pe.transpose(ps_t[:, g], sel[:, q, g], c.ident[:])
                    mm.then_inc(selt_ps, 1)
                if inside(k, 2):
                    p = (q - 2) % RING
                    pe.wait_ge(val_done, k - 1)
                    wait_count(pe, copy_done, (k - 2 - 1) * G)
                    wait_count(pe, head_done, (k - 2 - 1) * G)
                    for g in range(G):
                        out = ps_n[2 * b + g // 2][:, g % 2]
                        pe.matmul(out[:, 0], val[:, b, g], sel[:, p, g], start=True, stop=True)
                        mm = pe.matmul(out[:, 1], weight[:, b, g], sel[:, p, g], start=True, stop=True)
                    mm.then_inc(sums_done, 1)
                if inside(k, 1):
                    o = (q - 1) % 2
                    pe.wait_ge(score_done, k)
                    wait_count(pe, prefix_done, k - 1)
                    for g in range(G):
                        mm = pe.matmul(ps_s[:, g * P:(g + 1) * P], score[:, o, g], c.ident[:],
                                       start=True, stop=True)
                    mm.then_inc(score_t, 1)
                if inside(k, 0):
                    pe.wait_ge(selt_done, k + 1)
                    pe.wait_ge(win_in[b], turn2(k) * (16 * G) + 16 * G)
                    wait_count(pe, z_done, k)
                    for g in range(G):
                        mm = pe.matmul(ps_x[:, g], sel_t[:, b, g], win[:, b, g], start=True, stop=True)
                    mm.then_inc(spread_done, 1)
                if inside(k, 1):
                    o = (q - 1) % 2
                    pe.wait_ge(drop_done, k)
                    wait_count(pe, exp_done, k - 1)
                    for g in range(G):
                        pe.matmul(ps_m[:, g * heads:(g + 1) * heads], top[:, o, g * P:(g + 1) * P],
                                  c.ident[0:heads, 0:heads], start=True, stop=True)
                    pe.matmul(ps_m[:, G * heads:], hsel[:], drop[:, o], start=True, stop=True)\
                      .then_inc(top_ps, 1)
            staggered(pe, emit, 2)

        @block.scalar
        def _(act):
            def emit(k, q):
                b = q % 2
                if inside(k, 0):
                    act.wait_ge(selt_ps, k + 1)
                    wait_count(act, spread_done, k - 1)
                    act.activation(sel_t[:, b], ps_t, ACT.Copy).then_inc(selt_done, 1)
                if inside(k, 2):
                    for g in range(G):
                        n0 = window_start(act, first, k - 2, g)
                        if g == 0:
                            act.wait_ge(sums_done, k - 1)
                            act.wait_ge(cleared, 1)
                        wait_count(act, copy_done, (k - 2) * G + g)
                        act.activation(c.num[:, :, bass.ds(n0 + 1, P - 1)],
                                       ps_n[2 * b + g // 2][:, g % 2, :, 1:P], ACT.Copy)\
                           .then_inc(copy_done, 1)
                if inside(k, 1):
                    o, p = (q - 1) % 2, (q - 1) % RING
                    act.wait_ge(less_done, k)
                    wait_count(act, sums_done, k - 2)
                    act.activation(weight[:, o].rearrange("p g (h c) -> p (g h) c", h=heads),
                                   replicate(less[:, o].rearrange("p g h -> p (g h)"), 2, width), ACT.Exp)
                    wait_count(act, head_done, (k - 3) * G)
                    act.activation(keep[:, p], ps_m[:, G * heads:], ACT.Exp).then_inc(exp_done, 1)
            staggered(act, emit, 2)

        @block.vector
        def _(dve):
            dve.memset(prefix[:, 1], 0.0).then_inc(first_prefix, 1)

            def emit(k, q):
                b = q % 2
                if inside(k, 0):
                    wait_count(dve, sums_done, k - RING + 1)
                    dve.tensor_tensor(sel[:, q], replicate(c.iota_f[:], 1, G),
                                      replicate(slot[:, bass.ds(k * G, G)], 2, P),
                                      ALU.is_equal).then_inc(sel_done, 1)
                if inside(k, 2):
                    p = (q - 2) % RING
                    dve.wait_ge(exp_done, k - 1)
                    wait_count(dve, sums_done, k - 3)
                    dve.tensor_tensor(val[:, b], rows[:, p, :, v0:], weight[:, b], ALU.mult).then_inc(val_done, 1)
                if inside(k, 1):
                    o, p = (q - 1) % 2, (q - 1) % RING
                    dve.wait_ge(z_done, k)
                    if not dot:
                        dve.scalar_tensor_tensor(z[:, o], z[:, o], LEAK, z[:, o], ALU.mult, ALU.max)\
                           .then_inc(leaky_done, 1)
                        dve.wait_ge(leaky_done, k)
                        dve.tensor_tensor(z[:, o], z[:, o], replicate(c.att[:], 1, G), ALU.mult)\
                           .then_inc(prod_done, 1)
                        dve.wait_ge(prod_done, k)
                    wait_count(dve, score_t, k - 2)
                    dve.tensor_reduce(score[:, o], z[:, o].rearrange("p g (h c) -> p g h c", h=heads),
                                      AX.X, ALU.add).then_inc(score_done, 1)
                    dve.wait_ge(score_t, k)
                    dve.wait_ge(run_in[o], turn2(k, 1) * 16 + 16)
                    if isinstance(k, int) and k == 1:
                        dve.wait_ge(first_prefix, 1)
                    dve.tensor_tensor_scan(prefix[:, o], run[:, o, 0], ps_s, prefix[:, 1 - o, G * P - 1:],
                                           ALU.add, ALU.max).then_inc(prefix_done, 1)
                    dve.wait_ge(prefix_done, k)
                    wait_count(dve, top_ps, k - 2)
                    dve.tensor_tensor_scan(top[:, o, ::-1], run[:, o, 1, ::-1], prefix[:, o, ::-1], -BIG,
                                           ALU.add, ALU.max).then_inc(top_done, 1)
                    dve.wait_ge(top_done, k)
                    dve.tensor_tensor(drop[:, o, 1:G], prefix[:, o, P - 1:(G - 1) * P:P],
                                      top[:, o, P::P], ALU.subtract).then_inc(chain, 1)
                    dve.tensor_tensor(drop[:, o, 0:1], prefix[:, 1 - o, G * P - 1:], top[:, o, 0:1],
                                      ALU.subtract).then_inc(chain, 1)
                    dve.wait_ge(chain, k * 2)
                    dve.tensor_single_scalar(drop[:, o], drop[:, o], 0.0, ALU.min).then_inc(drop_done, 1)
                if inside(k, 0):
                    dve.wait_ge(spread_done, k + 1)
                    dve.wait_ge(landed[q], landed_before[q] + turn4(k) * (16 * G) + 16 * G)
                    wait_count(dve, score_done, k - 1)
                    dve.tensor_tensor(z[:, b], ps_x, rows[:, q, :, 0:D], ALU.mult if dot else ALU.add)\
                       .then_inc(z_done, 1)
                if inside(k, 1):
                    o = (q - 1) % 2
                    dve.wait_ge(top_ps, k)
                    wait_count(dve, exp_done, k - 2)
                    dve.tensor_tensor(less[:, o], score[:, o],
                                      ps_m[:, 0:G * heads].rearrange("p (g h) -> p g h", g=G),
                                      ALU.subtract).then_inc(less_done, 1)
                if inside(k, 2):
                    p = (q - 2) % RING
                    for g in range(G):
                        n0 = window_start(dve, first, k - 2, g)
                        if g == 0:
                            dve.wait_ge(copy_done, (k - 1) * G)
                        wait_count(dve, head_done, (k - 2) * G + g)
                        if isinstance(k, int) and k == 2 and g == 0:
                            dve.wait_ge(cleared, 1)
                        at = c.num[:, :, bass.ds(n0, 1)]
                        dve.scalar_tensor_tensor(at, at, keep[:, p, g:g + 1],
                                                 ps_n[2 * b + g // 2][:, g % 2, :, 0:1],
                                                 ALU.mult, ALU.add).then_inc(head_done, 1)
            staggered(dve, emit, 2)
        c.pool_count = [n + 16 * T // RING for n in landed_before]


def edge_score_pass(nc, c, table, window_table, slot, real_slot, first, index):
    with ExitStack() as st:
        kit = Kit(nc, st)
        slots = kit.sb("l1_slots", [P, RING, G], I32)
        rows = kit.sb("l1_rows", [P, RING, G, D + 4])
        win = kit.sb("l1_win", [P, 2, G, 4])
        sel = kit.sb("l1_sel", [P, 2, G, P])
        sel_t = kit.sb("l1_sel_t", [P, 2, G, P])
        real = kit.sb("l1_real", [P, 2, G, P])
        scaled = kit.sb("l1_scaled", [P, 2, G, P])
        e = kit.sb("l1_e", [P, 2, 3, G])
        weight = kit.sb("l1_weight", [P, 2, G])
        ps_t = kit.ps("l1_ps_t", [P, G, P])
        ps_x = kit.ps("l1_ps_x", [P, G, 4])
        ps_n = [kit.ps(f"l1_ps_n{i}", [P, 2, 2, P]) for i in range(4)]
        (staged, sel_done, selt_ps, selt_done, spread_done, chain, e_done, exp_done, scaled_done,
         sums_done, copy_done, head_done, cleared) = (
            kit.sem(f"l1_{n}") for n in
            ("staged", "sel_done", "selt_ps", "selt_done", "spread_done", "chain", "e_done", "exp_done",
             "scaled_done", "sums_done", "copy_done", "head_done", "cleared"))
        landed, landed_before = c.pool_dma, list(c.pool_count)
        win_in = [kit.sem(f"l1_win_in{i}") for i in range(2)]
        block = st.enter_context(nc.Block())

        @block.sync
        def _(sp):
            def emit(k, q):
                if inside(k, 0):
                    b = q % 2
                    starts = [window_start(sp, first, k, g) for g in range(G)]
                    wait_count(sp, spread_done, k - 1)
                    for g in range(G):
                        sp.dma_start(win[:, b, g, :], window_table[bass.ds(starts[g], P), :])\
                          .then_inc(win_in[b], 16)
            staggered(sp, emit, 0)

        @block.gpsimd
        def _(pool):
            pool.memset(c.num[:], 0.0).then_inc(cleared, 1)

            def emit(k, q):
                if inside(k, 0):
                    wait_count(pool, sums_done, k - RING + 1)
                    gather_rows(pool, c, k, q, slots, table, index, rows, staged, landed)
            staggered(pool, emit, 0)

        @block.tensor
        def _(pe):
            def emit(k, q):
                b = q % 2
                if inside(k, 0):
                    pe.wait_ge(sel_done, k + 1)
                    wait_count(pe, selt_done, k)
                    for g in range(G):
                        mm = pe.transpose(ps_t[:, g], sel[:, b, g], c.ident[:])
                    mm.then_inc(selt_ps, 1)
                if inside(k, 1):
                    o, p = (q - 1) % 2, (q - 1) % RING
                    pe.wait_ge(scaled_done, k)
                    wait_count(pe, copy_done, (k - 2) * G)
                    wait_count(pe, head_done, (k - 2) * G)
                    for g in range(G):
                        out = ps_n[2 * o + g // 2][:, g % 2]
                        pe.matmul(out[:, 0], rows[:, p, g, 0:D], scaled[:, o, g], start=True, stop=True)
                        mm = pe.matmul(out[:, 1], c.ones[:], scaled[:, o, g], start=True, stop=True)
                    mm.then_inc(sums_done, 1)
                if inside(k, 0):
                    pe.wait_ge(selt_done, k + 1)
                    pe.wait_ge(win_in[b], turn2(k) * (16 * G) + 16 * G)
                    wait_count(pe, e_done, k)
                    for g in range(G):
                        mm = pe.matmul(ps_x[:, g], sel_t[:, b, g], win[:, b, g], start=True, stop=True)
                    mm.then_inc(spread_done, 1)
            staggered(pe, emit, 1)

        @block.scalar
        def _(act):
            def emit(k, q):
                b = q % 2
                if inside(k, 0):
                    act.wait_ge(selt_ps, k + 1)
                    wait_count(act, spread_done, k - 1)
                    act.activation(sel_t[:, b], ps_t, ACT.Copy).then_inc(selt_done, 1)
                if inside(k, 1):
                    o = (q - 1) % 2
                    for g in range(G):
                        n0 = window_start(act, first, k - 1, g)
                        if g == 0:
                            act.wait_ge(sums_done, k)
                            act.wait_ge(cleared, 1)
                        wait_count(act, copy_done, (k - 1) * G + g)
                        act.activation(c.num[:, :, bass.ds(n0 + 1, P - 1)],
                                       ps_n[2 * o + g // 2][:, g % 2, :, 1:P], ACT.Copy)\
                           .then_inc(copy_done, 1)
                if inside(k, 0):
                    act.wait_ge(e_done, k + 1)
                    wait_count(act, scaled_done, k - 1)
                    act.activation(weight[:, b], e[:, b, 2], ACT.Exp).then_inc(exp_done, 1)
            staggered(act, emit, 1)

        @block.vector
        def _(dve):
            def emit(k, q):
                b = q % 2
                if inside(k, 0):
                    wait_count(dve, selt_done, k - 1)
                    dve.tensor_tensor(sel[:, b], replicate(c.iota_f[:], 1, G),
                                      replicate(slot[:, bass.ds(k * G, G)], 2, P),
                                      ALU.is_equal).then_inc(sel_done, 1)
                    dve.tensor_tensor(real[:, b], replicate(c.iota_f[:], 1, G),
                                      replicate(real_slot[:, bass.ds(k * G, G)], 2, P),
                                      ALU.is_equal).then_inc(chain, 1)
                if inside(k, 1):
                    o = (q - 1) % 2
                    dve.wait_ge(exp_done, k)
                    wait_count(dve, sums_done, k - 2)
                    dve.tensor_tensor(scaled[:, o], real[:, o], replicate(weight[:, o], 2, P), ALU.mult)\
                       .then_inc(scaled_done, 1)
                if inside(k, 0):
                    dve.wait_ge(spread_done, k + 1)
                    dve.wait_ge(landed[q], landed_before[q] + turn4(k) * (16 * G) + 16 * G)
                    wait_count(dve, exp_done, k - 1)
                    dve.tensor_tensor(e[:, b, 0], ps_x[:, :, 0], rows[:, q, :, D], ALU.add).then_inc(chain, 1)
                    dve.wait_ge(chain, k * 3 + 2)
                    dve.scalar_tensor_tensor(e[:, b, 1], e[:, b, 0], LEAK, e[:, b, 0], ALU.mult, ALU.max)\
                       .then_inc(chain, 1)
                    dve.wait_ge(chain, k * 3 + 3)
                    dve.tensor_scalar(e[:, b, 2], e[:, b, 1], -2.0, 2.0, ALU.max, ALU.min).then_inc(e_done, 1)
                if inside(k, 1):
                    o = (q - 1) % 2
                    for g in range(G):
                        n0 = window_start(dve, first, k - 1, g)
                        if g == 0:
                            dve.wait_ge(copy_done, k * G)
                        wait_count(dve, head_done, (k - 1) * G + g)
                        if isinstance(k, int) and k == 1 and g == 0:
                            dve.wait_ge(cleared, 1)
                        at = c.num[:, :, bass.ds(n0, 1)]
                        dve.tensor_tensor(at, at, ps_n[2 * o + g // 2][:, g % 2, :, 0:1], ALU.add)\
                           .then_inc(head_done, 1)
            staggered(dve, emit, 1)
        c.pool_count = [n + 16 * T // RING for n in landed_before]


def sum_pass(nc, c, name, table, real_slot, first, index, acc, counts):
    with ExitStack() as st:
        kit = Kit(nc, st)
        parts = 2 if counts else 1
        slots = kit.sb(f"{name}_slots", [P, RING, G], I32)
        rows = kit.sb(f"{name}_rows", [P, RING, G, D])
        sel = kit.sb(f"{name}_sel", [P, RING, G, P])
        ps_n = [kit.ps(f"{name}_ps_n{i}", [P, 2, 2, P]) for i in range(4)]
        staged, sel_done, sums_done, copy_done, head_done, cleared = (
            kit.sem(f"{name}_{n}") for n in
            ("staged", "sel_done", "sums_done", "copy_done", "head_done", "cleared"))
        landed, landed_before = c.pool_dma, list(c.pool_count)
        block = st.enter_context(nc.Block())

        @block.gpsimd
        def _(pool):
            pool.memset(acc[:, 0:parts], 0.0).then_inc(cleared, 1)

            def emit(k, q):
                if inside(k, 0):
                    wait_count(pool, sums_done, k - RING + 1)
                    gather_rows(pool, c, k, q, slots, table, index, rows, staged, landed)
            staggered(pool, emit, 0)

        @block.tensor
        def _(pe):
            def emit(k, q):
                b = q % 2
                if inside(k, 0):
                    pe.wait_ge(sel_done, k + 1)
                    pe.wait_ge(landed[q], landed_before[q] + turn4(k) * (16 * G) + 16 * G)
                    wait_count(pe, copy_done, (k - 1) * G)
                    wait_count(pe, head_done, (k - 1) * G)
                    for g in range(G):
                        out = ps_n[2 * b + g // 2][:, g % 2]
                        mm = pe.matmul(out[:, 0], rows[:, q, g], sel[:, q, g], start=True, stop=True)
                        if counts:
                            mm = pe.matmul(out[:, 1], c.ones[:], sel[:, q, g], start=True, stop=True)
                    mm.then_inc(sums_done, 1)
            staggered(pe, emit, 0)

        @block.scalar
        def _(act):
            def emit(k, q):
                b = q % 2
                if inside(k, 0):
                    for g in range(G):
                        n0 = window_start(act, first, k, g)
                        if g == 0:
                            act.wait_ge(sums_done, k + 1)
                            act.wait_ge(cleared, 1)
                        wait_count(act, copy_done, k * G + g)
                        act.activation(acc[:, 0:parts, bass.ds(n0 + 1, P - 1)],
                                       ps_n[2 * b + g // 2][:, g % 2, 0:parts, 1:P], ACT.Copy)\
                           .then_inc(copy_done, 1)
            staggered(act, emit, 0)

        @block.vector
        def _(dve):
            def emit(k, q):
                if inside(k, 0):
                    wait_count(dve, sums_done, k - RING + 1)
                    dve.tensor_tensor(sel[:, q], replicate(c.iota_f[:], 1, G),
                                      replicate(real_slot[:, bass.ds(k * G, G)], 2, P),
                                      ALU.is_equal).then_inc(sel_done, 1)
                if inside(k, 1):
                    o = (q - 1) % 2
                    for g in range(G):
                        n0 = window_start(dve, first, k - 1, g)
                        if g == 0:
                            dve.wait_ge(copy_done, k * G)
                        wait_count(dve, head_done, (k - 1) * G + g)
                        if isinstance(k, int) and k == 1 and g == 0:
                            dve.wait_ge(cleared, 1)
                        at = acc[:, 0:parts, bass.ds(n0, 1)]
                        dve.tensor_tensor(at, at, ps_n[2 * o + g // 2][:, g % 2, 0:parts, 0:1], ALU.add)\
                           .then_inc(head_done, 1)
            staggered(dve, emit, 1)
        c.pool_count = [n + 16 * T // RING for n in landed_before]


def load_weights(nc, c, w):
    with ExitStack() as st:
        kit = Kit(nc, st)
        att_cols = kit.sb("att_cols", [P, 2])
        kernel_t = kit.sb("kernel_t", [P, P])
        zero_rows = kit.sb("zero_rows", [P, D])
        ps_t, ps_a = kit.ps("w_ps_t", [P, P]), kit.ps("w_ps_a", [P, 2])
        cleared, loaded, turned, copied = (kit.sem(n) for n in ("w_cleared", "w_loaded", "w_turned", "w_copied"))
        block = st.enter_context(nc.Block())
        row = lambda a: a.rearrange("(a n) -> a n", a=1)
        col = lambda a: a.rearrange("(p a) -> p a", a=1)
        loads = [(c.w0[:, 0:D], w["L0_gnn_W_l"]), (c.w0[:, D:2 * D], w["L0_gnn_W_r"]),
                 (c.b0[:, 0:D], row(w["L0_gnn_b_l"])), (c.b0[:, D:2 * D], row(w["L0_gnn_b_r"])),
                 (c.w1[:, 0:D], w["L1_gnn_kernel"]),
                 (c.w2[:, 0:D], w["L2_gnn_key_kernel"]), (c.w2[:, D:2 * D], w["L2_gnn_kernel"]),
                 (c.w2[:, 2 * D:], w["L2_gnn_query_kernel"]),
                 (c.b2[:, 0:D], row(w["L2_gnn_key_bias"])), (c.b2[:, 2 * D:], row(w["L2_gnn_query_bias"])),
                 (c.bias0[:], col(w["L0_gnn_bias"])), (c.gamma[:], col(w["L0_gnn_gamma"])),
                 (c.beta[:], col(w["L0_gnn_beta"])), (c.bias2[:], col(w["L2_gnn_bias"])),
                 (c.att[:], row(w["L0_gnn_att"].rearrange("h c -> (h c)")).to_broadcast([P, D])),
                 (att_cols[:, 0:1], w["L1_gnn_kernel_attention"][D:2 * D, :]),
                 (att_cols[:, 1:2], w["L1_gnn_kernel_attention"][0:D, :])]
        for l in range(2):
            loads += [(c.wn[:, l], w["L3_gnn_Wn"][l]), (c.wl[:, l], w["L3_gnn_Wl"][l]),
                      (c.wa[:, l], w["L3_gnn_Wa"][l])]
        pads = [(c.win0, D), (c.win1, 4), (c.win2, D)]

        @block.gpsimd
        def _(pool):
            pool.memset(c.w1[:], 0.0).then_inc(cleared, 1)
            pool.memset(c.b2[:], 0.0).then_inc(cleared, 1)
            pool.memset(zero_rows[:], 0.0).then_inc(cleared, 1)

        @block.sync
        def _(sp):
            sp.wait_ge(cleared, 3)
            for to, of in loads:
                sp.dma_start(to, of).then_inc(loaded, 16)
            for table, width in pads:
                sp.dma_start(table[NP:NW, :], zero_rows[:, 0:width]).then_inc(loaded, 16)
            sp.wait_ge(loaded, 16 * (len(loads) + len(pads)))

        @block.tensor
        def _(pe):
            pe.wait_ge(loaded, 16 * (len(loads) + len(pads)))
            pe.transpose(ps_t, c.w1[:, 0:D], c.ident[:]).then_inc(turned, 1)
            pe.wait_ge(copied, 1)
            pe.matmul(ps_a, kernel_t[:], att_cols[:], start=True, stop=True).then_inc(turned, 1)

        @block.vector
        def _(dve):
            dve.wait_ge(turned, 1)
            dve.tensor_copy(kernel_t[:], ps_t).then_inc(copied, 1)
            dve.wait_ge(turned, 2)
            dve.tensor_copy(c.w1[:, D:D + 1], ps_a[:, 0:1]).then_inc(copied, 1)
            dve.tensor_copy(c.w1[:, D + 4:D + 5], ps_a[:, 1:2]).then_inc(copied, 1)


STAGES = {
    "load": ["turn", "take0", "take1"],
    "gat": ["den", "recip", "ratio", "bias", "a_mean", "a_center", "a_square", "a_var", "a_std", "a_rstd",
            "a_norm", "affine", "negative", "exp", "elu", "residual"],
    "edge": ["den", "recip", "ratio", "residual"],
    "dot": ["recip", "ratio", "residual"],
    "rel0": ["degree", "root", "inverse", "has_in", "products", "sum", "scaled", "self_l", "add_l", "no_in",
             "self_a", "add_a", "rrelu"],
}
LN_STEPS = ["b_mean", "b_center", "b_square", "b_var", "b_std", "b_rstd", "b_norm"]
STAGES["rel1"] = STAGES["rel0"] + ["residual"]


def node_step(nc, c, stage, weight, bias, relu, outputs, layer=0, x_dram=None, keep_in=None):
    steps = STAGES[stage] + (LN_STEPS if stage in ("gat", "edge", "dot", "rel1") else []) + ["keep"]
    order = {s: i for i, s in enumerate(steps)}
    per_j = len(steps)
    width = weight.shape[-1]
    with ExitStack() as st:
        kit = Kit(nc, st)
        name = f"n_{stage}"
        a, b, d, s = (kit.sb(f"{name}_{x}", [P, CW]) for x in "abds")
        m = kit.sb(f"{name}_m", [P, CW]) if stage[:3] == "rel" else None
        x_rows = kit.sb(f"{name}_x_rows", [P, CB, D]) if stage == "load" else None
        tab = kit.sb(f"{name}_tab", [P, CB, width])
        pa, pb, pc = (kit.ps(f"{name}_p{x}", [P, 2, 512]) for x in "abc")
        pt = [kit.ps(f"{name}_pt{i}", [P, 512]) for i in range(2)]
        step_done, tab_mm, tab_cp, x_in, x_zero = (kit.sem(f"{name}_{x}") for x in
                                                   ("step_done", "tab_mm", "tab_cp", "x_in", "x_zero"))
        stored = kit.sem(f"{name}_stored")
        block = st.enter_context(nc.Block())
        whole = lambda t: t[:, 0:2 * HW] if len(t.shape) == 2 else t
        halves = lambda t: t[:, 0:CW].rearrange("p (h w) -> p h w", h=2)
        banks = lambda t: t[:, :, 0:HW]

        def here(eng, step, j):
            if step not in order:
                return False
            wait_count(eng, step_done, j * per_j + order[step])
            return True

        def last(j):
            return isinstance(j, int) and j == CS - 1

        def run(eng, body):
            body(0)
            with eng.Fori(1, CS - 1) as j:
                body(j)
            body(CS - 1)

        @block.sync
        def _(sp):
            def body(j):
                if stage == "load":
                    wait_count(sp, step_done, j * per_j)
                    if last(j):
                        full, rest = divmod(N - (CS - 1) * CW, P)
                        sp.wait_ge(x_zero, 1)
                        sp.dma_start(x_rows[:, 0:full], x_dram[j * CW:j * CW + full * P, :]
                                     .rearrange("(i p) d -> p i d", p=P)).then_inc(x_in, 16)
                        sp.dma_start(x_rows[0:rest, full], x_dram[N - rest:N, :]).then_inc(x_in, 16)
                    else:
                        sp.dma_start(x_rows[:], x_dram[bass.ds(j * CW, CW), :]
                                     .rearrange("(i p) d -> p i d", p=P)).then_inc(x_in, 16)
                sp.wait_ge(tab_cp, j * CB + CB)
                for table, c0, c1 in outputs:
                    if last(j) and table.shape[0] == N:
                        full, rest = divmod(N - (CS - 1) * CW, P)
                        sp.dma_start(table[j * CW:j * CW + full * P, :].rearrange("(i p) d -> p i d", p=P),
                                     tab[:, 0:full, c0:c1]).then_inc(stored, 16)
                        sp.dma_start(table[N - rest:N, :], tab[0:rest, full, c0:c1]).then_inc(stored, 16)
                        n_stores = 16 * (CS + 1)
                    else:
                        sp.dma_start(table[bass.ds(j * CW, CW), :].rearrange("(i p) d -> p i d", p=P),
                                     tab[:, :, c0:c1]).then_inc(stored, 16)
                        n_stores = 16 * len(outputs) * CS
                if last(j):
                    sp.wait_ge(stored, n_stores)
            run(sp, body)

        @block.tensor
        def _(pe):
            def mean(out, of):
                for h in range(2):
                    mm = pe.matmul(out[:, h, 0:HW], c.mean_w[:], of[:, h * HW:(h + 1) * HW],
                                   start=True, stop=True)
                mm.then_inc(step_done, 1)

            def body(j):
                if here(pe, "turn", j):
                    pe.wait_ge(x_in, j * 16 + (32 if last(j) else 16))
                    for i in range(CB):
                        mm = pe.transpose(pa[:, i // 4, (i % 4) * P:(i % 4 + 1) * P], x_rows[:, i], c.ident[:])
                    mm.then_inc(step_done, 1)
                if here(pe, "products", j):
                    feats = c.x if stage == "rel0" else c.hidden
                    for out, w, of in ((pa, c.wn, c.rel[:, 0]), (pb, c.wl, feats), (pc, c.wa, feats)):
                        for h in range(2):
                            mm = pe.matmul(out[:, h, 0:HW], w[:, layer], of[:, bass.ds(j * CW + h * HW, HW)],
                                           start=True, stop=True)
                    mm.then_inc(step_done, 1)
                for t in "ab":
                    if here(pe, f"{t}_mean", j):
                        mean(pa, a)
                    if here(pe, f"{t}_var", j):
                        mean(pb, s)
                wait_count(pe, step_done, j * per_j + order["keep"])
                for i in range(CB):
                    wait_count(pe, tab_cp, j * CB + max(i - 1, 0))
                    out = pt[i % 2][:, 0:width]
                    if bias is not None:
                        pe.matmul(out, c.one_row[:], bias[:], start=True, stop=False)
                    pe.matmul(out, a[:, i * P:(i + 1) * P], weight, start=bias is None, stop=True)\
                      .then_inc(tab_mm, 1)
            def body_runtime(j):
                body(j)
            run(pe, body_runtime)

        @block.scalar
        def _(act):
            def body(j):
                if here(act, "root", j):
                    act.activation(b[:], b[:], ACT.Sqrt).then_inc(step_done, 1)
                for t in "ab":
                    if here(act, f"{t}_square", j):
                        act.activation(s[:], d[:], ACT.Square).then_inc(step_done, 1)
                    if here(act, f"{t}_std", j):
                        act.activation(halves(s), banks(pb), ACT.Sqrt, bias=c.eps[:]).then_inc(step_done, 1)
                    if t == "a" and here(act, "exp", j):
                        act.activation(b[:], b[:], ACT.Exp).then_inc(step_done, 1)
                wait_count(act, stored, j * (16 * len(outputs)))
                for i in range(CB):
                    act.wait_ge(tab_mm, j * CB + i + 1)
                    at = 0
                    for c0, c1 in [*relu, (width, width)]:
                        if c0 > at:
                            ins = act.activation(tab[:, i, at:c0], pt[i % 2][:, at:c0], ACT.Copy)
                        if c1 > c0:
                            ins = act.activation(tab[:, i, c0:c1], pt[i % 2][:, c0:c1], ACT.Relu)
                        at = c1
                    ins.then_inc(tab_cp, 1)
            run(act, body)

        @block.vector
        def _(dve):
            def body(j):
                at = lambda t: t[:, bass.ds(j * CW, CW)]
                if stage == "load":
                    wait_count(dve, tab_mm, j * CB)
                    here(dve, "take0", j)
                    dve.tensor_copy(a[:, 0:512], pa[:, 0]).then_inc(step_done, 1)
                    here(dve, "take1", j)
                    dve.tensor_copy(a[:, 512:CW], pa[:, 1, 0:CW - 512]).then_inc(step_done, 1)
                if here(dve, "den", j):
                    dve.tensor_single_scalar(b[:], at(c.num[:, 1]), 1e-16 if stage == "gat" else 1e-9,
                                             ALU.add).then_inc(step_done, 1)
                if here(dve, "recip", j):
                    dve.reciprocal(b[:], b[:] if stage != "dot" else at(c.num[:, 1])).then_inc(step_done, 1)
                if here(dve, "ratio", j):
                    wait_count(dve, tab_mm, j * CB)
                    dve.tensor_tensor(a[:], at(c.num[:, 0]), b[:], ALU.mult).then_inc(step_done, 1)
                if here(dve, "bias", j):
                    dve.tensor_single_scalar(a[:], a[:], c.bias0[:], ALU.add).then_inc(step_done, 1)
                if here(dve, "degree", j):
                    dve.tensor_single_scalar(b[:], at(c.rel[:, 1]), 1.0, ALU.max).then_inc(step_done, 1)
                if here(dve, "inverse", j):
                    dve.reciprocal(b[:], b[:]).then_inc(step_done, 1)
                if here(dve, "has_in", j):
                    dve.tensor_single_scalar(m[:], at(c.rel[:, 1]), 1.0, ALU.min).then_inc(step_done, 1)
                if here(dve, "sum", j):
                    wait_count(dve, tab_mm, j * CB)
                    dve.tensor_tensor(halves(a), banks(pa), halves(at(c.num[:, 0])), ALU.add)\
                       .then_inc(step_done, 1)
                if here(dve, "scaled", j):
                    dve.tensor_tensor(a[:], a[:], b[:], ALU.mult).then_inc(step_done, 1)
                if here(dve, "self_l", j):
                    dve.tensor_tensor(halves(d), banks(pb), halves(m), ALU.mult).then_inc(step_done, 1)
                if here(dve, "add_l", j):
                    dve.tensor_tensor(a[:], a[:], d[:], ALU.add).then_inc(step_done, 1)
                if here(dve, "no_in", j):
                    dve.tensor_scalar(m[:], m[:], -1.0, 1.0, ALU.mult, ALU.add).then_inc(step_done, 1)
                if here(dve, "self_a", j):
                    dve.tensor_tensor(halves(d), banks(pc), halves(m), ALU.mult).then_inc(step_done, 1)
                if here(dve, "add_a", j):
                    dve.tensor_tensor(a[:], a[:], d[:], ALU.add).then_inc(step_done, 1)
                if here(dve, "rrelu", j):
                    dve.scalar_tensor_tensor(a[:], a[:], RRELU, a[:], ALU.mult, ALU.max).then_inc(step_done, 1)
                for t in "ab":
                    if t == "b" and here(dve, "residual", j):
                        if stage == "gat":
                            dve.scalar_tensor_tensor(a[:], a[:], -1.0, at(c.x), ALU.add, ALU.add)\
                               .then_inc(step_done, 1)
                        elif stage == "dot":
                            dve.scalar_tensor_tensor(a[:], a[:], c.bias2[:], at(c.x), ALU.add, ALU.add)\
                               .then_inc(step_done, 1)
                        else:
                            dve.tensor_tensor(a[:], a[:], at(c.x), ALU.add).then_inc(step_done, 1)
                    if here(dve, f"{t}_center", j):
                        dve.tensor_tensor(halves(d), halves(a), banks(pa), ALU.subtract).then_inc(step_done, 1)
                    if here(dve, f"{t}_rstd", j):
                        dve.reciprocal(s[:], s[:]).then_inc(step_done, 1)
                    if here(dve, f"{t}_norm", j):
                        dve.tensor_tensor(a[:], d[:], s[:], ALU.mult).then_inc(step_done, 1)
                    if t == "a" and here(dve, "affine", j):
                        dve.tensor_scalar(a[:], a[:], c.gamma[:], c.beta[:], ALU.mult, ALU.add)\
                           .then_inc(step_done, 1)
                    if t == "a" and here(dve, "negative", j):
                        dve.tensor_single_scalar(b[:], a[:], 0.0, ALU.min).then_inc(step_done, 1)
                    if t == "a" and here(dve, "elu", j):
                        dve.scalar_tensor_tensor(a[:], a[:], 0.0, b[:], ALU.max, ALU.add).then_inc(step_done, 1)
                here(dve, "keep", j)
                if keep_in is not None:
                    dve.tensor_single_scalar(at(keep_in), a[:], 1.0, ALU.mult).then_inc(step_done, 1)
                else:
                    dve.nop().then_inc(step_done, 1)
            run(dve, body)

        @block.gpsimd
        def _(pool):
            if stage == "load":
                pool.wait_ge(step_done, (CS - 2) * per_j + order["turn"] + 1)
                pool.memset(x_rows[:], 0.0).then_inc(x_zero, 1)


def build(nc, x, src, dst, etype, weights, out):
    class Memory:
        pass

    c = Memory()
    dram = lambda name, shape: nc.dram_tensor(name, shape, F32, kind="Internal").ap()
    sorted_dst, sorted_src = dram("sorted_dst", (POS, 4)), dram("sorted_src", (POS, 4))
    runs_dst, runs_src = dram("runs_dst", (2, POS)), dram("runs_src", (2, POS))
    tab0, tab1, tab2 = dram("tab0", (NP, D)), dram("tab1", (NP, D + 4)), dram("tab2", (NP, 2 * D))
    tab3, tab4 = dram("tab3", (NP, D)), dram("tab4", (NP, D))
    c.win0, c.win1, c.win2 = dram("win0", (NW, D)), dram("win1", (NW, 4)), dram("win2", (NW, D))
    with ExitStack() as st:
        kit = Kit(nc, st)
        c.pool_dma = [kit.sem(f"pool_dma{i}") for i in range(RING)]
        c.pool_count = [0] * RING
        c.ident, c.ones, c.mean_w = kit.sb("ident", [P, P]), kit.sb("ones", [P, P]), kit.sb("mean_w", [P, P])
        c.identb = kit.sb("identb", [P, P], BF16)
        c.before, c.after, c.first_row = (kit.sb(n, [P, P]) for n in ("before", "after", "first_row"))
        c.hsel4, c.hsel8 = kit.sb("hsel4", [4, P]), kit.sb("hsel8", [8, P])
        c.fence = kit.sb("fence", [1, 1])
        c.one_row, c.eps = kit.sb("one_row", [1, P]), kit.sb("eps", [P, 1])
        c.iota_f, c.iota_b, c.node_id = kit.sb("iota_f", [P, P]), kit.sb("iota_b", [P, P], BF16), kit.sb("node_id", [P, NT])
        c.w0, c.b0 = kit.sb("w0", [P, 2 * D]), kit.sb("b0", [1, 2 * D])
        c.w1 = kit.sb("w1", [P, D + 8])
        c.w2, c.b2 = kit.sb("w2", [P, 3 * D]), kit.sb("b2", [1, 3 * D])
        c.wn, c.wl, c.wa = (kit.sb(n, [P, 2, D]) for n in ("wn", "wl", "wa"))
        c.bias0, c.gamma, c.beta, c.bias2 = (kit.sb(n, [P, 1]) for n in ("bias0", "gamma", "beta", "bias2"))
        c.att = kit.sb("att", [P, D])
        lists = {}
        for n in ("dst", "src"):
            lists[n] = (kit.sb(f"slot_{n}", [P, T]), kit.sb(f"real_slot_{n}", [P, T]),
                        kit.sb(f"first_{n}", [1, T], I32), kit.sb(f"neighbour_{n}", [P, T], I32))
        etype_at = kit.sb("etype_at", [P, T], I32)
        constants(nc, c)
        load_weights(nc, c, weights)
        with ExitStack() as sort_scope:
            edge_kit = Kit(nc, sort_scope)
            c.edge = edge_kit.sb("edge", [ET, 3, UT])
            c.low, c.high = edge_kit.sb("low", [ET, 2, UT]), edge_kit.sb("high", [ET, 2, UT])
            edge_columns(nc, c, src, dst, etype)
            counting_sort(nc, c, 1, dst, sorted_dst)
            counting_sort(nc, c, 0, src, sorted_src)
        for n, rows, runs in (("dst", sorted_dst, runs_dst), ("src", sorted_src, runs_src)):
            slot, real_slot, first, neighbour = lists[n]
            read_sorted(nc, c, n, rows, runs, slot, real_slot, first, neighbour,
                        etype_at if n == "dst" else None)
        x_at = kit.sb("x_at", [P, NP])
        num = kit.sb("num", [P, 2, NW])
        c.x, c.num = x_at[:], num[:]
        slot_d, real_d, first_d, nb_d = lists["dst"]
        slot_s, real_s, first_s, nb_s = lists["src"]
        node_step(nc, c, "load", c.w0[:], c.b0, [], [(tab0, 0, D), (c.win0, D, 2 * D)], x_dram=x, keep_in=c.x)
        attention_pass(nc, c, "l0", 4, False, tab0, c.win0, runs_dst, slot_d, first_d, nb_d)
        node_step(nc, c, "gat", c.w1[:], None, [], [(tab1, 0, D + 4), (c.win1, D + 4, D + 8)], keep_in=c.x)
        edge_score_pass(nc, c, tab1, c.win1, slot_s, real_s, first_s, nb_s)
        node_step(nc, c, "edge", c.w2[:], c.b2, [(0, D), (2 * D, 3 * D)], [(tab2, 0, 2 * D), (c.win2, 2 * D, 3 * D)],
                  keep_in=c.x)
        attention_pass(nc, c, "l2", 8, True, tab2, c.win2, runs_src, slot_s, first_s, nb_s)
        node_step(nc, c, "dot", c.wn[:, 0], None, [], [(tab3, 0, D)], keep_in=c.x)
        rel = kit.sb("rel", [P, 2, NW])
        c.rel, c.hidden = rel[:], c.num[:, 1]
        sum_pass(nc, c, "rel", weights["L3_gnn_rel_emb"], real_d, first_d, etype_at, c.rel, True)
        sum_pass(nc, c, "l3a", tab3, real_d, first_d, nb_d, c.num, False)
        node_step(nc, c, "rel0", c.wn[:, 1], None, [], [(tab4, 0, D)], layer=0, keep_in=c.hidden)
        sum_pass(nc, c, "l3b", tab4, real_d, first_d, nb_d, c.num, False)
        node_step(nc, c, "rel1", c.ident[:], None, [], [(out, 0, D)], layer=1)


_INS = ["x", "src", "dst", "edge_type_200", "L0_gnn_W_l", "L0_gnn_b_l", "L0_gnn_W_r", "L0_gnn_b_r", "L0_gnn_att",
        "L0_gnn_bias", "L0_gnn_gamma", "L0_gnn_beta", "L1_gnn_kernel", "L1_gnn_kernel_attention",
        "L2_gnn_query_kernel", "L2_gnn_query_bias", "L2_gnn_key_kernel", "L2_gnn_key_bias", "L2_gnn_kernel",
        "L2_gnn_bias", "L3_gnn_rel_emb", "L3_gnn_Wn", "L3_gnn_Wl", "L3_gnn_Wa"]


def kernel(**inputs):
    import concourse.bacc as _bacc
    from concourse.bass_utils import run_bass_kernel_spmd as _run

    nc = _bacc.Bacc("TRN2", target_bir_lowering=False, num_devices=1)
    arrays, aps = {}, {}
    for name in _INS:
        a = np.ascontiguousarray(inputs[name])
        arrays[f"in_{name}_dram"] = a
        aps[name] = nc.dram_tensor(f"in_{name}_dram", a.shape, mybir.dt.from_np(a.dtype), kind="ExternalInput").ap()
    out = nc.dram_tensor("out_0_dram", (N, D), F32, kind="ExternalOutput").ap()
    build(nc, aps["x"], aps["src"], aps["dst"], aps["edge_type_200"], aps, out)
    r = _run(nc, [arrays], core_ids=[0])
    return r.results[0]["out_0_dram"]
```

```python
from contextlib import ExitStack

import numpy as np
import concourse.bass as bass
from concourse import mybir

F32 = mybir.dt.float32
BF16 = mybir.dt.bfloat16
I32 = mybir.dt.int32
ALU = mybir.AluOpType
ACT = mybir.ActivationFunctionType
AX = mybir.AxisListType

P = 128
N, E, D = 6250, 100000, 128
NT = -(-N // P)
NP = NT * P
NW = NP + P
ET = 125
UT = E // ET
UG = 8
US = UT // UG
G = 4
RING = 6
T = -(-(E + NP) // (P * G * RING)) * G * RING
GROUPS = T // G
POS = T * P
PADS = POS - E - NP
TB = T // 8
NBLK = T // TB
PR = 12
BIG = 1e30
LEAK = 0.2
RRELU = (1.0 / 8.0 + 1.0 / 3.0) / 2.0
LN_EPS = 1e-5
RELS = 200
CB = 7
CW = CB * P
CS = NP // CW
HW = CW // 2


def replicate(ap, dim, count):
    a = ap.unsqueeze(dim)
    shape = list(a.shape)
    shape[dim] = count
    return a.to_broadcast(shape)


class Kit:

    def __init__(self, nc, stack):
        self.nc, self.stack, self.sems = nc, stack, 0

    def sb(self, name, shape, dt=F32):
        return self.stack.enter_context(self.nc.sbuf_tensor(name, shape, dt))

    def ps(self, name, shape, dt=F32):
        size = int(np.prod(shape[1:]))
        bank = 512 if dt == F32 else 1024
        t = self.stack.enter_context(self.nc.psum_tensor(name, [shape[0], -(-size // bank) * bank], dt))
        letters = "abcd"[:len(shape) - 1]
        sizes = {x: n for x, n in zip(letters[1:], shape[2:])}
        return t[:, 0:size].rearrange(f"p ({' '.join(letters)}) -> p {' '.join(letters)}", **sizes)

    def sem(self, name):
        if not self.sems:
            self.stack.callback(self.nc.all_engine_barrier)
        self.sems += 1
        sem = self.stack.enter_context(self.nc.semaphore(name))
        self.stack.callback(self.nc.sync.sem_clear, sem)
        return sem


def staggered(eng, emit, lag):
    for k in range(RING):
        emit(k, k % RING)
    with eng.Fori(1, GROUPS // RING) as m:
        for q in range(RING):
            emit(m * RING + q, q)
    for k in range(GROUPS, GROUPS + lag):
        emit(k, k % RING)


def in_pairs(eng, body):
    body(0)
    with eng.Fori(1, US // 2) as m:
        body(m)


def inside(k, lag):
    return not isinstance(k, int) or 0 <= k - lag < GROUPS


def wait_count(eng, sem, value):
    if not isinstance(value, int) or value > 0:
        eng.wait_ge(sem, value)


def turn(k, lag=0):
    return (k - lag) // RING


def turn2(k, lag=0):
    return (k - lag) // 2


def constants(nc, c):
    with ExitStack() as st:
        kit = Kit(nc, st)
        cst_done, cst_int, cst_cast = kit.sem("cst_done"), kit.sem("cst_int"), kit.sem("cst_cast")
        io = kit.sb("iota_int", [P, P], I32)
        nodes = kit.sb("nodes_int", [P, NT], I32)
        block = st.enter_context(nc.Block())

        @block.gpsimd
        def _(pool):
            n = 0
            for t, v in ((c.ident, 0.0), (c.identb, 0.0), (c.ones, 1.0), (c.mean_w, 1.0 / D),
                         (c.before, 1.0), (c.after, 1.0), (c.first_row, 0.0), (c.hsel4, 1.0), (c.hsel8, 1.0),
                         (c.one_row, 1.0), (c.eps, LN_EPS)):
                pool.memset(t[:], v).then_inc(cst_done, 1)
                n += 1
            pool.iota(io[:], pattern=[[1, P]], base=0, channel_multiplier=0).then_inc(cst_int, 1)
            pool.iota(nodes[:], pattern=[[P, NT]], base=0, channel_multiplier=1).then_inc(cst_int, 1)
            pool.wait_ge(cst_done, n)
            for t in (c.ident, c.identb):
                pool.affine_select(out=t[:], in_=t[:], compare_op=ALU.not_equal, fill=1.0, base=0,
                                   pattern=[[-1, P]], channel_multiplier=1).then_inc(cst_done, 1)
            pool.affine_select(out=c.before[:], in_=c.before[:], compare_op=ALU.is_gt, fill=0.0, base=0,
                               pattern=[[1, P]], channel_multiplier=-1).then_inc(cst_done, 1)
            pool.affine_select(out=c.after[:], in_=c.after[:], compare_op=ALU.is_gt, fill=0.0, base=0,
                               pattern=[[-1, P]], channel_multiplier=1).then_inc(cst_done, 1)
            pool.affine_select(out=c.first_row[:], in_=c.first_row[:], compare_op=ALU.not_equal, fill=1.0,
                               base=0, pattern=[[0, P]], channel_multiplier=1).then_inc(cst_done, 1)
            for t, heads in ((c.hsel4, 4), (c.hsel8, 8)):
                w = D // heads
                pool.affine_select(out=t[:], in_=t[:], compare_op=ALU.is_ge, fill=0.0, base=0,
                                   pattern=[[1, P]], channel_multiplier=-w).then_inc(cst_done, 1)
                n += 1
                pool.wait_ge(cst_done, n + 5)
                pool.affine_select(out=t[:], in_=t[:], compare_op=ALU.is_ge, fill=0.0, base=w - 1,
                                   pattern=[[-1, P]], channel_multiplier=w).then_inc(cst_done, 1)
                n += 1

        @block.vector
        def _(dve):
            dve.wait_ge(cst_int, 2)
            dve.tensor_copy(c.iota_f[:], io[:]).then_inc(cst_cast, 1)
            dve.tensor_copy(c.iota_b[:], io[:]).then_inc(cst_cast, 1)
            dve.tensor_copy(c.node_id[:], nodes[:]).then_inc(cst_cast, 1)


def edge_columns(nc, c, src, dst, etype):
    with ExitStack() as st:
        kit = Kit(nc, st)
        rows = kit.sb("edge_rows", [100, 3, UG, ET], I32)
        rows_f = kit.sb("edge_rows_f", [100, 3, UG, ET])
        cols_i = kit.sb("edge_cols_i", [ET, 2, UT], I32)
        part_i = kit.sb("edge_part_i", [ET, 2, UT], I32)
        ps = [kit.ps(f"edge_ps{i}", [ET, UG // 2, P]) for i in range(6)]
        loaded, floated, turned, copied = (kit.sem(n) for n in
                                           ("edges_loaded", "edges_floated", "edges_turned", "edges_copied"))
        block = st.enter_context(nc.Block())

        @block.sync
        def _(sp):
            for f, a in enumerate((src, dst, etype)):
                sp.dma_start(rows[:, f], a.rearrange("(b t j) -> t b j", b=UG, j=ET)).then_inc(loaded, 16)

        @block.tensor
        def _(pe):
            pe.wait_ge(floated, 1)
            for f in range(3):
                for b in range(UG):
                    mm = pe.transpose(ps[2 * f + b // 4][:, b % 4, 0:100], rows_f[:, f, b, :],
                                      c.ident[0:100, 0:100])
            mm.then_inc(turned, 1)

        @block.vector
        def _(dve):
            dve.wait_ge(loaded, 48)
            dve.tensor_copy(rows_f[:], rows[:]).then_inc(floated, 1)
            dve.wait_ge(turned, 1)
            for f in range(3):
                for h in range(2):
                    cols = c.edge[:, f, 400 * h:400 * h + 400].rearrange("p (b t) -> p b t", b=4)
                    dve.tensor_copy(cols, ps[2 * f + h][:, :, 0:100]).then_inc(copied, 1)
            dve.wait_ge(copied, 6)
            dve.tensor_copy(cols_i[:], c.edge[:, 0:2, :]).then_inc(copied, 1)
            dve.wait_ge(copied, 7)
            dve.tensor_single_scalar(part_i[:], cols_i[:], 7, ALU.arith_shift_right).then_inc(copied, 1)
            dve.wait_ge(copied, 8)
            dve.tensor_copy(c.high[:], part_i[:]).then_inc(copied, 1)
            dve.wait_ge(copied, 9)
            dve.tensor_single_scalar(part_i[:], cols_i[:], P - 1, ALU.bitwise_and).then_inc(copied, 1)
            dve.wait_ge(copied, 10)
            dve.tensor_copy(c.low[:], part_i[:]).then_inc(copied, 1)


def counting_sort(nc, c, key, key_dram, sorted_rows):
    name = ("src", "dst")[key]
    with ExitStack() as st:
        kit = Kit(nc, st)
        lo = kit.sb(f"{name}_lo", [ET, 2, UG, P], BF16)
        hi = kit.sb(f"{name}_hi", [ET, 2, UG, NT], BF16)
        zero_lo = kit.sb(f"{name}_zero_lo", [ET, P], BF16)
        lo_t = kit.sb(f"{name}_lo_t", [P, 2, UG, ET])
        key_row = kit.sb(f"{name}_key_row", [ET, 2, UG, ET], I32)
        table = kit.sb(f"{name}_table", [P, UG + 1, NT])
        count = kit.sb(f"{name}_count", [P, NT])
        ahead = kit.sb(f"{name}_ahead", [P, NT])
        total = kit.sb(f"{name}_total", [P, NT])
        begin = kit.sb(f"{name}_begin", [P, NT])
        begin_i = kit.sb(f"{name}_begin_i", [P, NT], I32)
        self_row = kit.sb(f"{name}_self_row", [P, NT, 4])
        pad_row = kit.sb(f"{name}_pad_row", [PADS // PR, PR, 4])
        payload = kit.sb(f"{name}_payload", [ET, UT, 4])
        staged = kit.sb(f"{name}_staged", [ET, 2, UG, 4])
        same = kit.sb(f"{name}_same", [ET, UG, ET])
        same2 = kit.sb(f"{name}_same2", [ET, UG, ET])
        picked = kit.sb(f"{name}_picked", [ET, UG, NT])
        rank = kit.sb(f"{name}_rank", [ET, UG])
        base = kit.sb(f"{name}_base", [ET, UG])
        position = kit.sb(f"{name}_position", [ET, 2, UG], I32)
        zero_nt = kit.sb(f"{name}_zero_nt", [P, NT])
        ps_count = kit.ps(f"{name}_ps_count", [P, 512])
        ps_pre = kit.ps(f"{name}_ps_pre", [P, 2, NT])
        ps_hist = [kit.ps(f"{name}_ps_hist{i}", [P, UG, NT]) for i in range(2)]
        ps_lo_t = [kit.ps(f"{name}_ps_lo_t{i}", [P, UG, P], BF16) for i in range(2)]
        ps_base = kit.ps(f"{name}_ps_base", [ET, UG, NT])
        prep, zeroed, onehot, counted, off, prefixed, begun = (kit.sem(f"{name}_{n}") for n in
                                                 ("prep", "zeroed", "onehot", "counted", "off", "prefixed", "begun"))
        onehot2, hist_done, turned, turn_copied, table_done, base_done = (
            kit.sem(f"{name}_{n}") for n in
            ("onehot2", "hist_done", "turned", "turn_copied", "table_done", "base_done"))
        chain, pos_done, pay_done = (kit.sem(f"{name}_{n}") for n in ("chain", "pos_done", "pay_done"))
        fenced = kit.sem(f"{name}_fenced")
        row_in = [kit.sem(f"{name}_row_in{i}") for i in range(2)]
        *sent, self_sent = c.pool_dma[0:3]
        before = list(c.pool_count)
        keys_by_step = key_dram.rearrange("(s n) -> s n", s=US)
        block = st.enter_context(nc.Block())

        def one_hots(dve, s, b, sem):
            low = c.low[:, key, bass.ds(s * UG, UG)]
            high = c.high[:, key, bass.ds(s * UG, UG)]
            dve.tensor_tensor(lo[:, b], replicate(low, 2, P), replicate(c.iota_b[0:ET, :], 1, UG),
                              ALU.is_equal).then_inc(sem, 1)
            dve.tensor_tensor(hi[:, b], replicate(high, 2, NT), replicate(c.iota_b[0:ET, 0:NT], 1, UG),
                              ALU.is_equal).then_inc(sem, 1)

        @block.vector
        def _(dve):
            dve.memset(zero_lo[:], 0.0).then_inc(zeroed, 1)
            def two_steps(m):
                for b in range(2):
                    wait_count(dve, counted, m * 2 + b)
                    one_hots(dve, m * 2 + b, b, onehot)
            in_pairs(dve, two_steps)
            dve.wait_ge(counted, US + 1)
            dve.tensor_single_scalar(count[:], ps_count[:, 0:NT], 1.0, ALU.add).then_inc(off, 1)
            dve.wait_ge(prefixed, 1)
            dve.tensor_copy(ahead[:], ps_pre[:, 0]).then_inc(chain, 1)
            dve.tensor_copy(total[:], ps_pre[:, 1]).then_inc(chain, 1)
            dve.memset(zero_nt[:], 0.0).then_inc(chain, 1)
            dve.wait_ge(chain, 3)
            dve.tensor_tensor_scan(begin[:], total[:], zero_nt[:], 0.0, ALU.add, ALU.add).then_inc(chain, 1)
            dve.wait_ge(chain, 4)
            dve.tensor_tensor(begin[:], begin[:], total[:], ALU.subtract).then_inc(chain, 1)
            dve.wait_ge(chain, 5)
            dve.tensor_tensor(begin[:], begin[:], ahead[:], ALU.add).then_inc(chain, 1)
            dve.wait_ge(chain, 6)
            dve.tensor_copy(begin_i[:], begin[:]).then_inc(begun, 1)
            dve.tensor_single_scalar(table[:, 0], begin[:], 1.0, ALU.add).then_inc(chain, 1)
            dve.wait_ge(chain, 7)
            def two_steps(m):
                for b in range(2):
                    s = m * 2 + b
                    cb = s * 6 + 7
                    one_hots(dve, s, b, onehot2)
                    dve.wait_ge(row_in[b], m * 16 + 16)
                    keys = c.edge[:, key, bass.ds(s * UG, UG)]
                    dve.tensor_tensor(same[:], key_row[:, b], replicate(keys, 2, ET), ALU.is_equal)\
                       .then_inc(chain, 1)
                    dve.wait_ge(chain, cb + 1)
                    dve.tensor_tensor(same2[:], same[:], replicate(c.after[0:ET, 0:ET], 1, UG), ALU.mult)\
                       .then_inc(chain, 1)
                    dve.wait_ge(chain, cb + 2)
                    dve.tensor_reduce(rank[:], same2[:], AX.X, ALU.add).then_inc(chain, 1)
                    dve.wait_ge(hist_done, s + 1)
                    for g in range(UG):
                        if g:
                            wait_count(dve, table_done, s * UG + g)
                        dve.tensor_tensor(table[:, g + 1], table[:, g], ps_hist[b][:, g], ALU.add)\
                           .then_inc(table_done, 1)
                    dve.wait_ge(base_done, s + 1)
                    dve.tensor_tensor(picked[:], ps_base[:], hi[:, b], ALU.mult).then_inc(chain, 1)
                    dve.wait_ge(table_done, s * UG + UG)
                    dve.tensor_copy(table[:, 0], table[:, UG]).then_inc(chain, 1)
                    dve.wait_ge(chain, cb + 5)
                    dve.tensor_reduce(base[:], picked[:], AX.X, ALU.add).then_inc(chain, 1)
                    dve.wait_ge(chain, cb + 6)
                    wait_count(dve, sent[b], before[b] + m * (16 * UG))
                    dve.tensor_tensor(position[:, b], base[:], rank[:], ALU.add).then_inc(pos_done, 1)
            in_pairs(dve, two_steps)

        @block.tensor
        def _(pe):
            pe.wait_ge(zeroed, 1)
            pe.matmul(ps_count[:, 0:NT], zero_lo[:], zero_lo[:, 0:NT], start=True, stop=False,
                      skip_group_check=True).then_inc(counted, 1)
            def two_steps(m):
                for b in range(2):
                    pe.wait_ge(onehot, (m * 2 + b) * 2 + 2)
                    for g in range(UG):
                        mm = pe.matmul(ps_count[:, 0:NT], lo[:, b, g], hi[:, b, g], start=False, stop=False,
                                       skip_group_check=True)
                    mm.then_inc(counted, 1)
            in_pairs(pe, two_steps)
            pe.wait_ge(off, 1)
            pe.matmul(ps_pre[:, 0], c.before[:], count[:], start=True, stop=True)
            pe.matmul(ps_pre[:, 1], c.ones[:], count[:], start=True, stop=True).then_inc(prefixed, 1)
            def two_steps(m):
                for b in range(2):
                    s = m * 2 + b
                    pe.wait_ge(onehot2, s * 2 + 2)
                    for g in range(UG):
                        mm = pe.transpose(ps_lo_t[b][:, g, 0:ET], lo[:, b, g], c.identb[0:ET, 0:ET])
                    mm.then_inc(turned, 1)
                    for g in range(UG):
                        mm = pe.matmul(ps_hist[b][:, g], lo[:, b, g], hi[:, b, g], start=True, stop=True)
                    mm.then_inc(hist_done, 1)
                    pe.wait_ge(turn_copied, s + 1)
                    pe.wait_ge(table_done, s * UG + UG - 1)
                    for g in range(UG):
                        mm = pe.matmul(ps_base[:, g], lo_t[:, b, g], table[:, g], start=True, stop=True)
                    mm.then_inc(base_done, 1)
            in_pairs(pe, two_steps)

        @block.scalar
        def _(act):
            act.activation(payload[:, :, 0], c.edge[:, 1 - key, :], ACT.Copy).then_inc(pay_done, 1)
            act.activation(payload[:, :, 1], c.edge[:, key, :], ACT.Copy).then_inc(pay_done, 1)
            act.activation(payload[:, :, 2], c.edge[:, 2, :], ACT.Copy).then_inc(pay_done, 1)
            act.wait_ge(pay_done, 3)
            act.wait_ge(prep, 6)
            def two_steps(m):
                for b in range(2):
                    s = m * 2 + b
                    act.wait_ge(turned, s + 1)
                    act.activation(lo_t[:, b], ps_lo_t[b][:, :, 0:ET], ACT.Copy).then_inc(turn_copied, 1)
                    wait_count(act, sent[b], before[b] + m * (16 * UG))
                    act.activation(staged[:, b], payload[:, bass.ds(s * UG, UG), :], ACT.Copy)\
                       .then_inc(pay_done, 1)
            in_pairs(act, two_steps)

        @block.sync
        def _(sp):
            def two_steps(m):
                for b in range(2):
                    s = m * 2 + b
                    wait_count(sp, pos_done, m * 2)
                    row = keys_by_step[bass.ds(s, 1), :].to_broadcast([ET, UG * ET])
                    sp.dma_start(key_row[:, b].rearrange("p g j -> p (g j)"), row).then_inc(row_in[b], 16)
            in_pairs(sp, two_steps)

        @block.gpsimd
        def _(pool):
            pool.memset(payload[:, :, 3], 1.0).then_inc(prep, 1)
            pool.tensor_copy(self_row[:, :, 0], c.node_id[:]).then_inc(prep, 1)
            pool.tensor_copy(self_row[:, :, 1], c.node_id[:]).then_inc(prep, 1)
            pool.memset(self_row[:, :, 2:4], 0.0).then_inc(prep, 1)
            pool.memset(pad_row[:, :, 0:2], float(NP - 1)).then_inc(prep, 1)
            pool.memset(pad_row[:, :, 2:4], 0.0).then_inc(prep, 1)
            pool.wait_ge(prep, 6)
            pool.dma_start(sorted_rows[E + NP:POS, :].rearrange("(p n) f -> p (n f)", n=PR),
                           pad_row[:].rearrange("p n f -> p (n f)")).then_inc(self_sent, 16)
            pool.wait_ge(begun, 1)
            for b in range(NT):
                pool.indirect_dma_start(sorted_rows, bass.IndirectOffsetOnAxis(ap=begin_i[:, b:b + 1], axis=0),
                                        self_row[:, b, :], None).then_inc(self_sent, 16)
            def two_steps(m):
                for b in range(2):
                    s = m * 2 + b
                    pool.wait_ge(pay_done, s + 4)
                    wait_count(pool, fenced, s)
                    pool.wait_ge(pos_done, s + 1)
                    pool.tensor_tensor(c.fence[:], c.ones[0:1, 0:1], c.ones[0:1, 0:1], ALU.add)\
                        .then_inc(fenced, 1)
                    for g in range(UG):
                        pool.indirect_dma_start(
                            sorted_rows, bass.IndirectOffsetOnAxis(ap=position[:, b, g:g + 1], axis=0),
                            staged[:, b, g, :], None).then_inc(sent[b], 16)
            in_pairs(pool, two_steps)
            pool.wait_ge(self_sent, before[2] + 16 * (NT + 1))
            for b in range(2):
                wait_count(pool, sent[b], before[b] + 16 * UG * (US // 2))
        c.pool_count[0:3] = [before[0] + 8 * UG * US, before[1] + 8 * UG * US, before[2] + 16 * (NT + 1)]


def read_sorted(nc, c, name, sorted_rows, runs, slot, real_slot, first, neighbour, etype):
    with ExitStack() as st:
        kit = Kit(nc, st)
        rows = kit.sb(f"{name}_rows", [TB, NBLK, P, 4])
        start = kit.sb(f"{name}_start", [TB, NBLK, 2, P])
        cols = kit.sb(f"{name}_cols", [P, 4, T])
        tmp = kit.sb(f"{name}_tmp", [P, T])
        ps = [kit.ps(f"{name}_ps{i}", [P, 4, P]) for i in range(2)]
        ps_first = [kit.ps(f"{name}_ps_first{i}", [P, T // 2]) for i in range(2)]
        loaded, turned, copied, step, stored = (kit.sem(f"{name}_back_{n}") for n in
                                                ("loaded", "turned", "copied", "step", "stored"))
        block = st.enter_context(nc.Block())
        n_steps = 8 + (etype is not None)

        @block.sync
        def _(sp):
            view = sorted_rows.rearrange("(b t p) f -> t b (p f)", t=TB, p=P)
            sp.dma_start(rows[:].rearrange("t b p f -> t b (p f)"), view).then_inc(loaded, 16)
            sp.wait_ge(step, 3)
            for kind in range(2):
                view = runs[kind].rearrange("(b t p) -> t b p", t=TB, p=P)
                sp.dma_start(view, start[:, :, kind, :]).then_inc(stored, 16)
            sp.wait_ge(stored, 32)

        @block.tensor
        def _(pe):
            pe.wait_ge(loaded, 16)
            for b in range(NBLK):
                if b >= 2:
                    pe.wait_ge(copied, b - 1)
                for f in range(4):
                    mm = pe.transpose(ps[b % 2][:, f, 0:TB], rows[:, b, :, f], c.ident[0:TB, 0:TB])
                mm.then_inc(turned, 1)
            pe.wait_ge(copied, NBLK)
            for h in range(2):
                mm = pe.matmul(ps_first[h][:], c.first_row[:], cols[:, 1, h * (T // 2):(h + 1) * (T // 2)],
                               start=True, stop=True)
            mm.then_inc(turned, 1)

        @block.scalar
        def _(act):
            for b in range(NBLK):
                act.wait_ge(turned, b + 1)
                act.activation(cols[:, :, b * TB:(b + 1) * TB], ps[b % 2][:, :, 0:TB], ACT.Copy)\
                   .then_inc(copied, 1)

        @block.vector
        def _(dve):
            dve.wait_ge(loaded, 16)
            dve.tensor_scalar(start[:, :, 0, :], rows[:, :, :, 3], BIG, BIG, ALU.mult, ALU.subtract)\
               .then_inc(step, 1)
            dve.memset(start[:, :, 1, P - 1:P], -BIG).then_inc(step, 1)
            dve.tensor_scalar(start[:, :, 1, 0:P - 1], rows[:, :, 1:P, 3], BIG, BIG, ALU.mult, ALU.subtract)\
               .then_inc(step, 1)
            dve.wait_ge(turned, NBLK + 1)
            for h in range(2):
                part = slice(h * (T // 2), (h + 1) * (T // 2))
                dve.tensor_tensor(slot[:, part], cols[:, 1, part], ps_first[h][:], ALU.subtract)\
                   .then_inc(step, 1)
            dve.wait_ge(step, 5)
            dve.tensor_single_scalar(tmp[:], slot[:], 1.0, ALU.add).then_inc(step, 1)
            dve.wait_ge(step, 6)
            dve.tensor_tensor(tmp[:], tmp[:], cols[:, 3, :], ALU.mult).then_inc(step, 1)
            dve.wait_ge(step, 7)
            dve.tensor_single_scalar(real_slot[:], tmp[:], -1.0, ALU.add).then_inc(step, 1)
            dve.tensor_copy(neighbour[:], cols[:, 0, :]).then_inc(step, 1)
            dve.tensor_copy(first[:], cols[0:1, 1, :]).then_inc(step, 1)
            if etype is not None:
                dve.tensor_copy(etype[:], cols[:, 2, :]).then_inc(step, 1)


def gather_rows(pool, c, k, q, slots, table, index, rows, staged, fenced, used, landed, landed_before):
    half = RING // 2
    if q % half == 0:
        for r in range(q, q + half):
            wait_count(pool, landed[r], landed_before[r] + turn(k) * (16 * G))
        pool.tensor_copy(slots[:, q * G:(q + half) * G], index[:, bass.ds(k * G, half * G)]).then_inc(staged, 1)
        pool.wait_ge(staged, k // half + 1)
    wait_count(pool, used, k - RING + 1)
    wait_count(pool, fenced, k)
    pool.tensor_tensor(c.fence[:], c.ones[0:1, 0:1], c.ones[0:1, 0:1], ALU.add).then_inc(fenced, 1)
    for g in range(G):
        pool.indirect_dma_start(rows[:, q, g, :], None, table,
                                bass.IndirectOffsetOnAxis(ap=slots[:, q * G + g:q * G + g + 1], axis=0))\
            .then_inc(landed[q], 16)


def window_starts(nc, engine, first, k):
    return nc.values_load_multi_w_load_instructions(first[0:1, bass.ds(k * G, G)], engines=[engine],
                                                    min_val=0, max_val=NP - 1)[1]


def attention_pass(nc, c, name, heads, dot, table, window_table, runs, slot, first, index):
    width = D // heads
    rw = 2 * D if dot else D
    v0 = rw - D
    engine = mybir.EngineType
    with ExitStack() as st:
        kit = Kit(nc, st)
        slots = kit.sb(f"{name}_slots", [P, RING * G], I32)
        rows = kit.sb(f"{name}_rows", [P, RING, G, rw])
        win = kit.sb(f"{name}_win", [P, 2, G, D])
        run = kit.sb(f"{name}_run", [heads, 2, 2, G * P])
        sel = kit.sb(f"{name}_sel", [P, RING, G, P])
        sel_t = kit.sb(f"{name}_sel_t", [P, 2, G, P])
        z = kit.sb(f"{name}_z", [P, 2, G, D])
        score = kit.sb(f"{name}_score", [P, 2, G, heads])
        prefix = kit.sb(f"{name}_prefix", [heads, 2, G * P])
        top = kit.sb(f"{name}_top", [heads, 2, G * P])
        drop = kit.sb(f"{name}_drop", [heads, 2, G])
        less = kit.sb(f"{name}_less", [P, 2, G, heads])
        weight = kit.sb(f"{name}_weight", [P, 2, G, D])
        keep = kit.sb(f"{name}_keep", [P, RING, G])
        val = kit.sb(f"{name}_val", [P, 2, G, D])
        ps_t = kit.ps(f"{name}_ps_t", [P, G, P])
        ps_x = kit.ps(f"{name}_ps_x", [P, G, D])
        ps_s = kit.ps(f"{name}_ps_s", [heads, G * P])
        ps_m = kit.ps(f"{name}_ps_m", [P, G * heads + G])
        ps_n = [kit.ps(f"{name}_ps_n{i}", [P, 2, 2, P]) for i in range(4)]
        hsel = c.hsel4 if heads == 4 else c.hsel8
        (staged, fenced, sel_done, selt_ps, selt_done, spread_done, z_done, leaky_done, prod_done, score_done,
         score_t, prefix_done, top_done, drop_done, top_ps, less_done, exp_done, val_done, sums_done,
         copy_done, head_done, cleared, diff_done, first_prefix) = (
            kit.sem(f"{name}_{n}") for n in
            ("staged", "fenced", "sel_done", "selt_ps", "selt_done", "spread_done", "z_done", "leaky_done",
             "prod_done", "score_done", "score_t", "prefix_done", "top_done", "drop_done", "top_ps",
             "less_done", "exp_done", "val_done", "sums_done", "copy_done", "head_done", "cleared",
             "diff_done", "first_prefix"))
        landed, landed_before = c.pool_dma, list(c.pool_count)
        win_in = [kit.sem(f"{name}_win_in{i}") for i in range(2)]
        run_in = [kit.sem(f"{name}_run_in{i}") for i in range(2)]
        block = st.enter_context(nc.Block())

        @block.sync
        def _(sp):
            def emit(k, q):
                if inside(k, 0):
                    b = q % 2
                    starts = window_starts(nc, engine.SP, first, k)
                    wait_count(sp, spread_done, k - 1)
                    for g in range(G):
                        sp.dma_start(win[:, b, g, :], window_table[bass.ds(starts[g], P), :])\
                          .then_inc(win_in[b], 16)
                    wait_count(sp, top_done, k - 1)
                    rows_of = runs[:, bass.ds(k * G * P, G * P)]
                    sp.dma_start(run[:, b], replicate(rows_of, 0, heads)).then_inc(run_in[b], 16)
            staggered(sp, emit, 0)

        @block.gpsimd
        def _(pool):
            pool.memset(c.num[:], 0.0).then_inc(cleared, 1)

            def emit(k, q):
                if inside(k, 0):
                    gather_rows(pool, c, k, q, slots, table, index, rows, staged, fenced, val_done,
                                landed, landed_before)
            staggered(pool, emit, 0)

        @block.tensor
        def _(pe):
            def emit(k, q):
                b = q % 2
                if inside(k, 0):
                    pe.wait_ge(sel_done, k + 1)
                    wait_count(pe, selt_done, k)
                    for g in range(G):
                        mm = pe.transpose(ps_t[:, g], sel[:, q, g], c.ident[:])
                    mm.then_inc(selt_ps, 1)
                if inside(k, 4):
                    p = (q - 4) % RING
                    pe.wait_ge(val_done, k - 3)
                    wait_count(pe, head_done, (k - 5) * G)
                    for g in range(G):
                        out = ps_n[2 * b + g // 2][:, g % 2]
                        pe.matmul(out[:, 0], val[:, b, g], sel[:, p, g], start=True, stop=True)
                        mm = pe.matmul(out[:, 1], weight[:, b, g], sel[:, p, g], start=True, stop=True)
                    mm.then_inc(sums_done, 1)
                if inside(k, 0):
                    pe.wait_ge(selt_done, k + 1)
                    pe.wait_ge(win_in[b], turn2(k) * (16 * G) + 16 * G)
                    wait_count(pe, z_done, k)
                    for g in range(G):
                        mm = pe.matmul(ps_x[:, g], sel_t[:, b, g], win[:, b, g], start=True, stop=True)
                    mm.then_inc(spread_done, 1)
                if inside(k, 2):
                    pe.wait_ge(drop_done, k - 1)
                    wait_count(pe, exp_done, k - 2)
                    for g in range(G):
                        pe.matmul(ps_m[:, g * heads:(g + 1) * heads], top[:, b, g * P:(g + 1) * P],
                                  c.ident[0:heads, 0:heads], start=True, stop=True)
                    pe.matmul(ps_m[:, G * heads:], hsel[:], drop[:, b], start=True, stop=True)\
                      .then_inc(top_ps, 1)
                if inside(k, 1):
                    o = 1 - b
                    pe.wait_ge(score_done, k)
                    wait_count(pe, prefix_done, k - 1)
                    for g in range(G):
                        mm = pe.matmul(ps_s[:, g * P:(g + 1) * P], score[:, o, g], c.ident[:],
                                       start=True, stop=True)
                    mm.then_inc(score_t, 1)
            staggered(pe, emit, 4)

        @block.scalar
        def _(act):
            def emit(k, q):
                b = q % 2
                if inside(k, 4):
                    starts = window_starts(nc, engine.Activation, first, k - 4)
                if inside(k, 0):
                    act.wait_ge(selt_ps, k + 1)
                    wait_count(act, spread_done, k - 1)
                    act.activation(sel_t[:, b], ps_t, ACT.Copy).then_inc(selt_done, 1)
                if inside(k, 4):
                    for g in range(G):
                        if g == 0:
                            act.wait_ge(sums_done, k - 3)
                            if isinstance(k, int) and k == 4:
                                act.wait_ge(cleared, 1)
                        wait_count(act, copy_done, (k - 4) * G + g)
                        act.activation(c.num[:, :, bass.ds(starts[g] + 1, P - 1)],
                                       ps_n[2 * b + g // 2][:, g % 2, :, 1:P], ACT.Copy)\
                           .then_inc(copy_done, 1)
                if inside(k, 2):
                    p = (q - 2) % RING
                    act.wait_ge(less_done, k - 1)
                    wait_count(act, sums_done, k - 3)
                    act.activation(weight[:, b].rearrange("p g (h c) -> p (g h) c", h=heads),
                                   replicate(less[:, b].rearrange("p g h -> p (g h)"), 2, width), ACT.Exp)
                    act.activation(keep[:, p], ps_m[:, G * heads:], ACT.Exp).then_inc(exp_done, 1)
            staggered(act, emit, 4)

        @block.vector
        def _(dve):
            dve.memset(prefix[:, 1], 0.0).then_inc(first_prefix, 1)

            def emit(k, q):
                b = q % 2
                o = 1 - b
                if inside(k, 5):
                    starts = window_starts(nc, engine.DVE, first, k - 5)

                def head(g):
                    if inside(k, 5):
                        p = (q - 5) % RING
                        if g == 0:
                            dve.wait_ge(copy_done, (k - 4) * G)
                        wait_count(dve, head_done, (k - 5) * G + g)
                        at = c.num[:, :, bass.ds(starts[g], 1)]
                        dve.scalar_tensor_tensor(at, at, keep[:, p, g:g + 1],
                                                 ps_n[2 * o + g // 2][:, g % 2, :, 0:1],
                                                 ALU.mult, ALU.add).then_inc(head_done, 1)

                if inside(k, 0):
                    wait_count(dve, sums_done, k - RING + 1)
                    dve.tensor_tensor(sel[:, q], replicate(c.iota_f[:], 1, G),
                                      replicate(slot[:, bass.ds(k * G, G)], 2, P),
                                      ALU.is_equal).then_inc(sel_done, 1)
                if inside(k, 2):
                    dve.wait_ge(score_t, k - 1)
                    dve.wait_ge(run_in[b], turn2(k, 2) * 16 + 16)
                    if isinstance(k, int) and k == 2:
                        dve.wait_ge(first_prefix, 1)
                    wait_count(dve, prefix_done, k - 2)
                    dve.tensor_tensor_scan(prefix[:, b], run[:, b, 0], ps_s, prefix[:, o, G * P - 1:],
                                           ALU.add, ALU.max).then_inc(prefix_done, 1)
                head(0)
                if inside(k, 1) and not dot:
                    dve.wait_ge(z_done, k)
                    dve.scalar_tensor_tensor(z[:, o], z[:, o], LEAK, z[:, o], ALU.mult, ALU.max)\
                       .then_inc(leaky_done, 1)
                if inside(k, 2):
                    dve.wait_ge(prefix_done, k - 1)
                    wait_count(dve, top_ps, k - 3)
                    dve.tensor_tensor_scan(top[:, b, ::-1], run[:, b, 1, ::-1], prefix[:, b, ::-1], -BIG,
                                           ALU.add, ALU.max).then_inc(top_done, 1)
                head(1)
                if inside(k, 1) and not dot:
                    dve.wait_ge(leaky_done, k)
                    dve.tensor_tensor(z[:, o], z[:, o], replicate(c.att[:], 1, G), ALU.mult)\
                       .then_inc(prod_done, 1)
                if inside(k, 3):
                    p = (q - 3) % RING
                    dve.wait_ge(exp_done, k - 2)
                    wait_count(dve, sums_done, k - 4)
                    dve.tensor_tensor(val[:, o], rows[:, p, :, v0:], weight[:, o], ALU.mult).then_inc(val_done, 1)
                if inside(k, 2):
                    dve.wait_ge(top_done, k - 1)
                    dve.tensor_tensor(drop[:, b, 1:G], prefix[:, b, P - 1:(G - 1) * P:P],
                                      top[:, b, P::P], ALU.subtract).then_inc(diff_done, 1)
                    dve.tensor_tensor(drop[:, b, 0:1], prefix[:, o, G * P - 1:], top[:, b, 0:1],
                                      ALU.subtract).then_inc(diff_done, 1)
                head(2)
                if inside(k, 1):
                    if dot:
                        dve.wait_ge(z_done, k)
                    else:
                        dve.wait_ge(prod_done, k)
                    wait_count(dve, score_t, k - 2)
                    dve.tensor_reduce(score[:, o], z[:, o].rearrange("p g (h c) -> p g h c", h=heads),
                                      AX.X, ALU.add).then_inc(score_done, 1)
                if inside(k, 2):
                    dve.wait_ge(diff_done, (k - 1) * 2)
                    dve.tensor_single_scalar(drop[:, b], drop[:, b], 0.0, ALU.min).then_inc(drop_done, 1)
                head(3)
                if inside(k, 0):
                    dve.wait_ge(spread_done, k + 1)
                    dve.wait_ge(landed[q], landed_before[q] + turn(k) * (16 * G) + 16 * G)
                    wait_count(dve, score_done, k - 1)
                    dve.tensor_tensor(z[:, b], ps_x, rows[:, q, :, 0:D], ALU.mult if dot else ALU.add)\
                       .then_inc(z_done, 1)
                if inside(k, 2):
                    dve.wait_ge(top_ps, k - 1)
                    wait_count(dve, exp_done, k - 3)
                    dve.tensor_tensor(less[:, b], score[:, b],
                                      ps_m[:, 0:G * heads].rearrange("p (g h) -> p g h", g=G),
                                      ALU.subtract).then_inc(less_done, 1)
            staggered(dve, emit, 5)
        c.pool_count = [n + 16 * T // RING for n in landed_before]


def edge_score_pass(nc, c, table, window_table, slot, real_slot, first, index):
    engine = mybir.EngineType
    with ExitStack() as st:
        kit = Kit(nc, st)
        slots = kit.sb("l1_slots", [P, RING * G], I32)
        rows = kit.sb("l1_rows", [P, RING, G, D + 4])
        win = kit.sb("l1_win", [P, 2, G, 4])
        sel = kit.sb("l1_sel", [P, 2, G, P])
        sel_t = kit.sb("l1_sel_t", [P, 2, G, P])
        real = kit.sb("l1_real", [P, RING, G, P])
        e = kit.sb("l1_e", [P, 2, 3, G])
        weight = kit.sb("l1_weight", [P, 2, G])
        ps_t = kit.ps("l1_ps_t", [P, G, P])
        ps_x = [kit.ps(f"l1_ps_x{i}", [P, G, 4]) for i in range(2)]
        ps_n = [kit.ps(f"l1_ps_n{i}", [P, 2, 2, P]) for i in range(4)]
        (staged, fenced, sel_done, selt_ps, selt_done, spread_done, real_done, add_done, leaky_done, e_done,
         exp_done, scaled_done, sums_done, copy_done, head_done, cleared) = (
            kit.sem(f"l1_{n}") for n in
            ("staged", "fenced", "sel_done", "selt_ps", "selt_done", "spread_done", "real_done", "add_done",
             "leaky_done", "e_done", "exp_done", "scaled_done", "sums_done", "copy_done", "head_done",
             "cleared"))
        landed, landed_before = c.pool_dma, list(c.pool_count)
        win_in = [kit.sem(f"l1_win_in{i}") for i in range(2)]
        block = st.enter_context(nc.Block())

        @block.sync
        def _(sp):
            def emit(k, q):
                if inside(k, 0):
                    b = q % 2
                    starts = window_starts(nc, engine.SP, first, k)
                    wait_count(sp, spread_done, k - 1)
                    for g in range(G):
                        sp.dma_start(win[:, b, g, :], window_table[bass.ds(starts[g], P), :])\
                          .then_inc(win_in[b], 16)
            staggered(sp, emit, 0)

        @block.gpsimd
        def _(pool):
            pool.memset(c.num[:], 0.0).then_inc(cleared, 1)

            def emit(k, q):
                if inside(k, 0):
                    gather_rows(pool, c, k, q, slots, table, index, rows, staged, fenced, sums_done,
                                landed, landed_before)
            staggered(pool, emit, 0)

        @block.tensor
        def _(pe):
            def emit(k, q):
                b = q % 2
                if inside(k, 0):
                    pe.wait_ge(sel_done, k + 1)
                    wait_count(pe, selt_done, k)
                    for g in range(G):
                        mm = pe.transpose(ps_t[:, g], sel[:, b, g], c.ident[:])
                    mm.then_inc(selt_ps, 1)
                if inside(k, 3):
                    o, p = 1 - b, (q - 3) % RING
                    pe.wait_ge(scaled_done, k - 2)
                    wait_count(pe, head_done, (k - 4) * G)
                    for g in range(G):
                        out = ps_n[2 * o + g // 2][:, g % 2]
                        pe.matmul(out[:, 0], rows[:, p, g, 0:D], real[:, p, g], start=True, stop=True)
                        mm = pe.matmul(out[:, 1], c.ones[:], real[:, p, g], start=True, stop=True)
                    mm.then_inc(sums_done, 1)
                if inside(k, 0):
                    pe.wait_ge(selt_done, k + 1)
                    pe.wait_ge(win_in[b], turn2(k) * (16 * G) + 16 * G)
                    wait_count(pe, add_done, k - 1)
                    for g in range(G):
                        mm = pe.matmul(ps_x[b][:, g], sel_t[:, b, g], win[:, b, g], start=True, stop=True)
                    mm.then_inc(spread_done, 1)
            staggered(pe, emit, 3)

        @block.scalar
        def _(act):
            def emit(k, q):
                b = q % 2
                if inside(k, 3):
                    starts = window_starts(nc, engine.Activation, first, k - 3)
                if inside(k, 0):
                    act.wait_ge(selt_ps, k + 1)
                    wait_count(act, spread_done, k - 1)
                    act.activation(sel_t[:, b], ps_t, ACT.Copy).then_inc(selt_done, 1)
                if inside(k, 1):
                    act.wait_ge(e_done, k)
                    wait_count(act, scaled_done, k - 2)
                    act.activation(weight[:, 1 - b], e[:, 1 - b, 2], ACT.Exp).then_inc(exp_done, 1)
                if inside(k, 3):
                    for g in range(G):
                        if g == 0:
                            act.wait_ge(sums_done, k - 2)
                            if isinstance(k, int) and k == 3:
                                act.wait_ge(cleared, 1)
                        wait_count(act, copy_done, (k - 3) * G + g)
                        act.activation(c.num[:, :, bass.ds(starts[g] + 1, P - 1)],
                                       ps_n[2 * (1 - b) + g // 2][:, g % 2, :, 1:P], ACT.Copy)\
                           .then_inc(copy_done, 1)
            staggered(act, emit, 3)

        @block.vector
        def _(dve):
            def emit(k, q):
                b = q % 2
                o = 1 - b
                if inside(k, 4):
                    starts = window_starts(nc, engine.DVE, first, k - 4)

                def head(g):
                    if inside(k, 4):
                        if g == 0:
                            dve.wait_ge(copy_done, (k - 3) * G)
                        wait_count(dve, head_done, (k - 4) * G + g)
                        at = c.num[:, :, bass.ds(starts[g], 1)]
                        dve.tensor_tensor(at, at, ps_n[2 * b + g // 2][:, g % 2, :, 0:1], ALU.add)\
                           .then_inc(head_done, 1)

                if inside(k, 0):
                    wait_count(dve, selt_done, k - 1)
                    dve.tensor_tensor(sel[:, b], replicate(c.iota_f[:], 1, G),
                                      replicate(slot[:, bass.ds(k * G, G)], 2, P),
                                      ALU.is_equal).then_inc(sel_done, 1)
                if inside(k, 1):
                    dve.wait_ge(spread_done, k)
                    dve.wait_ge(landed[(q - 1) % RING],
                                landed_before[(q - 1) % RING] + turn(k, 1) * (16 * G) + 16 * G)
                    wait_count(dve, leaky_done, k - 2)
                    dve.tensor_tensor(e[:, o, 0], ps_x[o][:, :, 0], rows[:, (q - 1) % RING, :, D], ALU.add)\
                       .then_inc(add_done, 1)
                head(0)
                if inside(k, 0):
                    wait_count(dve, sums_done, k - RING + 1)
                    dve.tensor_tensor(real[:, q], replicate(c.iota_f[:], 1, G),
                                      replicate(real_slot[:, bass.ds(k * G, G)], 2, P),
                                      ALU.is_equal).then_inc(real_done, 1)
                if inside(k, 1):
                    dve.wait_ge(add_done, k)
                    dve.scalar_tensor_tensor(e[:, o, 1], e[:, o, 0], LEAK, e[:, o, 0], ALU.mult, ALU.max)\
                       .then_inc(leaky_done, 1)
                head(1)
                head(2)
                if inside(k, 2):
                    p = (q - 2) % RING
                    dve.wait_ge(exp_done, k - 1)
                    dve.wait_ge(real_done, k - 1)
                    dve.tensor_tensor(real[:, p], real[:, p], replicate(weight[:, b], 2, P), ALU.mult)\
                       .then_inc(scaled_done, 1)
                if inside(k, 1):
                    dve.wait_ge(leaky_done, k)
                    wait_count(dve, exp_done, k - 2)
                    dve.tensor_scalar(e[:, o, 2], e[:, o, 1], -2.0, 2.0, ALU.max, ALU.min).then_inc(e_done, 1)
                head(3)
            staggered(dve, emit, 4)
        c.pool_count = [n + 16 * T // RING for n in landed_before]


def sum_pass(nc, c, name, table, real_slot, first, index, acc, counts):
    with ExitStack() as st:
        kit = Kit(nc, st)
        parts = 2 if counts else 1
        slots = kit.sb(f"{name}_slots", [P, RING * G], I32)
        rows = kit.sb(f"{name}_rows", [P, RING, G, D])
        sel = kit.sb(f"{name}_sel", [P, RING, G, P])
        ps_n = [kit.ps(f"{name}_ps_n{i}", [P, 2, 2, P]) for i in range(4)]
        staged, fenced, sel_done, sums_done, copy_done, head_done, cleared = (
            kit.sem(f"{name}_{n}") for n in
            ("staged", "fenced", "sel_done", "sums_done", "copy_done", "head_done", "cleared"))
        landed, landed_before = c.pool_dma, list(c.pool_count)
        block = st.enter_context(nc.Block())

        @block.gpsimd
        def _(pool):
            pool.memset(acc[:, 0:parts], 0.0).then_inc(cleared, 1)

            def emit(k, q):
                if inside(k, 0):
                    gather_rows(pool, c, k, q, slots, table, index, rows, staged, fenced, sums_done,
                                landed, landed_before)
            staggered(pool, emit, 0)

        @block.tensor
        def _(pe):
            def emit(k, q):
                b = q % 2
                if inside(k, 0):
                    pe.wait_ge(sel_done, k + 1)
                    pe.wait_ge(landed[q], landed_before[q] + turn(k) * (16 * G) + 16 * G)
                    wait_count(pe, copy_done, (k - 1) * G)
                    wait_count(pe, head_done, (k - 1) * G)
                    for g in range(G):
                        out = ps_n[2 * b + g // 2][:, g % 2]
                        mm = pe.matmul(out[:, 0], rows[:, q, g], sel[:, q, g], start=True, stop=True)
                        if counts:
                            mm = pe.matmul(out[:, 1], c.ones[:], sel[:, q, g], start=True, stop=True)
                    mm.then_inc(sums_done, 1)
            staggered(pe, emit, 0)

        @block.scalar
        def _(act):
            def emit(k, q):
                b = q % 2
                if inside(k, 0):
                    starts = window_starts(nc, mybir.EngineType.Activation, first, k)
                    for g in range(G):
                        n0 = starts[g]
                        if g == 0:
                            act.wait_ge(sums_done, k + 1)
                            act.wait_ge(cleared, 1)
                        wait_count(act, copy_done, k * G + g)
                        act.activation(acc[:, 0:parts, bass.ds(n0 + 1, P - 1)],
                                       ps_n[2 * b + g // 2][:, g % 2, 0:parts, 1:P], ACT.Copy)\
                           .then_inc(copy_done, 1)
            staggered(act, emit, 0)

        @block.vector
        def _(dve):
            def emit(k, q):
                if inside(k, 0):
                    wait_count(dve, sums_done, k - RING + 1)
                    dve.tensor_tensor(sel[:, q], replicate(c.iota_f[:], 1, G),
                                      replicate(real_slot[:, bass.ds(k * G, G)], 2, P),
                                      ALU.is_equal).then_inc(sel_done, 1)
                if inside(k, 1):
                    o = (q - 1) % 2
                    starts = window_starts(nc, mybir.EngineType.DVE, first, k - 1)
                    for g in range(G):
                        n0 = starts[g]
                        if g == 0:
                            dve.wait_ge(copy_done, k * G)
                        wait_count(dve, head_done, (k - 1) * G + g)
                        if isinstance(k, int) and k == 1 and g == 0:
                            dve.wait_ge(cleared, 1)
                        at = acc[:, 0:parts, bass.ds(n0, 1)]
                        dve.tensor_tensor(at, at, ps_n[2 * o + g // 2][:, g % 2, 0:parts, 0:1], ALU.add)\
                           .then_inc(head_done, 1)
            staggered(dve, emit, 1)
        c.pool_count = [n + 16 * T // RING for n in landed_before]


def load_weights(nc, c, w):
    with ExitStack() as st:
        kit = Kit(nc, st)
        att_cols = kit.sb("att_cols", [P, 2])
        kernel_t = kit.sb("kernel_t", [P, P])
        zero_rows = kit.sb("zero_rows", [P, D])
        ps_t, ps_a = kit.ps("w_ps_t", [P, P]), kit.ps("w_ps_a", [P, 2])
        cleared, loaded, turned, copied = (kit.sem(n) for n in ("w_cleared", "w_loaded", "w_turned", "w_copied"))
        block = st.enter_context(nc.Block())
        row = lambda a: a.rearrange("(a n) -> a n", a=1)
        col = lambda a: a.rearrange("(p a) -> p a", a=1)
        loads = [(c.w0[:, 0:D], w["L0_gnn_W_l"]), (c.w0[:, D:2 * D], w["L0_gnn_W_r"]),
                 (c.b0[:, 0:D], row(w["L0_gnn_b_l"])), (c.b0[:, D:2 * D], row(w["L0_gnn_b_r"])),
                 (c.w1[:, 0:D], w["L1_gnn_kernel"]),
                 (c.w2[:, 0:D], w["L2_gnn_key_kernel"]), (c.w2[:, D:2 * D], w["L2_gnn_kernel"]),
                 (c.w2[:, 2 * D:], w["L2_gnn_query_kernel"]),
                 (c.b2[:, 0:D], row(w["L2_gnn_key_bias"])), (c.b2[:, 2 * D:], row(w["L2_gnn_query_bias"])),
                 (c.bias0[:], col(w["L0_gnn_bias"])), (c.gamma[:], col(w["L0_gnn_gamma"])),
                 (c.beta[:], col(w["L0_gnn_beta"])), (c.bias2[:], col(w["L2_gnn_bias"])),
                 (c.att[:], row(w["L0_gnn_att"].rearrange("h c -> (h c)")).to_broadcast([P, D])),
                 (att_cols[:, 0:1], w["L1_gnn_kernel_attention"][D:2 * D, :]),
                 (att_cols[:, 1:2], w["L1_gnn_kernel_attention"][0:D, :])]
        for l in range(2):
            loads += [(c.wn[:, l], w["L3_gnn_Wn"][l]), (c.wl[:, l], w["L3_gnn_Wl"][l]),
                      (c.wa[:, l], w["L3_gnn_Wa"][l])]
        pads = [(c.win0, D), (c.win1, 4), (c.win2, D)]

        @block.gpsimd
        def _(pool):
            pool.memset(c.w1[:], 0.0).then_inc(cleared, 1)
            pool.memset(c.b2[:], 0.0).then_inc(cleared, 1)
            pool.memset(zero_rows[:], 0.0).then_inc(cleared, 1)

        @block.sync
        def _(sp):
            sp.wait_ge(cleared, 3)
            for to, of in loads:
                sp.dma_start(to, of).then_inc(loaded, 16)
            for table, width in pads:
                sp.dma_start(table[NP:NW, :], zero_rows[:, 0:width]).then_inc(loaded, 16)
            sp.wait_ge(loaded, 16 * (len(loads) + len(pads)))

        @block.tensor
        def _(pe):
            pe.wait_ge(loaded, 16 * (len(loads) + len(pads)))
            pe.transpose(ps_t, c.w1[:, 0:D], c.ident[:]).then_inc(turned, 1)
            pe.wait_ge(copied, 1)
            pe.matmul(ps_a, kernel_t[:], att_cols[:], start=True, stop=True).then_inc(turned, 1)

        @block.vector
        def _(dve):
            dve.wait_ge(turned, 1)
            dve.tensor_copy(kernel_t[:], ps_t).then_inc(copied, 1)
            dve.wait_ge(turned, 2)
            dve.tensor_copy(c.w1[:, D:D + 1], ps_a[:, 0:1]).then_inc(copied, 1)
            dve.tensor_copy(c.w1[:, D + 4:D + 5], ps_a[:, 1:2]).then_inc(copied, 1)


STAGES = {
    "load": ["turn", "take0", "take1"],
    "gat": ["den", "recip", "ratio", "bias", "a_mean", "a_center", "a_square", "a_var", "a_std", "a_rstd",
            "a_norm", "affine", "negative", "exp", "elu", "residual"],
    "edge": ["den", "recip", "ratio", "residual"],
    "dot": ["recip", "ratio", "residual"],
    "rel0": ["degree", "root", "inverse", "has_in", "products", "sum", "scaled", "self_l", "add_l", "no_in",
             "self_a", "add_a", "rrelu"],
}
LN_STEPS = ["b_mean", "b_center", "b_square", "b_var", "b_std", "b_rstd", "b_norm"]
STAGES["rel1"] = STAGES["rel0"] + ["residual"]


def node_step(nc, c, stage, weight, bias, relu, outputs, layer=0, x_dram=None, keep_in=None):
    steps = STAGES[stage] + (LN_STEPS if stage in ("gat", "edge", "dot", "rel1") else []) + ["keep"]
    order = {s: i for i, s in enumerate(steps)}
    per_j = len(steps)
    width = weight.shape[-1]
    with ExitStack() as st:
        kit = Kit(nc, st)
        name = f"n_{stage}"
        a, b, d, s = (kit.sb(f"{name}_{x}", [P, CW]) for x in "abds")
        m = kit.sb(f"{name}_m", [P, CW]) if stage[:3] == "rel" else None
        x_rows = kit.sb(f"{name}_x_rows", [P, CB, D]) if stage == "load" else None
        tab = kit.sb(f"{name}_tab", [P, CB, width])
        pa, pb, pc = (kit.ps(f"{name}_p{x}", [P, 2, 512]) for x in "abc")
        pt = [kit.ps(f"{name}_pt{i}", [P, 512]) for i in range(2)]
        step_done, tab_mm, tab_cp, x_in, x_zero = (kit.sem(f"{name}_{x}") for x in
                                                   ("step_done", "tab_mm", "tab_cp", "x_in", "x_zero"))
        stored = kit.sem(f"{name}_stored")
        block = st.enter_context(nc.Block())
        whole = lambda t: t[:, 0:2 * HW] if len(t.shape) == 2 else t
        halves = lambda t: t[:, 0:CW].rearrange("p (h w) -> p h w", h=2)
        banks = lambda t: t[:, :, 0:HW]

        def here(eng, step, j):
            if step not in order:
                return False
            wait_count(eng, step_done, j * per_j + order[step])
            return True

        def last(j):
            return isinstance(j, int) and j == CS - 1

        def run(eng, body):
            body(0)
            with eng.Fori(1, CS - 1) as j:
                body(j)
            body(CS - 1)

        @block.sync
        def _(sp):
            def body(j):
                if stage == "load":
                    wait_count(sp, step_done, j * per_j)
                    if last(j):
                        full, rest = divmod(N - (CS - 1) * CW, P)
                        sp.wait_ge(x_zero, 1)
                        sp.dma_start(x_rows[:, 0:full], x_dram[j * CW:j * CW + full * P, :]
                                     .rearrange("(i p) d -> p i d", p=P)).then_inc(x_in, 16)
                        sp.dma_start(x_rows[0:rest, full], x_dram[N - rest:N, :]).then_inc(x_in, 16)
                    else:
                        sp.dma_start(x_rows[:], x_dram[bass.ds(j * CW, CW), :]
                                     .rearrange("(i p) d -> p i d", p=P)).then_inc(x_in, 16)
                sp.wait_ge(tab_cp, j * CB + CB)
                for table, c0, c1 in outputs:
                    if last(j) and table.shape[0] == N:
                        full, rest = divmod(N - (CS - 1) * CW, P)
                        sp.dma_start(table[j * CW:j * CW + full * P, :].rearrange("(i p) d -> p i d", p=P),
                                     tab[:, 0:full, c0:c1]).then_inc(stored, 16)
                        sp.dma_start(table[N - rest:N, :], tab[0:rest, full, c0:c1]).then_inc(stored, 16)
                        n_stores = 16 * (CS + 1)
                    else:
                        sp.dma_start(table[bass.ds(j * CW, CW), :].rearrange("(i p) d -> p i d", p=P),
                                     tab[:, :, c0:c1]).then_inc(stored, 16)
                        n_stores = 16 * len(outputs) * CS
                if last(j):
                    sp.wait_ge(stored, n_stores)
            run(sp, body)

        @block.tensor
        def _(pe):
            def mean(out, of):
                for h in range(2):
                    mm = pe.matmul(out[:, h, 0:HW], c.mean_w[:], of[:, h * HW:(h + 1) * HW],
                                   start=True, stop=True)
                mm.then_inc(step_done, 1)

            def body(j):
                if here(pe, "turn", j):
                    pe.wait_ge(x_in, j * 16 + (32 if last(j) else 16))
                    for i in range(CB):
                        mm = pe.transpose(pa[:, i // 4, (i % 4) * P:(i % 4 + 1) * P], x_rows[:, i], c.ident[:])
                    mm.then_inc(step_done, 1)
                if here(pe, "products", j):
                    feats = c.x if stage == "rel0" else c.hidden
                    for out, w, of in ((pa, c.wn, c.rel[:, 0]), (pb, c.wl, feats), (pc, c.wa, feats)):
                        for h in range(2):
                            mm = pe.matmul(out[:, h, 0:HW], w[:, layer], of[:, bass.ds(j * CW + h * HW, HW)],
                                           start=True, stop=True)
                    mm.then_inc(step_done, 1)
                for t in "ab":
                    if here(pe, f"{t}_mean", j):
                        mean(pa, a)
                    if here(pe, f"{t}_var", j):
                        mean(pb, s)
                wait_count(pe, step_done, j * per_j + order["keep"])
                for i in range(CB):
                    wait_count(pe, tab_cp, j * CB + max(i - 1, 0))
                    out = pt[i % 2][:, 0:width]
                    if bias is not None:
                        pe.matmul(out, c.one_row[:], bias[:], start=True, stop=False)
                    pe.matmul(out, a[:, i * P:(i + 1) * P], weight, start=bias is None, stop=True)\
                      .then_inc(tab_mm, 1)
            def body_runtime(j):
                body(j)
            run(pe, body_runtime)

        @block.scalar
        def _(act):
            def body(j):
                if here(act, "root", j):
                    act.activation(b[:], b[:], ACT.Sqrt).then_inc(step_done, 1)
                for t in "ab":
                    if here(act, f"{t}_square", j):
                        act.activation(s[:], d[:], ACT.Square).then_inc(step_done, 1)
                    if here(act, f"{t}_std", j):
                        act.activation(halves(s), banks(pb), ACT.Sqrt, bias=c.eps[:]).then_inc(step_done, 1)
                    if t == "a" and here(act, "exp", j):
                        act.activation(b[:], b[:], ACT.Exp).then_inc(step_done, 1)
                wait_count(act, stored, j * (16 * len(outputs)))
                for i in range(CB):
                    act.wait_ge(tab_mm, j * CB + i + 1)
                    at = 0
                    for c0, c1 in [*relu, (width, width)]:
                        if c0 > at:
                            ins = act.activation(tab[:, i, at:c0], pt[i % 2][:, at:c0], ACT.Copy)
                        if c1 > c0:
                            ins = act.activation(tab[:, i, c0:c1], pt[i % 2][:, c0:c1], ACT.Relu)
                        at = c1
                    ins.then_inc(tab_cp, 1)
            run(act, body)

        @block.vector
        def _(dve):
            def body(j):
                at = lambda t: t[:, bass.ds(j * CW, CW)]
                if stage == "load":
                    wait_count(dve, tab_mm, j * CB)
                    here(dve, "take0", j)
                    dve.tensor_copy(a[:, 0:512], pa[:, 0]).then_inc(step_done, 1)
                    here(dve, "take1", j)
                    dve.tensor_copy(a[:, 512:CW], pa[:, 1, 0:CW - 512]).then_inc(step_done, 1)
                if here(dve, "den", j):
                    dve.tensor_single_scalar(b[:], at(c.num[:, 1]), 1e-16 if stage == "gat" else 1e-9,
                                             ALU.add).then_inc(step_done, 1)
                if here(dve, "recip", j):
                    dve.reciprocal(b[:], b[:] if stage != "dot" else at(c.num[:, 1])).then_inc(step_done, 1)
                if here(dve, "ratio", j):
                    wait_count(dve, tab_mm, j * CB)
                    dve.tensor_tensor(a[:], at(c.num[:, 0]), b[:], ALU.mult).then_inc(step_done, 1)
                if here(dve, "bias", j):
                    dve.tensor_single_scalar(a[:], a[:], c.bias0[:], ALU.add).then_inc(step_done, 1)
                if here(dve, "degree", j):
                    dve.tensor_single_scalar(b[:], at(c.rel[:, 1]), 1.0, ALU.max).then_inc(step_done, 1)
                if here(dve, "inverse", j):
                    dve.reciprocal(b[:], b[:]).then_inc(step_done, 1)
                if here(dve, "has_in", j):
                    dve.tensor_single_scalar(m[:], at(c.rel[:, 1]), 1.0, ALU.min).then_inc(step_done, 1)
                if here(dve, "sum", j):
                    wait_count(dve, tab_mm, j * CB)
                    dve.tensor_tensor(halves(a), banks(pa), halves(at(c.num[:, 0])), ALU.add)\
                       .then_inc(step_done, 1)
                if here(dve, "scaled", j):
                    dve.tensor_tensor(a[:], a[:], b[:], ALU.mult).then_inc(step_done, 1)
                if here(dve, "self_l", j):
                    dve.tensor_tensor(halves(d), banks(pb), halves(m), ALU.mult).then_inc(step_done, 1)
                if here(dve, "add_l", j):
                    dve.tensor_tensor(a[:], a[:], d[:], ALU.add).then_inc(step_done, 1)
                if here(dve, "no_in", j):
                    dve.tensor_scalar(m[:], m[:], -1.0, 1.0, ALU.mult, ALU.add).then_inc(step_done, 1)
                if here(dve, "self_a", j):
                    dve.tensor_tensor(halves(d), banks(pc), halves(m), ALU.mult).then_inc(step_done, 1)
                if here(dve, "add_a", j):
                    dve.tensor_tensor(a[:], a[:], d[:], ALU.add).then_inc(step_done, 1)
                if here(dve, "rrelu", j):
                    dve.scalar_tensor_tensor(a[:], a[:], RRELU, a[:], ALU.mult, ALU.max).then_inc(step_done, 1)
                for t in "ab":
                    if t == "b" and here(dve, "residual", j):
                        if stage == "gat":
                            dve.scalar_tensor_tensor(a[:], a[:], -1.0, at(c.x), ALU.add, ALU.add)\
                               .then_inc(step_done, 1)
                        elif stage == "dot":
                            dve.scalar_tensor_tensor(a[:], a[:], c.bias2[:], at(c.x), ALU.add, ALU.add)\
                               .then_inc(step_done, 1)
                        else:
                            dve.tensor_tensor(a[:], a[:], at(c.x), ALU.add).then_inc(step_done, 1)
                    if here(dve, f"{t}_center", j):
                        dve.tensor_tensor(halves(d), halves(a), banks(pa), ALU.subtract).then_inc(step_done, 1)
                    if here(dve, f"{t}_rstd", j):
                        dve.reciprocal(s[:], s[:]).then_inc(step_done, 1)
                    if here(dve, f"{t}_norm", j):
                        dve.tensor_tensor(a[:], d[:], s[:], ALU.mult).then_inc(step_done, 1)
                    if t == "a" and here(dve, "affine", j):
                        dve.tensor_scalar(a[:], a[:], c.gamma[:], c.beta[:], ALU.mult, ALU.add)\
                           .then_inc(step_done, 1)
                    if t == "a" and here(dve, "negative", j):
                        dve.tensor_single_scalar(b[:], a[:], 0.0, ALU.min).then_inc(step_done, 1)
                    if t == "a" and here(dve, "elu", j):
                        dve.scalar_tensor_tensor(a[:], a[:], 0.0, b[:], ALU.max, ALU.add).then_inc(step_done, 1)
                here(dve, "keep", j)
                if keep_in is not None:
                    dve.tensor_single_scalar(at(keep_in), a[:], 1.0, ALU.mult).then_inc(step_done, 1)
                else:
                    dve.nop().then_inc(step_done, 1)
            run(dve, body)

        @block.gpsimd
        def _(pool):
            if stage == "load":
                pool.wait_ge(step_done, (CS - 2) * per_j + order["turn"] + 1)
                pool.memset(x_rows[:], 0.0).then_inc(x_zero, 1)


def build(nc, x, src, dst, etype, weights, out):
    class Memory:
        pass

    c = Memory()
    dram = lambda name, shape: nc.dram_tensor(name, shape, F32, kind="Internal").ap()
    sorted_dst, sorted_src = dram("sorted_dst", (POS, 4)), dram("sorted_src", (POS, 4))
    runs_dst, runs_src = dram("runs_dst", (2, POS)), dram("runs_src", (2, POS))
    tab0, tab1, tab2 = dram("tab0", (NP, D)), dram("tab1", (NP, D + 4)), dram("tab2", (NP, 2 * D))
    tab3, tab4 = dram("tab3", (NP, D)), dram("tab4", (NP, D))
    c.win0, c.win1, c.win2 = dram("win0", (NW, D)), dram("win1", (NW, 4)), dram("win2", (NW, D))
    with ExitStack() as st:
        kit = Kit(nc, st)
        c.pool_dma = [kit.sem(f"pool_dma{i}") for i in range(RING)]
        c.pool_count = [0] * RING
        c.ident, c.ones, c.mean_w = kit.sb("ident", [P, P]), kit.sb("ones", [P, P]), kit.sb("mean_w", [P, P])
        c.identb = kit.sb("identb", [P, P], BF16)
        c.before, c.after, c.first_row = (kit.sb(n, [P, P]) for n in ("before", "after", "first_row"))
        c.hsel4, c.hsel8 = kit.sb("hsel4", [4, P]), kit.sb("hsel8", [8, P])
        c.fence = kit.sb("fence", [1, 1])
        c.one_row, c.eps = kit.sb("one_row", [1, P]), kit.sb("eps", [P, 1])
        c.iota_f, c.iota_b, c.node_id = kit.sb("iota_f", [P, P]), kit.sb("iota_b", [P, P], BF16), kit.sb("node_id", [P, NT])
        c.w0, c.b0 = kit.sb("w0", [P, 2 * D]), kit.sb("b0", [1, 2 * D])
        c.w1 = kit.sb("w1", [P, D + 8])
        c.w2, c.b2 = kit.sb("w2", [P, 3 * D]), kit.sb("b2", [1, 3 * D])
        c.wn, c.wl, c.wa = (kit.sb(n, [P, 2, D]) for n in ("wn", "wl", "wa"))
        c.bias0, c.gamma, c.beta, c.bias2 = (kit.sb(n, [P, 1]) for n in ("bias0", "gamma", "beta", "bias2"))
        c.att = kit.sb("att", [P, D])
        lists = {}
        for n in ("dst", "src"):
            lists[n] = (kit.sb(f"slot_{n}", [P, T]), kit.sb(f"real_slot_{n}", [P, T]),
                        kit.sb(f"first_{n}", [1, T], I32), kit.sb(f"neighbour_{n}", [P, T], I32))
        etype_at = kit.sb("etype_at", [P, T], I32)
        constants(nc, c)
        load_weights(nc, c, weights)
        with ExitStack() as sort_scope:
            edge_kit = Kit(nc, sort_scope)
            c.edge = edge_kit.sb("edge", [ET, 3, UT])
            c.low, c.high = edge_kit.sb("low", [ET, 2, UT]), edge_kit.sb("high", [ET, 2, UT])
            edge_columns(nc, c, src, dst, etype)
            counting_sort(nc, c, 1, dst, sorted_dst)
            counting_sort(nc, c, 0, src, sorted_src)
        for n, rows, runs in (("dst", sorted_dst, runs_dst), ("src", sorted_src, runs_src)):
            slot, real_slot, first, neighbour = lists[n]
            read_sorted(nc, c, n, rows, runs, slot, real_slot, first, neighbour,
                        etype_at if n == "dst" else None)
        x_at = kit.sb("x_at", [P, NP])
        num = kit.sb("num", [P, 2, NW])
        c.x, c.num = x_at[:], num[:]
        slot_d, real_d, first_d, nb_d = lists["dst"]
        slot_s, real_s, first_s, nb_s = lists["src"]
        node_step(nc, c, "load", c.w0[:], c.b0, [], [(tab0, 0, D), (c.win0, D, 2 * D)], x_dram=x, keep_in=c.x)
        attention_pass(nc, c, "l0", 4, False, tab0, c.win0, runs_dst, slot_d, first_d, nb_d)
        node_step(nc, c, "gat", c.w1[:], None, [], [(tab1, 0, D + 4), (c.win1, D + 4, D + 8)], keep_in=c.x)
        edge_score_pass(nc, c, tab1, c.win1, slot_s, real_s, first_s, nb_s)
        node_step(nc, c, "edge", c.w2[:], c.b2, [(0, D), (2 * D, 3 * D)], [(tab2, 0, 2 * D), (c.win2, 2 * D, 3 * D)],
                  keep_in=c.x)
        attention_pass(nc, c, "l2", 8, True, tab2, c.win2, runs_src, slot_s, first_s, nb_s)
        node_step(nc, c, "dot", c.wn[:, 0], None, [], [(tab3, 0, D)], keep_in=c.x)
        rel = kit.sb("rel", [P, 2, NW])
        c.rel, c.hidden = rel[:], c.num[:, 1]
        sum_pass(nc, c, "rel", weights["L3_gnn_rel_emb"], real_d, first_d, etype_at, c.rel, True)
        sum_pass(nc, c, "l3a", tab3, real_d, first_d, nb_d, c.num, False)
        node_step(nc, c, "rel0", c.wn[:, 1], None, [], [(tab4, 0, D)], layer=0, keep_in=c.hidden)
        sum_pass(nc, c, "l3b", tab4, real_d, first_d, nb_d, c.num, False)
        node_step(nc, c, "rel1", c.ident[:], None, [], [(out, 0, D)], layer=1)


_INS = ["x", "src", "dst", "edge_type_200", "L0_gnn_W_l", "L0_gnn_b_l", "L0_gnn_W_r", "L0_gnn_b_r", "L0_gnn_att",
        "L0_gnn_bias", "L0_gnn_gamma", "L0_gnn_beta", "L1_gnn_kernel", "L1_gnn_kernel_attention",
        "L2_gnn_query_kernel", "L2_gnn_query_bias", "L2_gnn_key_kernel", "L2_gnn_key_bias", "L2_gnn_kernel",
        "L2_gnn_bias", "L3_gnn_rel_emb", "L3_gnn_Wn", "L3_gnn_Wl", "L3_gnn_Wa"]


def kernel(**inputs):
    import concourse.bacc as _bacc
    from concourse.bass_utils import run_bass_kernel_spmd as _run

    nc = _bacc.Bacc("TRN2", target_bir_lowering=False, num_devices=1)
    arrays, aps = {}, {}
    for name in _INS:
        a = np.ascontiguousarray(inputs[name])
        arrays[f"in_{name}_dram"] = a
        aps[name] = nc.dram_tensor(f"in_{name}_dram", a.shape, mybir.dt.from_np(a.dtype), kind="ExternalInput").ap()
    out = nc.dram_tensor("out_0_dram", (N, D), F32, kind="ExternalOutput").ap()
    build(nc, aps["x"], aps["src"], aps["dst"], aps["edge_type_200"], aps, out)
    r = _run(nc, [arrays], core_ids=[0])
    return r.results[0]["out_0_dram"]
```

```python
from contextlib import ExitStack

import numpy as np
import concourse.bass as bass
from concourse import mybir

F32 = mybir.dt.float32
BF16 = mybir.dt.bfloat16
I32 = mybir.dt.int32
ALU = mybir.AluOpType
ACT = mybir.ActivationFunctionType
AX = mybir.AxisListType

P = 128
N, E, D = 6250, 100000, 128
NT = -(-N // P)
NP = NT * P
NW = NP + P
ET = 125
UT = E // ET
UG = 8
US = UT // UG
G = 4
RING = 6
T = -(-(E + NP) // (P * G * RING)) * G * RING
GROUPS = T // G
POS = T * P
PADS = POS - E - NP
TB = T // 8
NBLK = T // TB
PR = 12
BIG = 1e30
LEAK = 0.2
RRELU = (1.0 / 8.0 + 1.0 / 3.0) / 2.0
LN_EPS = 1e-5
RELS = 200
CB = 7
CW = CB * P
CS = NP // CW
HW = CW // 2


def replicate(ap, dim, count):
    a = ap.unsqueeze(dim)
    shape = list(a.shape)
    shape[dim] = count
    return a.to_broadcast(shape)


class Kit:

    def __init__(self, nc, stack):
        self.nc, self.stack, self.sems = nc, stack, 0

    def sb(self, name, shape, dt=F32):
        return self.stack.enter_context(self.nc.sbuf_tensor(name, shape, dt))

    def ps(self, name, shape, dt=F32):
        size = int(np.prod(shape[1:]))
        bank = 512 if dt == F32 else 1024
        t = self.stack.enter_context(self.nc.psum_tensor(name, [shape[0], -(-size // bank) * bank], dt))
        letters = "abcd"[:len(shape) - 1]
        sizes = {x: n for x, n in zip(letters[1:], shape[2:])}
        return t[:, 0:size].rearrange(f"p ({' '.join(letters)}) -> p {' '.join(letters)}", **sizes)

    def sem(self, name):
        if not self.sems:
            self.stack.callback(self.nc.all_engine_barrier)
        self.sems += 1
        sem = self.stack.enter_context(self.nc.semaphore(name))
        self.stack.callback(self.nc.sync.sem_clear, sem)
        return sem


def staggered(eng, emit, lag, ahead=0):
    turns = GROUPS // RING - ahead
    for k in range(-ahead, RING):
        emit(k, k % RING)
    with eng.Fori(1, turns) as m:
        for q in range(RING):
            emit(m * RING + q, q)
    for k in range(turns * RING, GROUPS + lag):
        emit(k, k % RING)


def in_pairs(eng, body):
    body(0)
    with eng.Fori(1, US // 2) as m:
        body(m)


def inside_steps(s, lag):
    return not isinstance(s, int) or 0 <= s - lag < US


def inside(k, lag):
    return not isinstance(k, int) or 0 <= k - lag < GROUPS


def wait_count(eng, sem, value):
    if not isinstance(value, int) or value > 0:
        eng.wait_ge(sem, value)


def turn(k, lag=0):
    return (k - lag) // RING


def turn2(k, lag=0):
    return (k - lag) // 2


def constants(nc, c):
    with ExitStack() as st:
        kit = Kit(nc, st)
        cst_done, cst_int, cst_cast = kit.sem("cst_done"), kit.sem("cst_int"), kit.sem("cst_cast")
        io = kit.sb("iota_int", [P, 2 * P], I32)
        nodes = kit.sb("nodes_int", [P, NT], I32)
        block = st.enter_context(nc.Block())

        @block.gpsimd
        def _(pool):
            n = 0
            for t, v in ((c.ident, 0.0), (c.identb, 0.0), (c.ones, 1.0), (c.mean_w, 1.0 / D),
                         (c.before, 1.0), (c.after, 1.0), (c.first_row, 0.0), (c.hsel4, 1.0), (c.hsel8, 1.0),
                         (c.one_row, 1.0), (c.eps, LN_EPS)):
                pool.memset(t[:], v).then_inc(cst_done, 1)
                n += 1
            pool.iota(io[:], pattern=[[1, 2 * P]], base=0, channel_multiplier=0).then_inc(cst_int, 1)
            pool.iota(nodes[:], pattern=[[P, NT]], base=0, channel_multiplier=1).then_inc(cst_int, 1)
            pool.wait_ge(cst_done, n)
            for t in (c.ident, c.identb):
                pool.affine_select(out=t[:], in_=t[:], compare_op=ALU.not_equal, fill=1.0, base=0,
                                   pattern=[[-1, P]], channel_multiplier=1).then_inc(cst_done, 1)
            pool.affine_select(out=c.before[:], in_=c.before[:], compare_op=ALU.is_gt, fill=0.0, base=0,
                               pattern=[[1, P]], channel_multiplier=-1).then_inc(cst_done, 1)
            pool.affine_select(out=c.after[:], in_=c.after[:], compare_op=ALU.is_gt, fill=0.0, base=0,
                               pattern=[[-1, P]], channel_multiplier=1).then_inc(cst_done, 1)
            pool.affine_select(out=c.first_row[:], in_=c.first_row[:], compare_op=ALU.not_equal, fill=1.0,
                               base=0, pattern=[[0, P]], channel_multiplier=1).then_inc(cst_done, 1)
            for t, heads in ((c.hsel4, 4), (c.hsel8, 8)):
                w = D // heads
                pool.affine_select(out=t[:], in_=t[:], compare_op=ALU.is_ge, fill=0.0, base=0,
                                   pattern=[[1, P]], channel_multiplier=-w).then_inc(cst_done, 1)
                n += 1
                pool.wait_ge(cst_done, n + 5)
                pool.affine_select(out=t[:], in_=t[:], compare_op=ALU.is_ge, fill=0.0, base=w - 1,
                                   pattern=[[-1, P]], channel_multiplier=w).then_inc(cst_done, 1)
                n += 1

        @block.vector
        def _(dve):
            dve.wait_ge(cst_int, 2)
            dve.tensor_copy(c.type_iota[:], io[:]).then_inc(cst_cast, 1)
            dve.tensor_copy(c.iota_b[:], io[:, 0:P]).then_inc(cst_cast, 1)
            dve.tensor_copy(c.node_id[:], nodes[:]).then_inc(cst_cast, 1)


def edge_columns(nc, c, src, dst, etype):
    with ExitStack() as st:
        kit = Kit(nc, st)
        rows = kit.sb("edge_rows", [100, 3, UG, ET], I32)
        rows_f = kit.sb("edge_rows_f", [100, 3, UG, ET])
        cols_i = kit.sb("edge_cols_i", [ET, 2, UT], I32)
        part_i = kit.sb("edge_part_i", [ET, 2, UT], I32)
        ps = [kit.ps(f"edge_ps{i}", [ET, UG // 2, P]) for i in range(6)]
        loaded, floated, turned, copied = (kit.sem(n) for n in
                                           ("edges_loaded", "edges_floated", "edges_turned", "edges_copied"))
        block = st.enter_context(nc.Block())

        @block.sync
        def _(sp):
            for f, a in enumerate((src, dst, etype)):
                sp.dma_start(rows[:, f], a.rearrange("(b t j) -> t b j", b=UG, j=ET)).then_inc(loaded, 16)

        @block.tensor
        def _(pe):
            pe.wait_ge(floated, 1)
            for f in range(3):
                for b in range(UG):
                    mm = pe.transpose(ps[2 * f + b // 4][:, b % 4, 0:100], rows_f[:, f, b, :],
                                      c.ident[0:100, 0:100])
            mm.then_inc(turned, 1)

        @block.vector
        def _(dve):
            dve.wait_ge(loaded, 48)
            dve.tensor_copy(rows_f[:], rows[:]).then_inc(floated, 1)
            dve.wait_ge(turned, 1)
            for f in range(3):
                for h in range(2):
                    cols = c.edge[:, f, 400 * h:400 * h + 400].rearrange("p (b t) -> p b t", b=4)
                    dve.tensor_copy(cols, ps[2 * f + h][:, :, 0:100]).then_inc(copied, 1)
            dve.wait_ge(copied, 6)
            dve.tensor_copy(cols_i[:], c.edge[:, 0:2, :]).then_inc(copied, 1)
            dve.wait_ge(copied, 7)
            dve.tensor_single_scalar(part_i[:], cols_i[:], 7, ALU.arith_shift_right).then_inc(copied, 1)
            dve.wait_ge(copied, 8)
            dve.tensor_copy(c.high[:], part_i[:]).then_inc(copied, 1)
            dve.wait_ge(copied, 9)
            dve.tensor_single_scalar(part_i[:], cols_i[:], P - 1, ALU.bitwise_and).then_inc(copied, 1)
            dve.wait_ge(copied, 10)
            dve.tensor_copy(c.low[:], part_i[:]).then_inc(copied, 1)


def counting_sorts(nc, c, key_dram, sorted_rows):
    KEYS = range(2)
    with ExitStack() as st:
        kit = Kit(nc, st)
        lo = kit.sb("lo", [ET, 2, UG, P], BF16)
        hi = kit.sb("hi", [ET, 2, UG, NT], BF16)
        zero_lo = kit.sb("zero_lo", [ET, P], BF16)
        lo_t = kit.sb("lo_t", [P, 2, UG, ET])
        key_row = kit.sb("key_row", [ET, 2, UG, ET], I32)
        table = kit.sb("table", [P, 2, UG + 1, NT])
        count, ahead, total, begin = (kit.sb(n, [P, 2, NT]) for n in ("count", "ahead", "total", "begin"))
        begin_i = kit.sb("begin_i", [P, 2, NT], I32)
        self_row = kit.sb("self_row", [P, NT, 4])
        pad_row = kit.sb("pad_row", [PADS // PR, PR, 4])
        payload = kit.sb("payload", [ET, 2, UT, 4])
        staged = kit.sb("staged", [ET, 2, UG, 4])
        same = kit.sb("same", [ET, 2, UG, ET])
        ranked = kit.sb("ranked", [ET, 2, UG, ET])
        picked = kit.sb("picked", [ET, 2, UG, NT])
        rank, base = kit.sb("rank", [ET, 2, UG]), kit.sb("base", [ET, 2, UG])
        position = kit.sb("position", [ET, 2, UG], I32)
        zero_nt = kit.sb("zero_nt", [P, NT])
        ps_count = kit.ps("ps_count", [P, NT])
        ps_pre = kit.ps("ps_pre", [P, 2, NT])
        ps_hist = [kit.ps(f"ps_hist{k}", [P, UG, NT]) for k in KEYS]
        ps_lo_t = [kit.ps(f"ps_lo_t{k}", [P, UG, P], BF16) for k in KEYS]
        ps_base = [kit.ps(f"ps_base{k}", [ET, UG, NT]) for k in KEYS]
        prep, zeroed, onehot, counted, off, prefixed, begun, chain, pay_done, fenced = (
            kit.sem(f"sort_{n}") for n in
            ("prep", "zeroed", "onehot", "counted", "off", "prefixed", "begun", "chain", "pay_done", "fenced"))
        (onehot2, same_done, hist_done, turned, turn_copied, table_done, base_done, rank_done, pos_done,
         pick_done, carry_done, stage_done, row_in) = (
            [kit.sem(f"sort_{n}{k}") for k in KEYS] for n in
            ("onehot2", "same_done", "hist_done", "turned", "turn_copied", "table_done", "base_done",
             "rank_done", "pos_done", "pick_done", "carry_done", "stage_done", "row_in"))
        *sent, self_sent = c.pool_dma[0:3]
        before = list(c.pool_count)
        keys_by_step = [k.rearrange("(s n) -> s n", s=US) for k in key_dram]
        block = st.enter_context(nc.Block())

        def one_hots(dve, key, s, b, sem):
            low = c.low[:, key, bass.ds(s * UG, UG)]
            high = c.high[:, key, bass.ds(s * UG, UG)]
            dve.tensor_tensor(lo[:, b], replicate(low, 2, P), replicate(c.iota_b[0:ET, :], 1, UG),
                              ALU.is_equal).then_inc(sem, 1)
            dve.tensor_tensor(hi[:, b], replicate(high, 2, NT), replicate(c.iota_b[0:ET, 0:NT], 1, UG),
                              ALU.is_equal).then_inc(sem, 1)

        def edge_steps(eng, body, lag):
            body(0)
            with eng.Fori(1, US) as s:
                body(s)
            for s in range(US, US + lag):
                body(s)

        @block.vector
        def _(dve):
            dve.memset(zero_lo[:], 0.0).then_inc(zeroed, 1)
            dve.memset(zero_nt[:], 0.0).then_inc(zeroed, 1)
            for key in KEYS:
                def two_steps(m):
                    for b in range(2):
                        wait_count(dve, counted, key * (US + 1) + m * 2 + b)
                        one_hots(dve, key, m * 2 + b, b, onehot)
                in_pairs(dve, two_steps)
                dve.wait_ge(counted, (key + 1) * (US + 1))
                dve.tensor_single_scalar(count[:, key], ps_count, 1.0, ALU.add).then_inc(off, 1)
                dve.wait_ge(prefixed, key + 1)
                dve.tensor_copy(ahead[:, key], ps_pre[:, 0]).then_inc(chain, 1)
                dve.tensor_copy(total[:, key], ps_pre[:, 1]).then_inc(chain, 1)
                dve.wait_ge(zeroed, 2)
                dve.wait_ge(chain, key * 6 + 2)
                dve.tensor_tensor_scan(begin[:, key], total[:, key], zero_nt[:], 0.0, ALU.add, ALU.add)\
                   .then_inc(chain, 1)
                dve.wait_ge(chain, key * 6 + 3)
                dve.tensor_tensor(begin[:, key], begin[:, key], total[:, key], ALU.subtract).then_inc(chain, 1)
                dve.wait_ge(chain, key * 6 + 4)
                dve.tensor_tensor(begin[:, key], begin[:, key], ahead[:, key], ALU.add).then_inc(chain, 1)
                dve.wait_ge(chain, key * 6 + 5)
                dve.tensor_copy(begin_i[:, key], begin[:, key]).then_inc(begun, 1)
                dve.tensor_single_scalar(table[:, key, 0], begin[:, key], 1.0, ALU.add).then_inc(chain, 1)
            dve.wait_ge(chain, 12)

            def rank_and_table(key, s):
                dve.wait_ge(row_in[key], s * 16 + 16)
                keys = c.edge[:, key, bass.ds(s * UG, UG)]
                dve.tensor_tensor(same[:, key], key_row[:, key], replicate(keys, 2, ET), ALU.is_equal)\
                   .then_inc(same_done[key], 1)
                one_hots(dve, key, s, key, onehot2[key])
                dve.wait_ge(same_done[key], s + 1)
                dve.tensor_tensor(ranked[:, key], same[:, key], replicate(c.after[0:ET, 0:ET], 1, UG),
                                  ALU.mult).then_inc(rank_done[key], 1)
                dve.wait_ge(hist_done[key], s + 1)
                wait_count(dve, carry_done[key], s)
                dve.tensor_tensor(table[:, key, 1:], replicate(table[:, key, 0], 1, UG), ps_hist[key],
                                  ALU.add).then_inc(table_done[key], 1)
                dve.wait_ge(rank_done[key], s * 2 + 1)
                dve.tensor_reduce(rank[:, key], ranked[:, key], AX.X, ALU.add).then_inc(rank_done[key], 1)

            def positions(key, s):
                dve.wait_ge(base_done[key], s + 1)
                dve.tensor_tensor(picked[:, key], ps_base[key], hi[:, key], ALU.mult).then_inc(pick_done[key], 1)
                dve.tensor_copy(table[:, key, 0], table[:, key, UG]).then_inc(carry_done[key], 1)
                dve.wait_ge(pick_done[key], s * 2 + 1)
                dve.tensor_reduce(base[:, key], picked[:, key], AX.X, ALU.add).then_inc(pick_done[key], 1)
                wait_count(dve, sent[key], before[key] + s * (16 * UG))
                dve.wait_ge(rank_done[key], s * 2 + 2)
                dve.wait_ge(pick_done[key], s * 2 + 2)
                dve.tensor_tensor(position[:, key], base[:, key], rank[:, key], ALU.add)\
                   .then_inc(pos_done[key], 1)

            def step(s):
                now, lagging = inside_steps(s, 0), inside_steps(s, 1)
                if now:
                    rank_and_table(0, s)
                if lagging:
                    positions(1, s - 1)
                if now:
                    rank_and_table(1, s)
                    positions(0, s)
            edge_steps(dve, step, 1)

        @block.tensor
        def _(pe):
            pe.wait_ge(zeroed, 1)
            for key in KEYS:
                if key:
                    pe.wait_ge(off, key)
                pe.matmul(ps_count, zero_lo[:], zero_lo[:, 0:NT], start=True, stop=False,
                          skip_group_check=True).then_inc(counted, 1)
                def two_steps(m):
                    for b in range(2):
                        pe.wait_ge(onehot, key * 2 * US + (m * 2 + b) * 2 + 2)
                        for g in range(UG):
                            mm = pe.matmul(ps_count, lo[:, b, g], hi[:, b, g], start=False, stop=False,
                                           skip_group_check=True)
                        mm.then_inc(counted, 1)
                in_pairs(pe, two_steps)
                pe.wait_ge(off, key + 1)
                if key:
                    pe.wait_ge(chain, 2)
                pe.matmul(ps_pre[:, 0], c.before[:], count[:, key], start=True, stop=True)
                pe.matmul(ps_pre[:, 1], c.ones[:], count[:, key], start=True, stop=True).then_inc(prefixed, 1)

            def step(s):
                for key in KEYS:
                    pe.wait_ge(onehot2[key], s * 2 + 2)
                    for g in range(UG):
                        mm = pe.transpose(ps_lo_t[key][:, g, 0:ET], lo[:, key, g], c.identb[0:ET, 0:ET])
                    mm.then_inc(turned[key], 1)
                    for g in range(UG):
                        for r in range(g + 1):
                            mm = pe.matmul(ps_hist[key][:, g], lo[:, key, r], hi[:, key, r],
                                           start=r == 0, stop=r == g)
                    mm.then_inc(hist_done[key], 1)
                    pe.wait_ge(turn_copied[key], s + 1)
                    pe.wait_ge(table_done[key], s + 1)
                    for g in range(UG):
                        mm = pe.matmul(ps_base[key][:, g], lo_t[:, key, g], table[:, key, g],
                                       start=True, stop=True)
                    mm.then_inc(base_done[key], 1)
            edge_steps(pe, step, 0)

        @block.scalar
        def _(act):
            for key in KEYS:
                act.activation(payload[:, key, :, 0], c.edge[:, 1 - key, :], ACT.Copy).then_inc(pay_done, 1)
                act.activation(payload[:, key, :, 1], c.edge[:, key, :], ACT.Copy).then_inc(pay_done, 1)
                act.activation(payload[:, key, :, 2], c.edge[:, 2, :], ACT.Copy).then_inc(pay_done, 1)
            act.wait_ge(pay_done, 6)
            act.wait_ge(prep, 6)

            def step(s):
                for key in KEYS:
                    act.wait_ge(turned[key], s + 1)
                    act.activation(lo_t[:, key], ps_lo_t[key][:, :, 0:ET], ACT.Copy).then_inc(turn_copied[key], 1)
                    wait_count(act, sent[key], before[key] + s * (16 * UG))
                    act.activation(staged[:, key], payload[:, key, bass.ds(s * UG, UG), :], ACT.Copy)\
                       .then_inc(stage_done[key], 1)
            edge_steps(act, step, 0)

        @block.sync
        def _(sp):
            def step(s):
                for key in KEYS:
                    wait_count(sp, same_done[key], s)
                    row = keys_by_step[key][bass.ds(s, 1), :].to_broadcast([ET, UG * ET])
                    sp.dma_start(key_row[:, key].rearrange("p g j -> p (g j)"), row).then_inc(row_in[key], 16)
            edge_steps(sp, step, 0)

        @block.gpsimd
        def _(pool):
            pool.memset(payload[:, :, :, 3], 1.0).then_inc(prep, 1)
            pool.tensor_copy(self_row[:, :, 0], c.node_id[:]).then_inc(prep, 1)
            pool.tensor_copy(self_row[:, :, 1], c.node_id[:]).then_inc(prep, 1)
            pool.memset(self_row[:, :, 2:4], 0.0).then_inc(prep, 1)
            pool.memset(pad_row[:, :, 0:2], float(NP - 1)).then_inc(prep, 1)
            pool.memset(pad_row[:, :, 2:4], 0.0).then_inc(prep, 1)
            pool.wait_ge(prep, 6)
            for key in KEYS:
                pool.dma_start(sorted_rows[key][E + NP:POS, :].rearrange("(p n) f -> p (n f)", n=PR),
                               pad_row[:].rearrange("p n f -> p (n f)")).then_inc(self_sent, 16)
            for key in KEYS:
                pool.wait_ge(begun, key + 1)
                for i in range(NT):
                    pool.indirect_dma_start(sorted_rows[key],
                                            bass.IndirectOffsetOnAxis(ap=begin_i[:, key, i:i + 1], axis=0),
                                            self_row[:, i, :], None).then_inc(self_sent, 16)

            def step(s):
                for key in KEYS:
                    pool.wait_ge(stage_done[key], s + 1)
                    wait_count(pool, fenced, s * 2 + key)
                    pool.wait_ge(pos_done[key], s + 1)
                    pool.tensor_tensor(c.fence[:], c.ones[0:1, 0:1], c.ones[0:1, 0:1], ALU.add)\
                        .then_inc(fenced, 1)
                    for g in range(UG):
                        pool.indirect_dma_start(
                            sorted_rows[key], bass.IndirectOffsetOnAxis(ap=position[:, key, g:g + 1], axis=0),
                            staged[:, key, g, :], None).then_inc(sent[key], 16)
            edge_steps(pool, step, 0)
            pool.wait_ge(self_sent, before[2] + 2 * 16 * (NT + 1))
            for key in KEYS:
                pool.wait_ge(sent[key], before[key] + 16 * UG * US)
        c.pool_count[0:3] = [before[0] + 16 * UG * US, before[1] + 16 * UG * US, before[2] + 2 * 16 * (NT + 1)]


def read_sorted(nc, c, name, sorted_rows, runs, slot, real_slot, first, neighbour, etype):
    with ExitStack() as st:
        kit = Kit(nc, st)
        rows = kit.sb(f"{name}_rows", [TB, NBLK, P, 4])
        start = kit.sb(f"{name}_start", [TB, NBLK, 2, P])
        cols = kit.sb(f"{name}_cols", [P, 4, T])
        tmp = kit.sb(f"{name}_tmp", [P, T])
        ps = [kit.ps(f"{name}_ps{i}", [P, 4, P]) for i in range(2)]
        ps_first = [kit.ps(f"{name}_ps_first{i}", [P, T // 2]) for i in range(2)]
        loaded, turned, copied, step, stored = (kit.sem(f"{name}_back_{n}") for n in
                                                ("loaded", "turned", "copied", "step", "stored"))
        block = st.enter_context(nc.Block())
        n_steps = 8 + (etype is not None)

        @block.sync
        def _(sp):
            view = sorted_rows.rearrange("(b t p) f -> t b (p f)", t=TB, p=P)
            sp.dma_start(rows[:].rearrange("t b p f -> t b (p f)"), view).then_inc(loaded, 16)
            sp.wait_ge(step, 3)
            for kind in range(2):
                view = runs[kind].rearrange("(b t p) -> t b p", t=TB, p=P)
                sp.dma_start(view, start[:, :, kind, :]).then_inc(stored, 16)
            sp.wait_ge(stored, 32)

        @block.tensor
        def _(pe):
            pe.wait_ge(loaded, 16)
            for b in range(NBLK):
                if b >= 2:
                    pe.wait_ge(copied, b - 1)
                for f in range(4):
                    mm = pe.transpose(ps[b % 2][:, f, 0:TB], rows[:, b, :, f], c.ident[0:TB, 0:TB])
                mm.then_inc(turned, 1)
            pe.wait_ge(copied, NBLK)
            for h in range(2):
                mm = pe.matmul(ps_first[h][:], c.first_row[:], cols[:, 1, h * (T // 2):(h + 1) * (T // 2)],
                               start=True, stop=True)
            mm.then_inc(turned, 1)

        @block.scalar
        def _(act):
            for b in range(NBLK):
                act.wait_ge(turned, b + 1)
                act.activation(cols[:, :, b * TB:(b + 1) * TB], ps[b % 2][:, :, 0:TB], ACT.Copy)\
                   .then_inc(copied, 1)

        @block.vector
        def _(dve):
            dve.wait_ge(loaded, 16)
            dve.tensor_scalar(start[:, :, 0, :], rows[:, :, :, 3], BIG, BIG, ALU.mult, ALU.subtract)\
               .then_inc(step, 1)
            dve.memset(start[:, :, 1, P - 1:P], -BIG).then_inc(step, 1)
            dve.tensor_scalar(start[:, :, 1, 0:P - 1], rows[:, :, 1:P, 3], BIG, BIG, ALU.mult, ALU.subtract)\
               .then_inc(step, 1)
            dve.wait_ge(turned, NBLK + 1)
            for h in range(2):
                part = slice(h * (T // 2), (h + 1) * (T // 2))
                dve.tensor_tensor(slot[:, part], cols[:, 1, part], ps_first[h][:], ALU.subtract)\
                   .then_inc(step, 1)
            dve.wait_ge(step, 5)
            dve.tensor_single_scalar(tmp[:], slot[:], 1.0, ALU.add).then_inc(step, 1)
            dve.wait_ge(step, 6)
            dve.tensor_tensor(tmp[:], tmp[:], cols[:, 3, :], ALU.mult).then_inc(step, 1)
            dve.wait_ge(step, 7)
            dve.tensor_single_scalar(real_slot[:], tmp[:], -1.0, ALU.add).then_inc(step, 1)
            dve.tensor_copy(neighbour[:], cols[:, 0, :]).then_inc(step, 1)
            dve.tensor_copy(first[:], cols[0:1, 1, :]).then_inc(step, 1)
            if etype is not None:
                dve.tensor_copy(etype[:], cols[:, 2, :]).then_inc(step, 1)


def gather_rows(pool, c, k, q, slots, table, index, rows, staged, fenced, used, landed, landed_before,
                per_group=1):
    half = RING // 2
    if q % half == 0:
        for r in range(q, q + half):
            wait_count(pool, landed[r], landed_before[r] + turn(k) * (16 * G))
        pool.tensor_copy(slots[:, q * G:(q + half) * G], index[:, bass.ds(k * G, half * G)]).then_inc(staged, 1)
        pool.wait_ge(staged, k // half + 1)
    wait_count(pool, used, (k - RING + 1) * per_group)
    wait_count(pool, fenced, k)
    pool.tensor_tensor(c.fence[:], c.ones[0:1, 0:1], c.ones[0:1, 0:1], ALU.add).then_inc(fenced, 1)
    for g in range(G):
        pool.indirect_dma_start(rows[:, q, g, :], None, table,
                                bass.IndirectOffsetOnAxis(ap=slots[:, q * G + g:q * G + g + 1], axis=0))\
            .then_inc(landed[q], 16)


def window_starts(nc, engine, first, k):
    return nc.values_load_multi_w_load_instructions(first[0:1, bass.ds(k * G, G)], engines=[engine],
                                                    min_val=0, max_val=NP - 1)[1]


def attention_pass(nc, c, name, heads, dot, table, window_table, runs, slot, first, index):
    width = D // heads
    rw = 2 * D if dot else D
    v0 = rw - D
    engine = mybir.EngineType
    with ExitStack() as st:
        kit = Kit(nc, st)
        slots = kit.sb(f"{name}_slots", [P, RING * G], I32)
        rows = kit.sb(f"{name}_rows", [P, RING, G, rw])
        win = kit.sb(f"{name}_win", [P, 2, G, D])
        run = kit.sb(f"{name}_run", [heads, 2, 2, G * P])
        sel = kit.sb(f"{name}_sel", [P, RING, G, P])
        sel_t = kit.sb(f"{name}_sel_t", [P, 2, G, P])
        z = kit.sb(f"{name}_z", [P, 2, G, D])
        score = kit.sb(f"{name}_score", [P, 2, G, heads])
        prefix = kit.sb(f"{name}_prefix", [heads, 2, G * P])
        top = kit.sb(f"{name}_top", [heads, 2, G * P])
        drop = kit.sb(f"{name}_drop", [heads, 2, G])
        less = kit.sb(f"{name}_less", [P, 2, G, heads])
        weight = kit.sb(f"{name}_weight", [P, 2, G, D])
        keep = kit.sb(f"{name}_keep", [P, RING, G])
        val = kit.sb(f"{name}_val", [P, 2, G, D])
        ps_t = kit.ps(f"{name}_ps_t", [P, G, P])
        ps_x = kit.ps(f"{name}_ps_x", [P, G, D])
        ps_s = kit.ps(f"{name}_ps_s", [heads, G * P])
        ps_m = kit.ps(f"{name}_ps_m", [P, G * heads + G])
        ps_n = [kit.ps(f"{name}_ps_n{i}", [P, 2, 2, P]) for i in range(4)]
        hsel = c.hsel4 if heads == 4 else c.hsel8
        (staged, fenced, sel_done, selt_ps, selt_done, spread_done, z_done, leaky_done, prod_done, score_done,
         score_t, prefix_done, top_done, drop_done, top_ps, less_done, exp_done, val_done, sums_done,
         copy_done, head_done, cleared, diff_done, first_prefix) = (
            kit.sem(f"{name}_{n}") for n in
            ("staged", "fenced", "sel_done", "selt_ps", "selt_done", "spread_done", "z_done", "leaky_done",
             "prod_done", "score_done", "score_t", "prefix_done", "top_done", "drop_done", "top_ps",
             "less_done", "exp_done", "val_done", "sums_done", "copy_done", "head_done", "cleared",
             "diff_done", "first_prefix"))
        landed, landed_before = c.pool_dma, list(c.pool_count)
        win_in = [kit.sem(f"{name}_win_in{i}") for i in range(2)]
        run_in = [kit.sem(f"{name}_run_in{i}") for i in range(2)]
        block = st.enter_context(nc.Block())

        @block.sync
        def _(sp):
            def emit(k, q):
                if inside(k, 0):
                    b = q % 2
                    starts = window_starts(nc, engine.SP, first, k)
                    wait_count(sp, spread_done, k - 1)
                    for g in range(G):
                        sp.dma_start(win[:, b, g, :], window_table[bass.ds(starts[g], P), :])\
                          .then_inc(win_in[b], 16)
                    wait_count(sp, top_done, k - 1)
                    rows_of = runs[:, bass.ds(k * G * P, G * P)]
                    sp.dma_start(run[:, b], replicate(rows_of, 0, heads)).then_inc(run_in[b], 16)
            staggered(sp, emit, 0)

        @block.gpsimd
        def _(pool):
            pool.memset(c.num[:], 0.0).then_inc(cleared, 1)

            def emit(k, q):
                if inside(k, 0):
                    gather_rows(pool, c, k, q, slots, table, index, rows, staged, fenced, val_done,
                                landed, landed_before)
            staggered(pool, emit, 0)

        @block.tensor
        def _(pe):
            def emit(k, q):
                b = q % 2
                if inside(k, 0):
                    pe.wait_ge(sel_done, k + 1)
                    wait_count(pe, selt_done, k)
                    for g in range(G):
                        mm = pe.transpose(ps_t[:, g], sel[:, q, g], c.ident[:])
                    mm.then_inc(selt_ps, 1)
                if inside(k, 4):
                    p = (q - 4) % RING
                    pe.wait_ge(val_done, k - 3)
                    wait_count(pe, head_done, (k - 5) * G)
                    for g in range(G):
                        out = ps_n[2 * b + g // 2][:, g % 2]
                        pe.matmul(out[:, 0], val[:, b, g], sel[:, p, g], start=True, stop=True)
                        mm = pe.matmul(out[:, 1], weight[:, b, g], sel[:, p, g], start=True, stop=True)
                    mm.then_inc(sums_done, 1)
                if inside(k, 0):
                    pe.wait_ge(selt_done, k + 1)
                    pe.wait_ge(win_in[b], turn2(k) * (16 * G) + 16 * G)
                    wait_count(pe, z_done, k)
                    for g in range(G):
                        mm = pe.matmul(ps_x[:, g], sel_t[:, b, g], win[:, b, g], start=True, stop=True)
                    mm.then_inc(spread_done, 1)
                if inside(k, 2):
                    pe.wait_ge(drop_done, k - 1)
                    wait_count(pe, exp_done, k - 2)
                    for g in range(G):
                        pe.matmul(ps_m[:, g * heads:(g + 1) * heads], top[:, b, g * P:(g + 1) * P],
                                  c.ident[0:heads, 0:heads], start=True, stop=True)
                    pe.matmul(ps_m[:, G * heads:], hsel[:], drop[:, b], start=True, stop=True)\
                      .then_inc(top_ps, 1)
                if inside(k, 1):
                    o = 1 - b
                    pe.wait_ge(score_done, k)
                    wait_count(pe, prefix_done, k - 1)
                    for g in range(G):
                        mm = pe.matmul(ps_s[:, g * P:(g + 1) * P], score[:, o, g], c.ident[:],
                                       start=True, stop=True)
                    mm.then_inc(score_t, 1)
            staggered(pe, emit, 4)

        @block.scalar
        def _(act):
            def emit(k, q):
                b = q % 2
                if inside(k, 4):
                    starts = window_starts(nc, engine.Activation, first, k - 4)
                if inside(k, 0):
                    act.wait_ge(selt_ps, k + 1)
                    wait_count(act, spread_done, k - 1)
                    act.activation(sel_t[:, b], ps_t, ACT.Copy).then_inc(selt_done, 1)
                if inside(k, 4):
                    for g in range(G):
                        if g == 0:
                            act.wait_ge(sums_done, k - 3)
                            if isinstance(k, int) and k == 4:
                                act.wait_ge(cleared, 1)
                        wait_count(act, copy_done, (k - 4) * G + g)
                        act.activation(c.num[:, :, bass.ds(starts[g] + 1, P - 1)],
                                       ps_n[2 * b + g // 2][:, g % 2, :, 1:P], ACT.Copy)\
                           .then_inc(copy_done, 1)
                if inside(k, 2):
                    p = (q - 2) % RING
                    act.wait_ge(less_done, k - 1)
                    wait_count(act, sums_done, k - 3)
                    act.activation(weight[:, b].rearrange("p g (h c) -> p (g h) c", h=heads),
                                   replicate(less[:, b].rearrange("p g h -> p (g h)"), 2, width), ACT.Exp)
                    act.activation(keep[:, p], ps_m[:, G * heads:], ACT.Exp).then_inc(exp_done, 1)
            staggered(act, emit, 4)

        @block.vector
        def _(dve):
            dve.memset(prefix[:, 1], 0.0).then_inc(first_prefix, 1)

            def emit(k, q):
                b = q % 2
                o = 1 - b
                if inside(k, 2):
                    dve.wait_ge(score_t, k - 1)
                    dve.wait_ge(run_in[b], turn2(k, 2) * 16 + 16)
                    if isinstance(k, int) and k == 2:
                        dve.wait_ge(first_prefix, 1)
                    wait_count(dve, prefix_done, k - 2)
                    dve.tensor_tensor_scan(prefix[:, b], run[:, b, 0], ps_s, prefix[:, o, G * P - 1:],
                                           ALU.add, ALU.max).then_inc(prefix_done, 1)

                def head(g):
                    if inside(k, 5):
                        p = (q - 5) % RING
                        if g == 0:
                            dve.wait_ge(copy_done, (k - 4) * G)
                        wait_count(dve, head_done, (k - 5) * G + g)
                        at = c.num[:, :, bass.ds(starts[g], 1)]
                        dve.scalar_tensor_tensor(at, at, keep[:, p, g:g + 1],
                                                 ps_n[2 * o + g // 2][:, g % 2, :, 0:1],
                                                 ALU.mult, ALU.add).then_inc(head_done, 1)

                if inside(k, 1) and not dot:
                    dve.wait_ge(z_done, k)
                    dve.scalar_tensor_tensor(z[:, o], z[:, o], LEAK, z[:, o], ALU.mult, ALU.max)\
                       .then_inc(leaky_done, 1)
                if inside(k, 3):
                    weighted_rows(k, q)
                if dot:
                    scores(k, q)
                if inside(k, 5):
                    starts = window_starts(nc, engine.DVE, first, k - 5)
                if inside(k, 2):
                    dve.wait_ge(prefix_done, k - 1)
                    wait_count(dve, top_ps, k - 3)
                    dve.tensor_tensor_scan(top[:, b, ::-1], run[:, b, 1, ::-1], prefix[:, b, ::-1], -BIG,
                                           ALU.add, ALU.max).then_inc(top_done, 1)
                if inside(k, 1) and not dot:
                    dve.wait_ge(leaky_done, k)
                    dve.tensor_tensor(z[:, o], z[:, o], replicate(c.att[:], 1, G), ALU.mult)\
                       .then_inc(prod_done, 1)
                head(0)
                if inside(k, 2):
                    dve.wait_ge(top_done, k - 1)
                    dve.tensor_tensor(drop[:, b, 1:G], prefix[:, b, P - 1:(G - 1) * P:P],
                                      top[:, b, P::P], ALU.subtract).then_inc(diff_done, 1)
                    dve.tensor_tensor(drop[:, b, 0:1], prefix[:, o, G * P - 1:], top[:, b, 0:1],
                                      ALU.subtract).then_inc(diff_done, 1)
                head(1)
                if inside(k, 2):
                    dve.wait_ge(diff_done, (k - 1) * 2)
                    dve.tensor_single_scalar(drop[:, b], drop[:, b], 0.0, ALU.min).then_inc(drop_done, 1)
                if not dot:
                    scores(k, q)
                head(2)
                if inside(k, -1):
                    wait_count(dve, sums_done, k - RING + 2)
                    dve.tensor_tensor(sel[:, (q + 1) % RING], replicate(c.iota_f, 1, G),
                                      replicate(slot[:, bass.ds((k + 1) * G, G)], 2, P),
                                      ALU.is_equal).then_inc(sel_done, 1)
                head(3)
                if inside(k, 0):
                    dve.wait_ge(spread_done, k + 1)
                    dve.wait_ge(landed[q], landed_before[q] + turn(k) * (16 * G) + 16 * G)
                    wait_count(dve, score_done, k - 1)
                    dve.tensor_tensor(z[:, b], ps_x, rows[:, q, :, 0:D], ALU.mult if dot else ALU.add)\
                       .then_inc(z_done, 1)
                if inside(k, 2):
                    dve.wait_ge(top_ps, k - 1)
                    wait_count(dve, exp_done, k - 3)
                    dve.tensor_tensor(less[:, b], score[:, b],
                                      ps_m[:, 0:G * heads].rearrange("p (g h) -> p g h", g=G),
                                      ALU.subtract).then_inc(less_done, 1)

            def weighted_rows(k, q):
                p, o = (q - 3) % RING, 1 - q % 2
                dve.wait_ge(exp_done, k - 2)
                wait_count(dve, sums_done, k - 4)
                dve.tensor_tensor(val[:, o], rows[:, p, :, v0:], weight[:, o], ALU.mult).then_inc(val_done, 1)

            def scores(k, q):
                if inside(k, 1):
                    o = 1 - q % 2
                    if dot:
                        dve.wait_ge(z_done, k)
                    else:
                        dve.wait_ge(prod_done, k)
                    wait_count(dve, score_t, k - 2)
                    dve.tensor_reduce(score[:, o], z[:, o].rearrange("p g (h c) -> p g h c", h=heads),
                                      AX.X, ALU.add).then_inc(score_done, 1)
            staggered(dve, emit, 5, ahead=1)
        c.pool_count = [n + 16 * T // RING for n in landed_before]


def edge_score_pass(nc, c, table, window_table, slot, real_slot, first, index):
    engine = mybir.EngineType
    with ExitStack() as st:
        kit = Kit(nc, st)
        slots = kit.sb("l1_slots", [P, RING * G], I32)
        rows = kit.sb("l1_rows", [P, RING, G, D + 4])
        win = kit.sb("l1_win", [P, 2, G, 4])
        sel = kit.sb("l1_sel", [P, 2, G, P])
        sel_t = kit.sb("l1_sel_t", [P, 2, G, P])
        real = kit.sb("l1_real", [P, RING, G, P])
        e = kit.sb("l1_e", [P, 2, 3, G])
        weight = kit.sb("l1_weight", [P, 2, G])
        ps_t = kit.ps("l1_ps_t", [P, G, P])
        ps_x = [kit.ps(f"l1_ps_x{i}", [P, G, 4]) for i in range(2)]
        ps_n = [kit.ps(f"l1_ps_n{i}", [P, 2, 2, P]) for i in range(4)]
        (staged, fenced, sel_done, selt_ps, selt_done, spread_done, real_done, add_done, leaky_done, e_done,
         exp_done, scaled_done, sums_done, copy_done, head_done, cleared) = (
            kit.sem(f"l1_{n}") for n in
            ("staged", "fenced", "sel_done", "selt_ps", "selt_done", "spread_done", "real_done", "add_done",
             "leaky_done", "e_done", "exp_done", "scaled_done", "sums_done", "copy_done", "head_done",
             "cleared"))
        landed, landed_before = c.pool_dma, list(c.pool_count)
        win_in = [kit.sem(f"l1_win_in{i}") for i in range(2)]
        block = st.enter_context(nc.Block())

        @block.sync
        def _(sp):
            def emit(k, q):
                if inside(k, 0):
                    b = q % 2
                    starts = window_starts(nc, engine.SP, first, k)
                    wait_count(sp, spread_done, k - 1)
                    for g in range(G):
                        sp.dma_start(win[:, b, g, :], window_table[bass.ds(starts[g], P), :])\
                          .then_inc(win_in[b], 16)
            staggered(sp, emit, 0)

        @block.gpsimd
        def _(pool):
            pool.memset(c.num[:], 0.0).then_inc(cleared, 1)

            def emit(k, q):
                if inside(k, 0):
                    gather_rows(pool, c, k, q, slots, table, index, rows, staged, fenced, sums_done,
                                landed, landed_before)
            staggered(pool, emit, 0)

        @block.tensor
        def _(pe):
            def emit(k, q):
                b = q % 2
                if inside(k, 0):
                    pe.wait_ge(sel_done, k + 1)
                    wait_count(pe, selt_done, k)
                    for g in range(G):
                        mm = pe.transpose(ps_t[:, g], sel[:, b, g], c.ident[:])
                    mm.then_inc(selt_ps, 1)
                if inside(k, 3):
                    o, p = 1 - b, (q - 3) % RING
                    pe.wait_ge(scaled_done, k - 2)
                    wait_count(pe, head_done, (k - 4) * G)
                    for g in range(G):
                        out = ps_n[2 * o + g // 2][:, g % 2]
                        pe.matmul(out[:, 0], rows[:, p, g, 0:D], real[:, p, g], start=True, stop=True)
                        mm = pe.matmul(out[:, 1], c.ones[:], real[:, p, g], start=True, stop=True)
                    mm.then_inc(sums_done, 1)
                if inside(k, 0):
                    pe.wait_ge(selt_done, k + 1)
                    pe.wait_ge(win_in[b], turn2(k) * (16 * G) + 16 * G)
                    wait_count(pe, add_done, k - 1)
                    for g in range(G):
                        mm = pe.matmul(ps_x[b][:, g], sel_t[:, b, g], win[:, b, g], start=True, stop=True)
                    mm.then_inc(spread_done, 1)
            staggered(pe, emit, 3)

        @block.scalar
        def _(act):
            def emit(k, q):
                b = q % 2
                if inside(k, 3):
                    starts = window_starts(nc, engine.Activation, first, k - 3)
                if inside(k, 0):
                    act.wait_ge(selt_ps, k + 1)
                    wait_count(act, spread_done, k - 1)
                    act.activation(sel_t[:, b], ps_t, ACT.Copy).then_inc(selt_done, 1)
                if inside(k, 3):
                    for g in range(G):
                        if g == 0:
                            act.wait_ge(sums_done, k - 2)
                            if isinstance(k, int) and k == 3:
                                act.wait_ge(cleared, 1)
                        wait_count(act, copy_done, (k - 3) * G + g)
                        act.activation(c.num[:, :, bass.ds(starts[g] + 1, P - 1)],
                                       ps_n[2 * (1 - b) + g // 2][:, g % 2, :, 1:P], ACT.Copy)\
                           .then_inc(copy_done, 1)
                if inside(k, 1):
                    act.wait_ge(e_done, k)
                    wait_count(act, scaled_done, k - 2)
                    act.activation(weight[:, 1 - b], e[:, 1 - b, 2], ACT.Exp).then_inc(exp_done, 1)
            staggered(act, emit, 3)

        @block.vector
        def _(dve):
            def emit(k, q):
                b = q % 2
                o = 1 - b
                def head(g):
                    if inside(k, 4):
                        if g == 0:
                            dve.wait_ge(copy_done, (k - 3) * G)
                        wait_count(dve, head_done, (k - 4) * G + g)
                        at = c.num[:, :, bass.ds(starts[g], 1)]
                        dve.tensor_tensor(at, at, ps_n[2 * b + g // 2][:, g % 2, :, 0:1], ALU.add)\
                           .then_inc(head_done, 1)

                if inside(k, 0):
                    wait_count(dve, selt_done, k - 1)
                    dve.tensor_tensor(sel[:, b], replicate(c.iota_f, 1, G),
                                      replicate(slot[:, bass.ds(k * G, G)], 2, P),
                                      ALU.is_equal).then_inc(sel_done, 1)
                if inside(k, 1):
                    dve.wait_ge(spread_done, k)
                    dve.wait_ge(landed[(q - 1) % RING],
                                landed_before[(q - 1) % RING] + turn(k, 1) * (16 * G) + 16 * G)
                    wait_count(dve, leaky_done, k - 2)
                    dve.tensor_tensor(e[:, o, 0], ps_x[o][:, :, 0], rows[:, (q - 1) % RING, :, D], ALU.add)\
                       .then_inc(add_done, 1)
                if inside(k, 0):
                    wait_count(dve, sums_done, k - RING + 1)
                    dve.tensor_tensor(real[:, q], replicate(c.iota_f, 1, G),
                                      replicate(real_slot[:, bass.ds(k * G, G)], 2, P),
                                      ALU.is_equal).then_inc(real_done, 1)
                if inside(k, 4):
                    starts = window_starts(nc, engine.DVE, first, k - 4)
                if inside(k, 1):
                    dve.wait_ge(add_done, k)
                    dve.scalar_tensor_tensor(e[:, o, 1], e[:, o, 0], LEAK, e[:, o, 0], ALU.mult, ALU.max)\
                       .then_inc(leaky_done, 1)
                head(0)
                head(1)
                if inside(k, 2):
                    p = (q - 2) % RING
                    dve.wait_ge(exp_done, k - 1)
                    dve.wait_ge(real_done, k - 1)
                    dve.tensor_tensor(real[:, p], real[:, p], replicate(weight[:, b], 2, P), ALU.mult)\
                       .then_inc(scaled_done, 1)
                head(2)
                if inside(k, 1):
                    dve.wait_ge(leaky_done, k)
                    wait_count(dve, exp_done, k - 2)
                    dve.tensor_scalar(e[:, o, 2], e[:, o, 1], -2.0, 2.0, ALU.max, ALU.min).then_inc(e_done, 1)
                head(3)
            staggered(dve, emit, 4)
        c.pool_count = [n + 16 * T // RING for n in landed_before]


def sum_pass(nc, c, name, table, real_slot, first, index, acc, types=None):
    with ExitStack() as st:
        kit = Kit(nc, st)
        parts = 1 if types is None else 3
        slots = kit.sb(f"{name}_slots", [P, RING * G], I32)
        rows = kit.sb(f"{name}_rows", [P, RING, G, D])
        sel = kit.sb(f"{name}_sel", [P, RING, G, P])
        kind = kit.sb(f"{name}_kind", [P, 3, G, 2 * P]) if types is not None else None
        ps_n = [kit.ps(f"{name}_ps_n{i}", [P, parts, P]) for i in range(2 * G)]
        staged, fenced, sel_done, kind_done, sums_done, copy_done, head_done, cleared = (
            kit.sem(f"{name}_{n}") for n in
            ("staged", "fenced", "sel_done", "kind_done", "sums_done", "copy_done", "head_done", "cleared"))
        landed, landed_before = c.pool_dma, list(c.pool_count)
        block = st.enter_context(nc.Block())

        @block.gpsimd
        def _(pool):
            def emit(k, q):
                if inside(k, 0):
                    gather_rows(pool, c, k, q, slots, table, index, rows, staged, fenced, sums_done,
                                landed, landed_before, G)
            staggered(pool, emit, 0)

        @block.tensor
        def _(pe):
            def emit(k, q):
                b = q % 2
                if inside(k, 0):
                    pe.wait_ge(landed[q], landed_before[q] + turn(k) * (16 * G) + 16 * G)
                    for g in range(G):
                        if g == 0:
                            pe.wait_ge(sel_done, k + 1)
                            if types is not None:
                                pe.wait_ge(kind_done, k + 1)
                        wait_count(pe, head_done, (k - 2) * G + g + 1)
                        mm = pe.matmul(ps_n[b * G + g][:, 0], rows[:, q, g], sel[:, q, g],
                                       start=True, stop=True)
                        for h in range(parts - 1):
                            mm = pe.matmul(ps_n[b * G + g][:, 1 + h], kind[:, q % 3, g, h * P:(h + 1) * P],
                                           sel[:, q, g], start=True, stop=True)
                        mm.then_inc(sums_done, 1)
            staggered(pe, emit, 0)

        @block.scalar
        def _(act):
            def emit(k, q):
                b = q % 2
                if inside(k, 0):
                    starts = window_starts(nc, mybir.EngineType.Activation, first, k)
                    for g in range(G):
                        act.wait_ge(sums_done, k * G + g + 1)
                        if isinstance(k, int) and k == 0 and g == 0:
                            act.wait_ge(cleared, 1)
                        wait_count(act, copy_done, k * G + g)
                        act.activation(acc[:, 0:parts, bass.ds(starts[g] + 1, P - 1)],
                                       ps_n[b * G + g][:, :, 1:P], ACT.Copy).then_inc(copy_done, 1)
            staggered(act, emit, 0)

        @block.vector
        def _(dve):
            dve.memset(acc[:, 0:parts], 0.0).then_inc(cleared, 1)

            def emit(k, q):
                if inside(k, 0):
                    wait_count(dve, sums_done, (k - RING + 1) * G)
                    dve.tensor_tensor(sel[:, q], replicate(c.iota_f, 1, G),
                                      replicate(real_slot[:, bass.ds(k * G, G)], 2, P),
                                      ALU.is_equal).then_inc(sel_done, 1)
                    if types is not None:
                        wait_count(dve, sums_done, (k - 2) * G)
                        dve.tensor_tensor(kind[:, q % 3], replicate(c.type_iota[:], 1, G),
                                          replicate(types[:, bass.ds(k * G, G)], 2, 2 * P),
                                          ALU.is_equal).then_inc(kind_done, 1)
                if inside(k, 2):
                    starts = window_starts(nc, mybir.EngineType.DVE, first, k - 2)
                    for g in range(G):
                        dve.wait_ge(copy_done, (k - 2) * G + g + 1)
                        wait_count(dve, head_done, (k - 2) * G + g)
                        if isinstance(k, int) and k == 2 and g == 0:
                            dve.wait_ge(cleared, 1)
                        at = acc[:, 0:parts, bass.ds(starts[g], 1)]
                        dve.tensor_tensor(at, at, ps_n[q % 2 * G + g][:, :, 0:1], ALU.add).then_inc(head_done, 1)
            staggered(dve, emit, 2)
        c.pool_count = [n + 16 * T // RING for n in landed_before]


def load_weights(nc, c, w):
    with ExitStack() as st:
        kit = Kit(nc, st)
        att_cols = kit.sb("att_cols", [P, 2])
        kernel_t = kit.sb("kernel_t", [P, P])
        zero_rows = kit.sb("zero_rows", [P, D])
        rel_rows = kit.sb("rel_rows", [RELS // 2, 2, D])
        rel_t = kit.sb("rel_t", [P, RELS])
        ps_t, ps_a = kit.ps("w_ps_t", [P, P]), kit.ps("w_ps_a", [P, 2])
        ps_rt = kit.ps("w_ps_rt", [P, RELS])
        ps_rw = kit.ps("w_ps_rw", [P, 2, 2, D])
        cleared, loaded, turned, copied = (kit.sem(n) for n in ("w_cleared", "w_loaded", "w_turned", "w_copied"))
        rel_zero = kit.sem("w_rel_zero")
        block = st.enter_context(nc.Block())
        row = lambda a: a.rearrange("(a n) -> a n", a=1)
        col = lambda a: a.rearrange("(p a) -> p a", a=1)
        loads = [(c.w0[:, 0:D], w["L0_gnn_W_l"]), (c.w0[:, D:2 * D], w["L0_gnn_W_r"]),
                 (c.b0[:, 0:D], row(w["L0_gnn_b_l"])), (c.b0[:, D:2 * D], row(w["L0_gnn_b_r"])),
                 (c.w1[:, 0:D], w["L1_gnn_kernel"]),
                 (c.w2[:, 0:D], w["L2_gnn_key_kernel"]), (c.w2[:, D:2 * D], w["L2_gnn_kernel"]),
                 (c.w2[:, 2 * D:], w["L2_gnn_query_kernel"]),
                 (c.b2[:, 0:D], row(w["L2_gnn_key_bias"])), (c.b2[:, 2 * D:], row(w["L2_gnn_query_bias"])),
                 (c.bias0[:], col(w["L0_gnn_bias"])), (c.gamma[:], col(w["L0_gnn_gamma"])),
                 (c.beta[:], col(w["L0_gnn_beta"])), (c.bias2[:], col(w["L2_gnn_bias"])),
                 (c.att[:], row(w["L0_gnn_att"].rearrange("h c -> (h c)")).to_broadcast([P, D])),
                 (att_cols[:, 0:1], w["L1_gnn_kernel_attention"][D:2 * D, :]),
                 (att_cols[:, 1:2], w["L1_gnn_kernel_attention"][0:D, :])]
        for l in range(2):
            loads += [(c.wn[:, l], w["L3_gnn_Wn"][l]), (c.wl[:, l], w["L3_gnn_Wl"][l]),
                      (c.wa[:, l], w["L3_gnn_Wa"][l])]
        loads.append((rel_rows[:], w["L3_gnn_rel_emb"].rearrange("(h r) d -> r h d", h=2)))
        pads = [(c.win0, D), (c.win1, 4), (c.win2, D)]

        @block.gpsimd
        def _(pool):
            pool.memset(c.w1[:], 0.0).then_inc(cleared, 1)
            pool.memset(c.b2[:], 0.0).then_inc(cleared, 1)
            pool.memset(zero_rows[:], 0.0).then_inc(cleared, 1)

        @block.sync
        def _(sp):
            sp.wait_ge(cleared, 3)
            for to, of in loads:
                sp.dma_start(to, of).then_inc(loaded, 16)
            for table, width in pads:
                sp.dma_start(table[NP:NW, :], zero_rows[:, 0:width]).then_inc(loaded, 16)
            sp.wait_ge(loaded, 16 * (len(loads) + len(pads)))

        @block.tensor
        def _(pe):
            pe.wait_ge(loaded, 16 * (len(loads) + len(pads)))
            pe.transpose(ps_t, c.w1[:, 0:D], c.ident[:]).then_inc(turned, 1)
            for h in range(2):
                mm = pe.transpose(ps_rt[:, h * (RELS // 2):(h + 1) * (RELS // 2)], rel_rows[:, h],
                                  c.ident[0:RELS // 2, 0:RELS // 2])
            mm.then_inc(turned, 1)
            pe.wait_ge(copied, 1)
            pe.matmul(ps_a, kernel_t[:], att_cols[:], start=True, stop=True).then_inc(turned, 1)
            pe.wait_ge(copied, 2)
            for h, (r0, r1) in enumerate(((0, P), (P, RELS))):
                for l in range(2):
                    mm = pe.matmul(ps_rw[0:r1 - r0, h, l], rel_t[:, r0:r1], c.wn[:, l], start=True, stop=True)
            mm.then_inc(turned, 1)

        @block.vector
        def _(dve):
            dve.memset(c.rel_w[:], 0.0).then_inc(rel_zero, 1)
            dve.wait_ge(turned, 1)
            dve.tensor_copy(kernel_t[:], ps_t).then_inc(copied, 1)
            dve.wait_ge(turned, 2)
            dve.tensor_copy(rel_t[:], ps_rt).then_inc(copied, 1)
            dve.wait_ge(turned, 4)
            dve.wait_ge(rel_zero, 1)
            dve.tensor_copy(c.rel_w[:, 0], ps_rw[:, 0]).then_inc(copied, 1)
            dve.tensor_copy(c.rel_w[0:RELS - P, 1], ps_rw[0:RELS - P, 1]).then_inc(copied, 1)
            dve.tensor_copy(c.w1[:, D:D + 1], ps_a[:, 0:1]).then_inc(copied, 1)
            dve.tensor_copy(c.w1[:, D + 4:D + 5], ps_a[:, 1:2]).then_inc(copied, 1)


STAGES = {
    "load": ["turn", "take0", "take1"],
    "gat": ["den", "recip", "ratio", "bias", "a_mean", "a_center", "a_square", "a_var", "a_std", "a_rstd",
            "a_diagonal", "a_spread", "a_norm", "affine", "negative", "exp", "elu", "residual"],
    "edge": ["den", "recip", "ratio", "residual"],
    "dot": ["recip", "ratio", "residual"],
    "rel0": ["counted", "degree", "root", "inverse", "has_in", "products", "sum", "scaled", "self_l", "add_l", "no_in",
             "self_a", "add_a", "rrelu"],
}
LN_STEPS = ["b_mean", "b_center", "b_square", "b_var", "b_std", "b_rstd", "b_diagonal", "b_spread", "b_norm"]
STAGES["rel1"] = STAGES["rel0"] + ["residual"]


def node_step(nc, c, stage, weight, bias, relu, outputs, layer=0, x_dram=None, keep_in=None):
    steps = STAGES[stage] + (LN_STEPS if stage in ("gat", "edge", "dot", "rel1") else []) + ["keep"]
    order = {s: i for i, s in enumerate(steps)}
    per_j = len(steps)
    width = weight.shape[-1]
    with ExitStack() as st:
        kit = Kit(nc, st)
        name = f"n_{stage}"
        a, b, d, s = (kit.sb(f"{name}_{x}", [P, CW]) for x in "abds")
        m = kit.sb(f"{name}_m", [P, CW]) if stage[:3] == "rel" else None
        x_rows = kit.sb(f"{name}_x_rows", [P, CB, D]) if stage == "load" else None
        std = kit.sb(f"{name}_std", [P, CB])
        tab = kit.sb(f"{name}_tab", [P, CB, width])
        pa, pb, pc = (kit.ps(f"{name}_p{x}", [P, 2, 512]) for x in "abc")
        pt = [kit.ps(f"{name}_pt{i}", [P, 512]) for i in range(2)]
        step_done, tab_mm, tab_cp, x_in, x_zero = (kit.sem(f"{name}_{x}") for x in
                                                   ("step_done", "tab_mm", "tab_cp", "x_in", "x_zero"))
        stored = kit.sem(f"{name}_stored")
        block = st.enter_context(nc.Block())
        halves = lambda t: t[:, 0:CW].rearrange("p (h w) -> p h w", h=2)
        banks = lambda t: t[:, :, 0:HW]

        def here(eng, step, j):
            if step not in order:
                return False
            wait_count(eng, step_done, j * per_j + order[step])
            return True

        def last(j):
            return isinstance(j, int) and j == CS - 1

        def run(eng, body):
            body(0)
            with eng.Fori(1, CS - 1) as j:
                body(j)
            body(CS - 1)

        @block.sync
        def _(sp):
            def body(j):
                if stage == "load":
                    wait_count(sp, step_done, j * per_j)
                    if last(j):
                        full, rest = divmod(N - (CS - 1) * CW, P)
                        sp.wait_ge(x_zero, 1)
                        sp.dma_start(x_rows[:, 0:full], x_dram[j * CW:j * CW + full * P, :]
                                     .rearrange("(i p) d -> p i d", p=P)).then_inc(x_in, 16)
                        sp.dma_start(x_rows[0:rest, full], x_dram[N - rest:N, :]).then_inc(x_in, 16)
                    else:
                        sp.dma_start(x_rows[:], x_dram[bass.ds(j * CW, CW), :]
                                     .rearrange("(i p) d -> p i d", p=P)).then_inc(x_in, 16)
                sp.wait_ge(tab_cp, j * CB + CB)
                for table, c0, c1 in outputs:
                    if last(j) and table.shape[0] == N:
                        full, rest = divmod(N - (CS - 1) * CW, P)
                        sp.dma_start(table[j * CW:j * CW + full * P, :].rearrange("(i p) d -> p i d", p=P),
                                     tab[:, 0:full, c0:c1]).then_inc(stored, 16)
                        sp.dma_start(table[N - rest:N, :], tab[0:rest, full, c0:c1]).then_inc(stored, 16)
                        n_stores = 16 * (CS + 1)
                    else:
                        sp.dma_start(table[bass.ds(j * CW, CW), :].rearrange("(i p) d -> p i d", p=P),
                                     tab[:, :, c0:c1]).then_inc(stored, 16)
                        n_stores = 16 * len(outputs) * CS
                if last(j):
                    sp.wait_ge(stored, n_stores)
            run(sp, body)

        @block.tensor
        def _(pe):
            def mean(out, of):
                for h in range(2):
                    mm = pe.matmul(out[:, h, 0:HW], c.mean_w[:], of[:, h * HW:(h + 1) * HW],
                                   start=True, stop=True)
                mm.then_inc(step_done, 1)

            def body(j):
                if here(pe, "turn", j):
                    pe.wait_ge(x_in, j * 16 + (32 if last(j) else 16))
                    for i in range(CB):
                        mm = pe.transpose(pa[:, i // 4, (i % 4) * P:(i % 4 + 1) * P], x_rows[:, i], c.ident[:])
                    mm.then_inc(step_done, 1)
                def times(out, w, of):
                    for h in range(2):
                        mm = pe.matmul(out[:, h, 0:HW], w[:, layer], of[:, bass.ds(j * CW + h * HW, HW)],
                                       start=True, stop=True)
                    return mm

                def by_type(out, w):
                    for h in range(2):
                        for t in range(2):
                            mm = pe.matmul(out[:, h, 0:HW], w(t), c.counts[:, t, bass.ds(j * CW + h * HW, HW)],
                                           start=t == 0, stop=t == 1)
                    return mm
                if stage[:3] == "rel":
                    feats = c.x if stage == "rel0" else c.hidden
                if here(pe, "counted", j):
                    by_type(pc, lambda t: c.ones[:]).then_inc(step_done, 1)
                    by_type(pa, lambda t: c.rel_w[:, t, layer])
                    times(pb, c.wl, feats)
                if here(pe, "products", j):
                    times(pc, c.wa, feats).then_inc(step_done, 1)
                for t in "ab":
                    if here(pe, f"{t}_mean", j):
                        mean(pa, a)
                    if here(pe, f"{t}_var", j):
                        for i in range(CB):
                            mm = pe.matmul(pb[:, 0, i:i + 1], s[:, i * P:(i + 1) * P], c.mean_w[:, 0:1],
                                           start=True, stop=True)
                        mm.then_inc(step_done, 1)
                    if here(pe, f"{t}_spread", j):
                        for h in range(2):
                            mm = pe.matmul(pb[:, h, 0:HW], c.ones[:], s[:, h * HW:(h + 1) * HW],
                                           start=True, stop=True)
                        mm.then_inc(step_done, 1)
                wait_count(pe, step_done, j * per_j + order["keep"])
                for i in range(CB):
                    wait_count(pe, tab_cp, j * CB + max(i - 1, 0))
                    out = pt[i % 2][:, 0:width]
                    if bias is not None:
                        pe.matmul(out, c.one_row[:], bias[:], start=True, stop=False)
                    pe.matmul(out, a[:, i * P:(i + 1) * P], weight, start=bias is None, stop=True)\
                      .then_inc(tab_mm, 1)
            run(pe, body)

        @block.scalar
        def _(act):
            def body(j):
                if here(act, "root", j):
                    act.activation(b[:], b[:], ACT.Sqrt).then_inc(step_done, 1)
                for t in "ab":
                    if here(act, f"{t}_square", j):
                        act.activation(s[:], d[:], ACT.Square).then_inc(step_done, 1)
                    if here(act, f"{t}_std", j):
                        act.activation(std[:], pb[:, 0, 0:CB], ACT.Sqrt, bias=c.eps[:]).then_inc(step_done, 1)
                    if t == "a" and here(act, "exp", j):
                        act.activation(b[:], b[:], ACT.Exp).then_inc(step_done, 1)
                wait_count(act, stored, j * (16 * len(outputs)))
                for i in range(CB):
                    act.wait_ge(tab_mm, j * CB + i + 1)
                    at = 0
                    for c0, c1 in [*relu, (width, width)]:
                        if c0 > at:
                            ins = act.activation(tab[:, i, at:c0], pt[i % 2][:, at:c0], ACT.Copy)
                        if c1 > c0:
                            ins = act.activation(tab[:, i, c0:c1], pt[i % 2][:, c0:c1], ACT.Relu)
                        at = c1
                    ins.then_inc(tab_cp, 1)
            run(act, body)

        @block.vector
        def _(dve):
            def body(j):
                at = lambda t: t[:, bass.ds(j * CW, CW)]
                if stage == "load":
                    wait_count(dve, tab_mm, j * CB)
                    here(dve, "take0", j)
                    dve.tensor_copy(a[:, 0:512], pa[:, 0]).then_inc(step_done, 1)
                    here(dve, "take1", j)
                    dve.tensor_copy(a[:, 512:CW], pa[:, 1, 0:CW - 512]).then_inc(step_done, 1)
                if here(dve, "den", j):
                    dve.tensor_single_scalar(b[:], at(c.num[:, 1]), 1e-16 if stage == "gat" else 1e-9,
                                             ALU.add).then_inc(step_done, 1)
                if here(dve, "recip", j):
                    dve.reciprocal(b[:], b[:] if stage != "dot" else at(c.num[:, 1])).then_inc(step_done, 1)
                if here(dve, "ratio", j):
                    wait_count(dve, tab_mm, j * CB)
                    dve.tensor_tensor(a[:], at(c.num[:, 0]), b[:], ALU.mult).then_inc(step_done, 1)
                if here(dve, "bias", j):
                    dve.tensor_single_scalar(a[:], a[:], c.bias0[:], ALU.add).then_inc(step_done, 1)
                if here(dve, "degree", j):
                    dve.tensor_single_scalar(halves(b), banks(pc), 1.0, ALU.max).then_inc(step_done, 1)
                if here(dve, "inverse", j):
                    dve.reciprocal(b[:], b[:]).then_inc(step_done, 1)
                if here(dve, "has_in", j):
                    dve.tensor_single_scalar(halves(m), banks(pc), 1.0, ALU.min).then_inc(step_done, 1)
                if here(dve, "sum", j):
                    wait_count(dve, tab_mm, j * CB)
                    dve.tensor_tensor(halves(a), banks(pa), halves(at(c.num[:, 0])), ALU.add)\
                       .then_inc(step_done, 1)
                if here(dve, "scaled", j):
                    dve.tensor_tensor(a[:], a[:], b[:], ALU.mult).then_inc(step_done, 1)
                if here(dve, "self_l", j):
                    dve.tensor_tensor(halves(d), banks(pb), halves(m), ALU.mult).then_inc(step_done, 1)
                if here(dve, "add_l", j):
                    dve.tensor_tensor(a[:], a[:], d[:], ALU.add).then_inc(step_done, 1)
                if here(dve, "no_in", j):
                    dve.tensor_scalar(m[:], m[:], -1.0, 1.0, ALU.mult, ALU.add).then_inc(step_done, 1)
                if here(dve, "self_a", j):
                    dve.tensor_tensor(halves(d), banks(pc), halves(m), ALU.mult).then_inc(step_done, 1)
                if here(dve, "add_a", j):
                    dve.tensor_tensor(a[:], a[:], d[:], ALU.add).then_inc(step_done, 1)
                if here(dve, "rrelu", j):
                    dve.scalar_tensor_tensor(a[:], a[:], RRELU, a[:], ALU.mult, ALU.max).then_inc(step_done, 1)
                for t in "ab":
                    if t == "b" and here(dve, "residual", j):
                        if stage == "gat":
                            dve.scalar_tensor_tensor(a[:], a[:], -1.0, at(c.x), ALU.add, ALU.add)\
                               .then_inc(step_done, 1)
                        elif stage == "dot":
                            dve.scalar_tensor_tensor(a[:], a[:], c.bias2[:], at(c.x), ALU.add, ALU.add)\
                               .then_inc(step_done, 1)
                        else:
                            dve.tensor_tensor(a[:], a[:], at(c.x), ALU.add).then_inc(step_done, 1)
                    if here(dve, f"{t}_center", j):
                        dve.tensor_tensor(halves(d), halves(a), banks(pa), ALU.subtract).then_inc(step_done, 1)
                    if here(dve, f"{t}_rstd", j):
                        dve.reciprocal(std[:], std[:]).then_inc(step_done, 1)
                    if here(dve, f"{t}_diagonal", j):
                        dve.tensor_tensor(s[:].rearrange("p (i n) -> p i n", i=CB), replicate(c.ident[:], 1, CB),
                                          replicate(std[:], 2, P), ALU.mult).then_inc(step_done, 1)
                    if here(dve, f"{t}_norm", j):
                        dve.tensor_tensor(halves(a), halves(d), banks(pb), ALU.mult).then_inc(step_done, 1)
                    if t == "a" and here(dve, "affine", j):
                        dve.tensor_scalar(a[:], a[:], c.gamma[:], c.beta[:], ALU.mult, ALU.add)\
                           .then_inc(step_done, 1)
                    if t == "a" and here(dve, "negative", j):
                        dve.tensor_single_scalar(b[:], a[:], 0.0, ALU.min).then_inc(step_done, 1)
                    if t == "a" and here(dve, "elu", j):
                        dve.scalar_tensor_tensor(a[:], a[:], 0.0, b[:], ALU.max, ALU.add).then_inc(step_done, 1)
                here(dve, "keep", j)
                if keep_in is not None:
                    dve.tensor_single_scalar(at(keep_in), a[:], 1.0, ALU.mult).then_inc(step_done, 1)
                else:
                    dve.nop().then_inc(step_done, 1)
            run(dve, body)

        @block.gpsimd
        def _(pool):
            if stage == "load":
                pool.wait_ge(step_done, (CS - 2) * per_j + order["turn"] + 1)
                pool.memset(x_rows[:], 0.0).then_inc(x_zero, 1)


def build(nc, x, src, dst, etype, weights, out):
    class Memory:
        pass

    c = Memory()
    dram = lambda name, shape: nc.dram_tensor(name, shape, F32, kind="Internal").ap()
    sorted_dst, sorted_src = dram("sorted_dst", (POS, 4)), dram("sorted_src", (POS, 4))
    runs_dst, runs_src = dram("runs_dst", (2, POS)), dram("runs_src", (2, POS))
    tab0, tab1, tab2 = dram("tab0", (NP, D)), dram("tab1", (NP, D + 4)), dram("tab2", (NP, 2 * D))
    tab3, tab4 = dram("tab3", (NP, D)), dram("tab4", (NP, D))
    c.win0, c.win1, c.win2 = dram("win0", (NW, D)), dram("win1", (NW, 4)), dram("win2", (NW, D))
    with ExitStack() as st:
        kit = Kit(nc, st)
        c.pool_dma = [kit.sem(f"pool_dma{i}") for i in range(RING)]
        c.pool_count = [0] * RING
        c.ident, c.ones, c.mean_w = kit.sb("ident", [P, P]), kit.sb("ones", [P, P]), kit.sb("mean_w", [P, P])
        c.identb = kit.sb("identb", [P, P], BF16)
        c.before, c.after, c.first_row = (kit.sb(n, [P, P]) for n in ("before", "after", "first_row"))
        c.hsel4, c.hsel8 = kit.sb("hsel4", [4, P]), kit.sb("hsel8", [8, P])
        c.fence = kit.sb("fence", [1, 1])
        c.one_row, c.eps = kit.sb("one_row", [1, P]), kit.sb("eps", [P, 1])
        c.type_iota = kit.sb("type_iota", [P, 2 * P])
        c.iota_f = c.type_iota[:, 0:P]
        c.iota_b, c.node_id = kit.sb("iota_b", [P, P], BF16), kit.sb("node_id", [P, NT])
        c.w0, c.b0 = kit.sb("w0", [P, 2 * D]), kit.sb("b0", [1, 2 * D])
        c.w1 = kit.sb("w1", [P, D + 8])
        c.w2, c.b2 = kit.sb("w2", [P, 3 * D]), kit.sb("b2", [1, 3 * D])
        c.wn, c.wl, c.wa = (kit.sb(n, [P, 2, D]) for n in ("wn", "wl", "wa"))
        c.bias0, c.gamma, c.beta, c.bias2 = (kit.sb(n, [P, 1]) for n in ("bias0", "gamma", "beta", "bias2"))
        c.att = kit.sb("att", [P, D])
        c.rel_w = kit.sb("rel_w", [P, 2, 2, D])
        lists = {}
        for n in ("dst", "src"):
            lists[n] = (kit.sb(f"slot_{n}", [P, T]), kit.sb(f"real_slot_{n}", [P, T]),
                        kit.sb(f"first_{n}", [1, T], I32), kit.sb(f"neighbour_{n}", [P, T], I32))
        etype_at = kit.sb("etype_at", [P, T])
        constants(nc, c)
        load_weights(nc, c, weights)
        with ExitStack() as sort_scope:
            edge_kit = Kit(nc, sort_scope)
            c.edge = edge_kit.sb("edge", [ET, 3, UT])
            c.low, c.high = edge_kit.sb("low", [ET, 2, UT]), edge_kit.sb("high", [ET, 2, UT])
            edge_columns(nc, c, src, dst, etype)
            counting_sorts(nc, c, (src, dst), (sorted_src, sorted_dst))
        for n, rows, runs in (("dst", sorted_dst, runs_dst), ("src", sorted_src, runs_src)):
            slot, real_slot, first, neighbour = lists[n]
            read_sorted(nc, c, n, rows, runs, slot, real_slot, first, neighbour,
                        etype_at if n == "dst" else None)
        x_at = kit.sb("x_at", [P, NP])
        num_scope = st.enter_context(ExitStack())
        num = num_scope.enter_context(nc.sbuf_tensor("num", [P, 2, NW], F32))
        c.x, c.num = x_at[:], num[:]
        slot_d, real_d, first_d, nb_d = lists["dst"]
        slot_s, real_s, first_s, nb_s = lists["src"]
        node_step(nc, c, "load", c.w0[:], c.b0, [], [(tab0, 0, D), (c.win0, D, 2 * D)], x_dram=x, keep_in=c.x)
        attention_pass(nc, c, "l0", 4, False, tab0, c.win0, runs_dst, slot_d, first_d, nb_d)
        node_step(nc, c, "gat", c.w1[:], None, [], [(tab1, 0, D + 4), (c.win1, D + 4, D + 8)], keep_in=c.x)
        edge_score_pass(nc, c, tab1, c.win1, slot_s, real_s, first_s, nb_s)
        node_step(nc, c, "edge", c.w2[:], c.b2, [(0, D), (2 * D, 3 * D)], [(tab2, 0, 2 * D), (c.win2, 2 * D, 3 * D)],
                  keep_in=c.x)
        attention_pass(nc, c, "l2", 8, True, tab2, c.win2, runs_src, slot_s, first_s, nb_s)
        node_step(nc, c, "dot", c.wn[:, 0], None, [], [(tab3, 0, D)], keep_in=c.x)
        num_scope.close()
        acc = kit.sb("acc", [P, 3, NW])
        c.num, c.counts = acc[:], acc[:, 1:3]
        sum_pass(nc, c, "l3a", tab3, real_d, first_d, nb_d, c.num, types=etype_at)
        hidden = kit.sb("hidden", [P, NP])
        c.hidden = hidden[:]
        node_step(nc, c, "rel0", c.wn[:, 1], None, [], [(tab4, 0, D)], layer=0, keep_in=c.hidden)
        sum_pass(nc, c, "l3b", tab4, real_d, first_d, nb_d, c.num)
        node_step(nc, c, "rel1", c.ident[:], None, [], [(out, 0, D)], layer=1)


_INS = ["x", "src", "dst", "edge_type_200", "L0_gnn_W_l", "L0_gnn_b_l", "L0_gnn_W_r", "L0_gnn_b_r", "L0_gnn_att",
        "L0_gnn_bias", "L0_gnn_gamma", "L0_gnn_beta", "L1_gnn_kernel", "L1_gnn_kernel_attention",
        "L2_gnn_query_kernel", "L2_gnn_query_bias", "L2_gnn_key_kernel", "L2_gnn_key_bias", "L2_gnn_kernel",
        "L2_gnn_bias", "L3_gnn_rel_emb", "L3_gnn_Wn", "L3_gnn_Wl", "L3_gnn_Wa"]


def kernel(**inputs):
    import concourse.bacc as _bacc
    from concourse.bass_utils import run_bass_kernel_spmd as _run

    nc = _bacc.Bacc("TRN2", target_bir_lowering=False, num_devices=1)
    arrays, aps = {}, {}
    for name in _INS:
        a = np.ascontiguousarray(inputs[name])
        arrays[f"in_{name}_dram"] = a
        aps[name] = nc.dram_tensor(f"in_{name}_dram", a.shape, mybir.dt.from_np(a.dtype), kind="ExternalInput").ap()
    out = nc.dram_tensor("out_0_dram", (N, D), F32, kind="ExternalOutput").ap()
    build(nc, aps["x"], aps["src"], aps["dst"], aps["edge_type_200"], aps, out)
    r = _run(nc, [arrays], core_ids=[0])
    return r.results[0]["out_0_dram"]
```
